# Optimizing a Trainium2 kernel written in Bass

```python
import numpy as np
import jax
import jax.numpy as jnp

def _softmax(x, axis=-1):
    return jax.nn.softmax(x, axis=axis)

def _gelu(x):
    return jax.nn.gelu(x, approximate=True)

def _silu(x):
    return jax.nn.silu(x)

def _sigmoid(x):
    return jax.nn.sigmoid(x)

def _layernorm(x, axis=-1, eps=1e-05):
    m = jnp.mean(x, axis=axis, keepdims=True)
    v = jnp.var(x, axis=axis, keepdims=True)
    return (x - m) / jnp.sqrt(v + eps)

def _scatter_add(tgt, idx, src, axis=0):
    return tgt.at[idx].add(src)

def _segment_sum(src, seg, n):
    return jax.ops.segment_sum(src, seg, n)
kernel_name = 'mk_vit_tower_d1_tok_img1024_r4_efafc0'

def setup_inputs(seed: int=0):
    np.random.seed(seed)
    _w = jnp.asarray

    def _rec_inputs():
        import jax
        import jax.numpy as jnp
        _rk = jax.random.key(seed)
        x = -0.00016672 + 0.999947 * jax.random.normal(jax.random.fold_in(_rk, 1), (64, 96, 96, 3), jnp.float32)
        return x
    x = _rec_inputs()

    def _L0_tok_setup():
        import jax, jax.numpy as jnp
        import numpy as np
        P = 16
        E = 256

        def patchify(images, patch_size):
            B, H, W, C = images.shape
            hp, wp = (H // patch_size, W // patch_size)
            x = images.reshape(B, hp, patch_size, wp, patch_size, C)
            x = x.transpose(0, 1, 3, 2, 4, 5)
            return x.reshape(B, hp * wp, patch_size * patch_size * C)
        key = jax.random.key(seed)
        k_img, k_w, k_b, k_pos = jax.random.split(key, 4)
        B, H, W, C = (64, 96, 96, 3)
        patch_dim = P * P * C
        patch_count = H // P * (W // P)
        images = jax.random.normal(k_img, (B, H, W, C), dtype=jnp.float32)
        W_proj = jax.random.normal(k_w, (E, patch_dim), dtype=jnp.float32) * patch_dim ** (-0.5)
        b_proj = jax.random.normal(k_b, (E,), dtype=jnp.float32) * 0.02
        pos_emb = jax.random.normal(k_pos, (patch_count, E), dtype=jnp.float32) * 0.02
        return {'images': images, 'W_proj': W_proj, 'b_proj': b_proj, 'pos_emb': pos_emb}
    _L0_tok_all = _L0_tok_setup()
    _L0_tok_in = {k: v for k, v in _L0_tok_all.items() if k in ('W_proj', 'b_proj', 'pos_emb')}
    del _L0_tok_all

    def _L0_attn_setup():
        import jax, jax.numpy as jnp
        import numpy as np
        DIM = 256
        N_HEADS = 16
        HEAD_DIM = DIM // N_HEADS
        FREQS = [31.0, 37.0, 41.0, 43.0, 47.0]
        TWO_PI = 2.0 * float(np.pi)
        key = jax.random.key(seed)
        ks = jax.random.split(key, 16)
        B, L = (2, 256)
        s = 0.02
        inp = {'x': jax.random.normal(ks[0], (B, L, DIM), dtype=jnp.float32), 'Wq': jax.random.normal(ks[1], (DIM, DIM), dtype=jnp.float32) * s, 'bq': jnp.zeros((DIM,), dtype=jnp.float32), 'Wk': jax.random.normal(ks[2], (DIM, DIM), dtype=jnp.float32) * s, 'bk': jnp.zeros((DIM,), dtype=jnp.float32), 'Wv': jax.random.normal(ks[3], (DIM, DIM), dtype=jnp.float32) * s, 'bv': jnp.zeros((DIM,), dtype=jnp.float32), 'Wo': jax.random.normal(ks[4], (DIM, DIM), dtype=jnp.float32) * s, 'bo': jnp.zeros((DIM,), dtype=jnp.float32), 'alpha': jax.random.normal(ks[5], (N_HEADS, len(FREQS)), dtype=jnp.float32) * 0.1, 'phi': jax.random.uniform(ks[6], (N_HEADS, len(FREQS)), dtype=jnp.float32) * TWO_PI, 'temperature': jnp.ones((1,), dtype=jnp.float32), 'gamma': jnp.ones((DIM,), dtype=jnp.float32), 'beta': jnp.zeros((DIM,), dtype=jnp.float32)}
        return inp
    _L0_attn_all = _L0_attn_setup()
    _L0_attn_in = {k: v for k, v in _L0_attn_all.items() if k in ('Wq', 'bq', 'Wk', 'bk', 'Wv', 'bv', 'Wo', 'bo', 'alpha', 'phi', 'temperature', 'gamma', 'beta')}
    del _L0_attn_all

    def _L0_ffn_setup():
        import jax, jax.numpy as jnp
        import numpy as np
        D_MODEL = 256
        EXPANSION = 4
        D_HIDDEN = D_MODEL * EXPANSION
        NUM_STAGES = int(np.log2(D_HIDDEN))

        def butterfly(y, weights, dim):
            lead = y.shape[:-1]
            for stage in range(weights.shape[0]):
                s = 2 ** stage
                nb = dim // (2 * s)
                yr = y.reshape(*lead, nb, 2, s)
                a = yr[..., 0, :]
                b = yr[..., 1, :]
                w = weights[stage].reshape(nb, s, 2, 2)
                na = w[..., 0, 0] * a + w[..., 0, 1] * b
                nb2 = w[..., 1, 0] * a + w[..., 1, 1] * b
                y = jnp.stack([na, nb2], axis=-2).reshape(*lead, dim)
            return y
        key = jax.random.key(seed)
        ks = jax.random.split(key, 6)
        B, S = (4, 512)
        x = jax.random.normal(ks[0], (B, S, D_MODEL), jnp.float32)
        W_exp = jax.random.normal(ks[1], (D_MODEL, D_HIDDEN), jnp.float32) * 0.02
        b_exp = jnp.zeros((D_HIDDEN,), jnp.float32)
        up_weights = jax.random.normal(ks[2], (NUM_STAGES, D_HIDDEN // 2, 2, 2), jnp.float32) * 0.02
        up_bias = jnp.zeros((D_HIDDEN,), jnp.float32)
        down_weights = jax.random.normal(ks[3], (NUM_STAGES, D_HIDDEN // 2, 2, 2), jnp.float32) * 0.02
        W_con = jax.random.normal(ks[4], (D_HIDDEN, D_MODEL), jnp.float32) * 0.02
        b_con = jnp.zeros((D_MODEL,), jnp.float32)
        down_bias = jnp.zeros((D_MODEL,), jnp.float32)
        return dict(x=x, W_exp=W_exp, b_exp=b_exp, up_weights=up_weights, up_bias=up_bias, down_weights=down_weights, W_con=W_con, b_con=b_con, down_bias=down_bias)
    _L0_ffn_all = _L0_ffn_setup()
    _L0_ffn_in = {k: v for k, v in _L0_ffn_all.items() if k in ('W_exp', 'b_exp', 'up_weights', 'up_bias', 'down_weights', 'W_con', 'b_con', 'down_bias')}
    del _L0_ffn_all
    return {'x': x, 'L0_tok_W_proj': _L0_tok_in['W_proj'], 'L0_tok_b_proj': _L0_tok_in['b_proj'], 'L0_tok_pos_emb': _L0_tok_in['pos_emb'], 'L0_attn_Wq': _L0_attn_in['Wq'], 'L0_attn_bq': _L0_attn_in['bq'], 'L0_attn_Wk': _L0_attn_in['Wk'], 'L0_attn_bk': _L0_attn_in['bk'], 'L0_attn_Wv': _L0_attn_in['Wv'], 'L0_attn_bv': _L0_attn_in['bv'], 'L0_attn_Wo': _L0_attn_in['Wo'], 'L0_attn_bo': _L0_attn_in['bo'], 'L0_attn_alpha': _L0_attn_in['alpha'], 'L0_attn_phi': _L0_attn_in['phi'], 'L0_attn_temperature': _L0_attn_in['temperature'], 'L0_attn_gamma': _L0_attn_in['gamma'], 'L0_attn_beta': _L0_attn_in['beta'], 'L0_ffn_W_exp': _L0_ffn_in['W_exp'], 'L0_ffn_b_exp': _L0_ffn_in['b_exp'], 'L0_ffn_up_weights': _L0_ffn_in['up_weights'], 'L0_ffn_up_bias': _L0_ffn_in['up_bias'], 'L0_ffn_down_weights': _L0_ffn_in['down_weights'], 'L0_ffn_W_con': _L0_ffn_in['W_con'], 'L0_ffn_b_con': _L0_ffn_in['b_con'], 'L0_ffn_down_bias': _L0_ffn_in['down_bias']}

def reference(x, L0_tok_W_proj, L0_tok_b_proj, L0_tok_pos_emb, L0_attn_Wq, L0_attn_bq, L0_attn_Wk, L0_attn_bk, L0_attn_Wv, L0_attn_bv, L0_attn_Wo, L0_attn_bo, L0_attn_alpha, L0_attn_phi, L0_attn_temperature, L0_attn_gamma, L0_attn_beta, L0_ffn_W_exp, L0_ffn_b_exp, L0_ffn_up_weights, L0_ffn_up_bias, L0_ffn_down_weights, L0_ffn_W_con, L0_ffn_b_con, L0_ffn_down_bias):
    import jax
    import jax.numpy as jnp

    def _L0_tok_ref(images, W_proj, b_proj, pos_emb):
        import jax, jax.numpy as jnp
        import numpy as np
        P = 16
        E = 256

        def patchify(images, patch_size):
            B, H, W, C = images.shape
            hp, wp = (H // patch_size, W // patch_size)
            x = images.reshape(B, hp, patch_size, wp, patch_size, C)
            x = x.transpose(0, 1, 3, 2, 4, 5)
            return x.reshape(B, hp * wp, patch_size * patch_size * C)
        patches = patchify(images, P)
        out = jnp.einsum('bnd,ed->bne', patches, W_proj) + b_proj + pos_emb[None, :, :]
        return out

    def _L0_attn_ref(x, Wq, bq, Wk, bk, Wv, bv, Wo, bo, alpha, phi, temperature, gamma, beta):
        import jax, jax.numpy as jnp
        import numpy as np
        DIM = 256
        N_HEADS = 16
        HEAD_DIM = DIM // N_HEADS
        FREQS = [31.0, 37.0, 41.0, 43.0, 47.0]
        TWO_PI = 2.0 * float(np.pi)
        B, L, D = x.shape
        H, hd = (N_HEADS, HEAD_DIM)
        q = (x @ Wq.T + bq).reshape(B, L, H, hd).transpose(0, 2, 1, 3)
        k = (x @ Wk.T + bk).reshape(B, L, H, hd).transpose(0, 2, 1, 3)
        v = (x @ Wv.T + bv).reshape(B, L, H, hd).transpose(0, 2, 1, 3)
        sim = jnp.einsum('bhid,bhjd->bhij', q, k) / jnp.sqrt(jnp.asarray(hd, x.dtype))
        temp = jnp.abs(temperature)[0] + 0.1
        sim = sim / temp
        scores = jnp.zeros_like(sim)
        for fi, freq in enumerate(FREQS):
            a = alpha[:, fi][None, :, None, None]
            p = phi[:, fi][None, :, None, None]
            scores = scores + a * jnp.sin(TWO_PI * sim / freq + p)
        w = jax.nn.sigmoid(scores)
        w = w / (jnp.sum(w, axis=-1, keepdims=True) + 1e-10)
        out = jnp.einsum('bhij,bhjd->bhid', w, v)
        out = out.transpose(0, 2, 1, 3).reshape(B, L, D)
        out = out @ Wo.T + bo
        mu = jnp.mean(out, axis=-1, keepdims=True)
        var = jnp.mean(jnp.square(out - mu), axis=-1, keepdims=True)
        return (out - mu) / jnp.sqrt(var + 1e-05) * gamma + beta

    def _L0_ffn_ref(x, W_exp, b_exp, up_weights, up_bias, down_weights, W_con, b_con, down_bias):
        import jax, jax.numpy as jnp
        import numpy as np
        D_MODEL = 256
        EXPANSION = 4
        D_HIDDEN = D_MODEL * EXPANSION
        NUM_STAGES = int(np.log2(D_HIDDEN))

        def butterfly(y, weights, dim):
            lead = y.shape[:-1]
            for stage in range(weights.shape[0]):
                s = 2 ** stage
                nb = dim // (2 * s)
                yr = y.reshape(*lead, nb, 2, s)
                a = yr[..., 0, :]
                b = yr[..., 1, :]
                w = weights[stage].reshape(nb, s, 2, 2)
                na = w[..., 0, 0] * a + w[..., 0, 1] * b
                nb2 = w[..., 1, 0] * a + w[..., 1, 1] * b
                y = jnp.stack([na, nb2], axis=-2).reshape(*lead, dim)
            return y
        h = jnp.einsum('bsd,dh->bsh', x, W_exp) + b_exp
        h = butterfly(h, up_weights, D_HIDDEN)
        h = jax.nn.gelu(h + up_bias, approximate=False)
        h = butterfly(h, down_weights, D_HIDDEN)
        y = jnp.einsum('bsh,hd->bsd', h, W_con) + b_con
        return y + down_bias
    h = _L0_tok_ref(x, L0_tok_W_proj, L0_tok_b_proj, L0_tok_pos_emb)
    h = h + _L0_attn_ref(_layernorm(h, axis=-1), L0_attn_Wq, L0_attn_bq, L0_attn_Wk, L0_attn_bk, L0_attn_Wv, L0_attn_bv, L0_attn_Wo, L0_attn_bo, L0_attn_alpha, L0_attn_phi, L0_attn_temperature, L0_attn_gamma, L0_attn_beta)
    h = h + _L0_ffn_ref(_layernorm(h, axis=-1), L0_ffn_W_exp, L0_ffn_b_exp, L0_ffn_up_weights, L0_ffn_up_bias, L0_ffn_down_weights, L0_ffn_W_con, L0_ffn_b_con, L0_ffn_down_bias)
    return h

_drawn_inputs = setup_inputs


def setup_inputs(seed=0):
    import zlib

    import numpy as np

    out = dict(_drawn_inputs(seed))
    spreads = {'L0_attn_bq': (0.0, 2.0),
     'L0_attn_bk': (0.0, 2.0),
     'L0_attn_bv': (0.0, 0.1),
     'L0_attn_bo': (0.0, 0.1),
     'L0_attn_gamma': (1.0, 0.2),
     'L0_attn_beta': (0.0, 0.1),
     'L0_ffn_b_exp': (0.0, 0.1),
     'L0_ffn_up_bias': (0.0, 0.1),
     'L0_ffn_b_con': (0.0, 0.1),
     'L0_ffn_down_bias': (0.0, 0.1)}
    factors = {'L0_tok_b_proj': 2.767,
     'L0_tok_pos_emb': 4.006,
     'L0_attn_Wq': 8.0,
     'L0_attn_Wk': 8.0,
     'L0_attn_alpha': 8.0,
     'L0_attn_phi': 8.0}
    for name, (base, spread) in spreads.items():
        noise = np.random.default_rng([zlib.crc32(name.encode()), seed]).standard_normal(out[name].shape)
        drawn = base * np.exp(spread * noise) if base else spread * noise
        out[name] = jnp.asarray(drawn.astype(out[name].dtype))
    for name, factor in factors.items():
        out[name] = (out[name] * factor).astype(out[name].dtype)
    return out
```

```python
from contextlib import ExitStack

import numpy as np

import concourse.bass as bass
from concourse import mybir

F32 = mybir.dt.float32
ALU = mybir.AluOpType
ACT = mybir.ActivationFunctionType
AX = mybir.AxisListType

P = 128
IMAGES, SIDE, CH, PATCH = 64, 96, 3, 16
GRID = SIDE // PATCH
TOK = GRID * GRID
PD = PATCH * PATCH * CH
ROW = PATCH * CH
E = 256
HEADS, HD = 16, 16
FREQS = [31.0, 37.0, 41.0, 43.0, 47.0]
NF = len(FREQS)
HID = 1024
NB = HID // P
LOW = 7
TWO_PI = 2.0 * float(np.pi)
SIN_SCALE = 6.283185
ROUND = 12582912.0

G = 4
IPG = IMAGES // G
TPG = IPG * TOK
TILES = [(t * P, min(P, TPG - t * P)) for t in range((TPG + P - 1) // P)]
NT = len(TILES)
HALF = TPG // 2
BH = IPG * GRID
KC = PD // P
MAINQ = 32
RESTQ = TOK - MAINQ
PAIRS = IPG // 2
QUADS = IPG // 4
MAIN = 4 * PAIRS * TOK
REST = QUADS * TOK
COLS = MAIN + REST
SLOT = 64
WORK_BANKS = 3
ROWS_IN = TOK + 7


def turn_order():
    def front(g):
        first = [("xT", g, wp, c) for wp in range(GRID) for c in range(2)]
        return first + [("tok", g, t) for t in range(NT)]

    def qkv(g):
        names = [("lnT", g, 0, t) for t in range(NT)]
        names += [(w, g, hg, hf) for w in "qk" for hg in range(2) for hf in range(2)]
        return names + [("v", g, t) for t in range(NT)]

    names = [("wT", k) for k in range(KC)] + [("attnT", w, k) for w in range(4) for k in range(2)]
    names += [("expT", a) for a in range(NB)] + [("heads",)] + [("rows", k) for k in range(2 * NT)]
    for side in "ud":
        names += [("bits", side, s, c) for s in range(LOW) for c in range(2 if s == LOW - 1 else 1)]
        if side == "u":
            names += [("low", "u", a) for a in range(NB)]
            names += [("upT", k, c) for k in range(2) for c in range(2)]
        else:
            names += [("lowT", c) for c in range(2)] + [("low", "d", a) for a in range(NB)]
    names += front(0) + qkv(0)
    for g in range(G + 1):
        if g > 0:
            names += [("lnT", g - 1, 1, t) for t in range(NT)]
            names += [("mm1", g - 1, m, hf) for m in range(NB) for hf in range(2)]
        if g + 1 < G:
            names += front(g + 1)
        if g > 0:
            names += [("mm2", g - 1, t) for t in range(NT)]
        if g + 1 < G:
            names += qkv(g + 1)
        if g < G:
            names += [("o", g, t) for t in range(NT)]
    return names


def shape_constants():
    ident = np.eye(P, dtype=np.float32)
    p = np.arange(P)
    fold = (p[:, None] % 64 == np.arange(64)[None, :])
    par = np.stack([(p // HD) % 2 == 0, (p // HD) % 2 == 1], 1)
    pair = p[:, None] // 32 == np.arange(4)[None, :]
    misc = np.concatenate([ident, fold, par, pair], 1).astype(np.float32)
    heads = np.zeros((HEADS, 10, P), np.float32)
    for hg in range(2):
        for r in range(4):
            heads[8 * hg + 2 * r + (p // 32) % 2, hg * 5 + r, p] = 1
        heads[8 * hg + (p % 32) // RESTQ, hg * 5 + 4, p] = 1
    bits = np.zeros((64, LOW, 2, P), np.float32)
    for s in range(LOW):
        bits[p >> (s + 1), s, (p >> s) & 1, p] = 1
    rows = np.zeros((ROWS_IN, 2 * NT, P), np.float32)
    for tt, (t0, tn) in enumerate(TILES):
        q = np.arange(tn)
        rows[(t0 + q) % TOK, tt, q] = 1
        rows[TOK, tt, :] = 1
    for k in range(5):
        rows[TOK + 1 + k, NT + k, :] = 1
    rows[TOK + 6, 2 * NT - 1, :] = 1
    return misc, heads.reshape(HEADS, 10 * P), bits.reshape(64, LOW * 2 * P), rows.reshape(ROWS_IN, 2 * NT * P)


def build(nc, t):
    order = turn_order()
    turn = {name: i for i, name in enumerate(order)}
    with ExitStack() as ctx:
        def sb(name, *shape):
            return ctx.enter_context(nc.sbuf_tensor(name, list(shape), F32))

        def sem(name):
            return ctx.enter_context(nc.semaphore(name))

        work = [ctx.enter_context(nc.psum_tensor(f"work{k}", [P, 512], F32)) for k in range(WORK_BANKS)]
        att = [ctx.enter_context(nc.psum_tensor(f"att{k}", [P, 512], F32)) for k in range(5)]

        misc = sb("misc", P, P + 64 + 2 + 4)
        ident, fold = misc[:, 0:P], misc[:, P:P + 64]
        par_mask, pair_mask = misc[:, P + 64:P + 66], misc[:, P + 66:P + 70]
        phi_alpha = sb("phi_alpha", HEADS, 2 * NF)
        turns_alpha = sb("turns_alpha", P, 10, 2 * NF)
        temp = sb("temp", P, 4)
        inv_freq = sb("inv_freq", P, NF)
        w_tok = sb("w_tok", P, KC, E)
        w_attn = sb("w_attn", P, 4, 2, E)
        w_up = sb("w_up", P, 2, HID)
        w_down = sb("w_down", P, NB, E)
        hid_bias = sb("hid_bias", P, NB)
        up_bias = sb("up_bias", P, NB)
        rows = sb("rows", P, 2 * NT, E)
        pos = rows[:, 0:NT, :]
        row_bv, row_bo, row_gamma, row_beta, row_con = (rows[:, NT + n, :] for n in range(5))
        qk_bias = sb("qk_bias", P, 2, 2)
        q_bias = sb("q_bias", P, 2, 2)
        half_pow = sb("half_pow", P, NT)
        high = sb("high", P, 2, 3, 4, 4)

        x_in = sb("x_in", BH, GRID, PD)
        pat_wo = sb("pat_wo", P, KC * TPG)
        patT = pat_wo[:, :].rearrange("p (k t) -> p k t", k=KC)
        WN = 2 * 2 * 2 * 8 * TOK
        wT = pat_wo[:, 0:WN].rearrange("p (n i m h q) -> p n i m h q", n=2, i=2, m=2, h=8)
        oT = pat_wo[:, WN:WN + 2 * TPG].rearrange("p (m b i) -> p m b i", m=2, b=IPG)
        h = sb("h", P, 3, NT, E)
        hb_on = sb("hb_on", P, 2 * NT * E)
        hb = hb_on[:, 0:NT * E].rearrange("p (t e) -> p t e", e=E)
        on = hb_on[:, NT * E:].rearrange("p (t e) -> p t e", e=E)
        xn = sb("xn", P, NT, E)
        xnT = sb("xnT", P, 2, TPG)
        stats = sb("stats", P, NT, 6)
        mv = sb("mv", P, 3, NT, 2)
        var = sb("var", P, 3, NT)
        rstd = sb("rstd", P, 3, NT)
        qm = sb("qm", P, 2, 2, TPG)
        kT = sb("kT", P, 2, TPG)
        q_rest = sb("q_rest", P, 2, IPG, 32)
        v_sl = sb("v_sl", P, QUADS, 2, E)
        sun = sb("sun", P, 5, COLS)
        s, u, n = sun[:, 0:2, :], sun[:, 2, :], sun[:, 3:5, :]
        acc = sb("acc", P, 2, 4, PAIRS, SLOT)
        acc_rest = sb("acc_rest", P, 2, QUADS, TOK)
        w_rest = sb("w_rest", P, 2, QUADS, 2, SLOT)
        sums = sb("sums", P, 2, 4 * PAIRS + QUADS)
        rsums = sb("rsums", P, 2, 4 * PAIRS + QUADS)
        even = sb("even", P, 2, 4, TOK)
        gT = sb("gT", P, NB, TPG)

        gT_f = gT[:, :, :].rearrange("p a b -> p (a b)")
        nat_tok = gT_f[:, 0:2 * PD].rearrange("p (m d) -> p m d", m=2)
        nat_attn = gT_f[:, 2 * PD:2 * PD + 8 * E].rearrange("p (w m e) -> p w m e", w=4, m=2)
        sun_f = sun[:, :, :].rearrange("p a b -> p (a b)")
        nat_exp = sun_f[:, 0:2 * HID].rearrange("p (m d) -> p m d", m=2)
        EB = E + 1
        expT = pat_wo[:, 0:NB * EB].rearrange("p (a e) -> p a e", a=NB)
        mixA = gT_f[:, 0:NB * EB].rearrange("p (a e) -> p a e", a=NB)
        qm_f = qm[:, :, :, :].rearrange("p a b c -> p (a b c)")
        mixB = qm_f[:, 0:NB * EB].rearrange("p (a e) -> p a e", a=NB)
        row_src = xnT[0:ROWS_IN, 0, 0:E]
        row_sel = hb_on[0:ROWS_IN, 0:2 * NT * P]
        head_sel = hb_on[0:HEADS, 2 * NT * P:2 * NT * P + 10 * P]
        h_f = h[:, 1:3, :, :].rearrange("p a b c -> p (a b c)")
        chain = [h_f[:, k * HID:(k + 1) * HID] for k in range(2)]
        v_f = v_sl[:, :, :, :].rearrange("p a b c -> p (a b c)")
        bit_sel = v_f[0:64, 0:LOW * 2 * P].rearrange("p (s i q) -> p s i q", s=LOW, i=2)
        kT_f = kT[:, :, :].rearrange("p a b -> p (a b)")
        lowT = kT_f[:, 0:HID].rearrange("p (a o) -> p a o", a=NB)
        acc_f = acc[:, :, :, :, :].rearrange("p a b c d -> p (a b c d)")
        stage_at = [32 * (2 ** st - 1) for st in range(LOW + 1)]
        stage_w = {}
        for side, flat in (("u", acc_f), ("d", sun_f[:, 2 * HID:])):
            for st in range(LOW):
                part = flat[0:2 ** (LOW - 1 - st), stage_at[st]:stage_at[st + 1]]
                stage_w[side, st] = part.rearrange("p (a k) -> p a k", a=NB)

        v_dram = nc.dram_tensor("v_scratch", (G, TPG, E), F32)

        filled = [sem(f"work_filled{k}") for k in range(WORK_BANKS)]
        drained = [sem(f"work_drained{k}") for k in range(WORK_BANKS)]
        small_loaded = sem("small_loaded")
        nat_loaded = sem("nat_loaded")
        exp_loaded = sem("exp_loaded")
        bits_loaded = sem("bits_loaded")
        down_bits_loaded = sem("down_bits_loaded")
        con_loaded = sem("con_loaded")
        x_loaded = [sem(f"x_loaded{wp}") for wp in range(GRID)]
        v_stored = sem("v_stored")
        v_loaded = sem("v_loaded")
        out_stored = sem("out_stored")
        consts_ready = sem("consts_ready")
        pool_ready = sem("pool_ready")
        mix_first = sem("mix_first")
        mix_done = sem("mix_done")
        hid_ready = sem("hid_ready")
        scores_filled = sem("scores_filled")
        scores_drained = sem("scores_drained")
        u_ready = sem("u_ready")
        rounded = sem("rounded")
        frac_ready = sem("frac_ready")
        sin_ready = sem("sin_ready")
        acc_done = sem("acc_done")
        weights_ready = sem("weights_ready")
        sums_step = sem("sums_step")
        recip_ready = sem("recip_ready")
        normed = sem("normed")
        rest_normed = sem("rest_normed")
        pads_zero = sem("pads_zero")
        trans_filled = sem("trans_filled")
        wT_act = sem("wT_act")
        wT_dve = sem("wT_dve")
        pv_filled = sem("pv_filled")
        even_ready = sem("even_ready")
        oT_ready = sem("oT_ready")
        stat_step = sem("stat_step")
        mv_ready = sem("mv_ready")
        var_ready = sem("var_ready")
        rstd_ready = sem("rstd_ready")
        xn_ready = sem("xn_ready")
        hb_ready = sem("hb_ready")
        on_step = sem("on_step")
        h1_ready = sem("h1_ready")
        q_rest_ready = sem("q_rest_ready")
        hc_ready = sem("hc_ready")

        def open_turn(pe, *name):
            i = turn[name]
            if i >= WORK_BANKS:
                pe.wait_ge(drained[i % WORK_BANKS], i // WORK_BANKS)
            return work[i % WORK_BANKS]

        def close_turn(ins, *name):
            ins.then_inc(filled[turn[name] % WORK_BANKS], 1)

        def wait_filled(eng, *name):
            i = turn[name]
            eng.wait_ge(filled[i % WORK_BANKS], i // WORK_BANKS + 1)
            return work[i % WORK_BANKS]

        def drain(ins, *name):
            ins.then_inc(drained[turn[name] % WORK_BANKS], 1)

        def wait_drained(eng, *name):
            i = turn[name]
            eng.wait_ge(drained[i % WORK_BANKS], i // WORK_BANKS + 1)

        ln_order = [(0, 0)]
        for g in range(G):
            ln_order += [(g + 1, 0)] * (g + 1 < G) + [(g, 1), (g, 2)]
        ln_at = {name: k for k, name in enumerate(ln_order)}
        xn_at = {(0, 0): 0}
        for g in range(G + 1):
            for name in ([(g - 1, 1)] if g > 0 else []) + ([(g + 1, 0)] if g + 1 < G else []):
                xn_at[name] = len(xn_at)

        misc_in, head_in, bit_in = t["misc"], t["heads"], t["bits"]
        block = ctx.enter_context(nc.Block())

        small = [
            (misc[:, :], misc_in), (head_sel[:, :], head_in),
            (phi_alpha[:, 0:NF], t["L0_attn_phi"]), (phi_alpha[:, NF:2 * NF], t["L0_attn_alpha"]),
            (temp[:, 0:1], t["L0_attn_temperature"].partition_broadcast(P)),
            (up_bias[:, :], t["L0_ffn_up_bias"].rearrange("(a p) -> p a", p=P)),
            (row_sel, t["rows"]),
            (row_src[0:TOK], t["L0_tok_pos_emb"]),
            (qk_bias[:, 0, :], t["L0_attn_bq"].rearrange("(m p) -> p m", p=P)),
            (qk_bias[:, 1, :], t["L0_attn_bk"].rearrange("(m p) -> p m", p=P)),
        ]
        for side, name in ((0, "up"), (1, "down")):
            w = t[f"L0_ffn_{name}_weights"]
            for st in range(3):
                small.append((high[:, side, st, :, :],
                              w[LOW + st].rearrange("(g p) o i -> p g (o i)", p=P)))
        for k, name in enumerate(("tok_b_proj", "attn_bv", "attn_bo", "attn_gamma", "attn_beta", "ffn_b_con",
                                  "ffn_down_bias")):
            small.append((row_src[TOK + k:TOK + k + 1], t[f"L0_{name}"].unsqueeze(0)))

        def mix_buffers(side, step):
            if side == 1 and step == 0:
                return w_down, mixB, E
            pair = (mixA, mixB) if step % 2 == 0 else (mixB, mixA)
            return *pair, EB if side == 0 else E

        def load_stages(eng, side, name):
            w = t[f"L0_ffn_{name}_weights"]
            for st in range(LOW):
                src = w[st].rearrange("(a i k) o j -> i a (k o j)", a=NB, k=2 ** st)
                eng.dma_start(stage_w[side, st], src).then_inc(bits_loaded if side == "u" else down_bits_loaded, 16)

        @block.sync
        def _(sp):
            def load_x(g):
                src = t["x"][g * IPG:(g + 1) * IPG].rearrange(
                    "b (hp i) (wp j) c -> (b hp) wp i (j c)", hp=GRID, wp=GRID)
                for wp in range(GRID):
                    if g > 0:
                        wait_filled(sp, "xT", g - 1, wp, 1)
                    sp.dma_start(x_in[:, wp, :].rearrange("p (i k) -> p i k", i=PATCH),
                                 src[:, wp]).then_inc(x_loaded[wp], 16)

            def move_v(g):
                wait_drained(sp, "v", g, NT - 1)
                full = TPG // P
                sp.dma_start(v_dram.ap()[g, 0:full * P, :].rearrange("(t p) e -> p t e", p=P),
                             xn[:, 0:full, :]).then_inc(v_stored, 16)
                sp.dma_start(v_dram.ap()[g, full * P:TPG, :], xn[0:TPG - full * P, full, :]).then_inc(v_stored, 16)
                sp.wait_ge(v_stored, 32 * (g + 1))
                if g > 0:
                    sp.wait_ge(pv_filled, QUADS * g)
                view = v_dram.ap()[g].rearrange("(q s i j) e -> s i j q e", q=QUADS, s=2, i=2)
                for sl in range(2):
                    for i in range(2):
                        sp.dma_start(v_sl[SLOT * sl:SLOT * sl + TOK, :, i, :], view[sl, i]).then_inc(v_loaded, 16)

            for w, name in enumerate(("Wq", "Wk", "Wv", "Wo")):
                sp.dma_start(nat_attn[:, w], t[f"L0_attn_{name}"].rearrange("(m p) e -> p m e", p=P))\
                  .then_inc(nat_loaded, 16)
            sp.dma_start(nat_tok, t["L0_tok_W_proj"].rearrange("(m p) d -> p m d", p=P)).then_inc(nat_loaded, 16)
            load_stages(sp, "u", "up")
            sp.dma_start(w_down[:, :, :], t["L0_ffn_W_con"].rearrange("(a p) e -> p a e", p=P)).then_inc(con_loaded, 16)
            sp.dma_start(bit_sel, bit_in.rearrange("p (s i q) -> p s i q", s=LOW, i=2)).then_inc(bits_loaded, 16)
            load_x(0)
            load_stages(sp, "d", "down")
            load_x(1)
            move_v(0)
            for g in range(G + 1):
                if g + 2 < G:
                    load_x(g + 2)
                if g > 0:
                    for tt, (t0, tn) in enumerate(TILES):
                        wait_drained(sp, "mm2", g - 1, tt)
                        sp.dma_start(t["out"].rearrange("b n e -> (b n) e")[
                            (g - 1) * TPG + t0:(g - 1) * TPG + t0 + tn, :],
                            h[0:tn, (g - 1) % 3, tt, :]).then_inc(out_stored, 16)
                if g + 1 < G:
                    move_v(g + 1)
            sp.wait_ge(out_stored, 16 * NT * G)

        @block.tensor
        def _(pe):
            def flip(out, in_, rows_):
                return pe.transpose(out, in_, ident[0:rows_, 0:rows_])

            pe.wait_ge(small_loaded, 16 * len(small))
            pe.wait_ge(nat_loaded, 16 * 5)
            for k in range(KC):
                b = open_turn(pe, "wT", k)
                for m in range(2):
                    ins = flip(b[:, m * P:(m + 1) * P], nat_tok[:, m, k * P:(k + 1) * P], P)
                close_turn(ins, "wT", k)
            for w in range(4):
                for k in range(2):
                    b = open_turn(pe, "attnT", w, k)
                    for m in range(2):
                        ins = flip(b[:, m * P:(m + 1) * P], nat_attn[:, w, m, k * P:(k + 1) * P], P)
                    close_turn(ins, "attnT", w, k)
            pe.wait_ge(exp_loaded, 32)
            for a in range(NB):
                b = open_turn(pe, "expT", a)
                for m in range(2):
                    ins = flip(b[:, m * P:(m + 1) * P], nat_exp[:, m, a * P:(a + 1) * P], P)
                close_turn(ins, "expT", a)
            b = open_turn(pe, "heads")
            for k in range(10):
                ins = pe.matmul(b[:, k * 2 * NF:(k + 1) * 2 * NF], head_sel[:, k * P:(k + 1) * P],
                                phi_alpha[:, :], start=True, stop=True)
            close_turn(ins, "heads")
            for k in range(2 * NT):
                b = open_turn(pe, "rows", k)
                close_turn(pe.matmul(b[:, 0:E], row_sel[:, k * P:(k + 1) * P], row_src, start=True, stop=True),
                           "rows", k)

            def stage_bits(side):
                for st in range(LOW):
                    rows_ = 2 ** (LOW - 1 - st)
                    parts = 2 if st == LOW - 1 else 1
                    for c in range(parts):
                        blocks = NB // parts
                        b = open_turn(pe, "bits", side, st, c)
                        width = blocks * 2 ** (st + 1)
                        for i in range(2):
                            src = stage_w[side, st][:, c * blocks:(c + 1) * blocks, :]
                            src = src.rearrange("p a (k i) -> p a k i", i=2)[:, :, :, i]
                            ins = pe.matmul(b[:, 0:width].rearrange("p (a k) -> p a k", a=blocks),
                                            bit_sel[0:rows_, st, i, :], src,
                                            start=(i == 0), stop=(i == 1))
                        close_turn(ins, "bits", side, st, c)

            def chain_out(side):
                return chain[LOW % 2].rearrange("p (a o) -> p a o", a=NB)

            pe.wait_ge(bits_loaded, 16 * (LOW + 1))
            stage_bits("u")
            wait_drained(pe, "bits", "u", LOW - 1, 1)
            wait_drained(pe, "expT", NB - 1)
            for a in range(NB):
                b = open_turn(pe, "low", "u", a)
                ins = pe.matmul(b[:, 0:EB], chain_out("u")[:, a, :], expT[:, a, :], start=True, stop=True)
                close_turn(ins, "low", "u", a)
            pe.wait_ge(mix_done, 3)
            for k in range(2):
                for c in range(2):
                    b = open_turn(pe, "upT", k, c)
                    for a in range(4):
                        ins = flip(b[:, a * P:(a + 1) * P], mixB[:, 4 * c + a, k * P:(k + 1) * P], P)
                    close_turn(ins, "upT", k, c)
            pe.wait_ge(down_bits_loaded, 16 * LOW)
            stage_bits("d")
            wait_drained(pe, "bits", "d", LOW - 1, 1)
            for c in range(2):
                b = open_turn(pe, "lowT", c)
                for a in range(4):
                    ins = flip(b[:, a * P:(a + 1) * P], chain_out("d")[:, 4 * c + a, :], P)
                close_turn(ins, "lowT", c)
            wait_drained(pe, "lowT", 1)
            pe.wait_ge(mix_done, 6)
            for a in range(NB):
                b = open_turn(pe, "low", "d", a)
                ins = pe.matmul(b[:, 0:E], lowT[:, a, :], mixB[:, a, 0:E], start=True, stop=True)
                close_turn(ins, "low", "d", a)

            def front(g):
                for wp in range(GRID):
                    pe.wait_ge(x_loaded[wp], 16 * (g + 1))
                    for c in range(2):
                        b = open_turn(pe, "xT", g, wp, c)
                        for k in range(3):
                            d0 = (3 * c + k) * P
                            ins = flip(b[:, k * BH:(k + 1) * BH], x_in[:, wp, d0:d0 + P], BH)
                        close_turn(ins, "xT", g, wp, c)
                wait_drained(pe, "xT", g, GRID - 1, 1)
                wait_drained(pe, "xT", g, GRID - 1, 0)
                for tt, (t0, tn) in enumerate(TILES):
                    b = open_turn(pe, "tok", g, tt)
                    for k in range(KC):
                        ins = pe.matmul(b[0:tn, 0:E], patT[:, k, t0:t0 + tn], w_tok[:, k, :],
                                        start=(k == 0), stop=(k == KC - 1))
                    close_turn(ins, "tok", g, tt)

            def ln_turns(g, which):
                for tt, (t0, tn) in enumerate(TILES):
                    pe.wait_ge(xn_ready, NT * xn_at[g, which] + tt + 1)
                    b = open_turn(pe, "lnT", g, which, tt)
                    for k in range(2):
                        ins = flip(b[:, k * P:k * P + tn], xn[0:tn, tt, k * P:(k + 1) * P], tn)
                    close_turn(ins, "lnT", g, which, tt)
                for tt in range(NT):
                    wait_drained(pe, "lnT", g, which, tt)

            def qkv(g):
                ln_turns(g, 0)
                for wi, w in enumerate("qk"):
                    for hg in range(2):
                        for hf in range(2):
                            b = open_turn(pe, w, g, hg, hf)
                            for k in range(2):
                                ins = pe.matmul(b[:, 0:HALF], w_attn[:, wi, k, hg * P:(hg + 1) * P],
                                                xnT[:, k, hf * HALF:(hf + 1) * HALF],
                                                start=(k == 0), stop=(k == 1))
                            close_turn(ins, w, g, hg, hf)
                for tt, (t0, tn) in enumerate(TILES):
                    b = open_turn(pe, "v", g, tt)
                    for k in range(2):
                        ins = pe.matmul(b[0:tn, 0:E], xnT[:, k, t0:t0 + tn], w_attn[:, 2, k, :],
                                        start=(k == 0), stop=(k == 1))
                    close_turn(ins, "v", g, tt)

            def scores(g):
                for hg in range(2):
                    wait_drained(pe, "q", g, hg, 0)
                    wait_drained(pe, "q", g, hg, 1)
                    wait_drained(pe, "k", g, hg, 0)
                    wait_drained(pe, "k", g, hg, 1)
                    pe.wait_ge(q_rest_ready, 2 * g + hg + 1)
                    if hg == 0 and g > 0:
                        pe.wait_ge(wT_act, QUADS * g)
                        pe.wait_ge(wT_dve, QUADS * g)
                        pe.wait_ge(oT_ready, 2 * QUADS * g)
                    if hg == 1:
                        pe.wait_ge(scores_drained, 2 * g + 1)
                    for m in range(PAIRS):
                        for r in range(4):
                            for i in range(2):
                                for par in range(2):
                                    t0 = (2 * m + i) * TOK
                                    c = 32 * (2 * i + par)
                                    pe.matmul(att[r][c:c + 32, m * TOK:(m + 1) * TOK],
                                              qm[32 * r:32 * r + 32, hg, par, t0:t0 + MAINQ],
                                              kT[32 * r:32 * r + 32, hg, t0:t0 + TOK],
                                              start=True, stop=True, skip_group_check=True)
                    for im in range(IPG):
                        c = 32 * (im % 4)
                        ins = pe.matmul(att[4][c:c + 32, (im // 4) * TOK:(im // 4 + 1) * TOK],
                                        q_rest[:, hg, im, :], kT[:, hg, im * TOK:(im + 1) * TOK],
                                        start=True, stop=True, skip_group_check=True)
                    ins.then_inc(scores_filled, 1)

            def turn_weights(g, q):
                if q == 0:
                    pe.wait_ge(normed, 2 * (g + 1))
                    pe.wait_ge(rest_normed, g + 1)
                    pe.wait_ge(scores_drained, 2 * g + 2)
                else:
                    pe.wait_ge(wT_act, QUADS * g + q)
                    pe.wait_ge(wT_dve, QUADS * g + q)
                for hg in range(2):
                    for r in range(4):
                        flip(att[hg][:, r * P:(r + 1) * P],
                             acc[:, hg, r, 2 * q:2 * q + 2, :].rearrange("p a b -> p (a b)"), P)
                for hg in range(2):
                    ins = pe.matmul(att[4][:, hg * 64:(hg + 1) * 64],
                                    w_rest[:, hg, q, :, :].rearrange("p a b -> p (a b)"), fold,
                                    start=True, stop=True, skip_group_check=True)
                ins.then_inc(trans_filled, 1)

            def values(g, q):
                n_ = QUADS * g + q
                pe.wait_ge(wT_act, n_ + 1)
                pe.wait_ge(wT_dve, n_ + 1)
                pe.wait_ge(v_loaded, 64 * (g + 1))
                if q > 0:
                    pe.wait_ge(oT_ready, 2 * n_)
                for hg in range(2):
                    for i in range(2):
                        for r in range(4):
                            for sl in range(2):
                                p0 = SLOT * sl
                                ins = pe.matmul(
                                    att[2 + sl][32 * r:32 * r + 32, (hg * 2 + i) * 72:(hg * 2 + i + 1) * 72],
                                    v_sl[p0:p0 + TOK, q, i, hg * P + 32 * r:hg * P + 32 * r + 32],
                                    wT[p0:p0 + TOK, n_ % 2, i, hg, 2 * r:2 * r + 2, :].rearrange(
                                        "p a b -> p (a b)"),
                                    start=True, stop=True, skip_group_check=True)
                ins.then_inc(pv_filled, 1)

            def out_proj(g):
                pe.wait_ge(oT_ready, 2 * QUADS * (g + 1))
                flat = oT[:, :, :, :].rearrange("p m b i -> p m (b i)")
                for tt, (t0, tn) in enumerate(TILES):
                    b = open_turn(pe, "o", g, tt)
                    for k in range(2):
                        ins = pe.matmul(b[0:tn, 0:E], flat[:, k, t0:t0 + tn], w_attn[:, 3, k, :],
                                        start=(k == 0), stop=(k == 1))
                    close_turn(ins, "o", g, tt)

            def mm1(g):
                for m in range(NB):
                    for hf in range(2):
                        b = open_turn(pe, "mm1", g, m, hf)
                        for k in range(2):
                            ins = pe.matmul(b[:, 0:HALF], w_up[:, k, m * P:(m + 1) * P],
                                            xnT[:, k, hf * HALF:(hf + 1) * HALF],
                                            start=(k == 0), stop=(k == 1))
                        close_turn(ins, "mm1", g, m, hf)

            def mm2(g):
                wait_drained(pe, "mm1", g, NB - 1, 1)
                for tt, (t0, tn) in enumerate(TILES):
                    b = open_turn(pe, "mm2", g, tt)
                    for k in range(NB):
                        ins = pe.matmul(b[0:tn, 0:E], gT[:, k, t0:t0 + tn], w_down[:, k, :],
                                        start=(k == 0), stop=(k == NB - 1))
                    close_turn(ins, "mm2", g, tt)

            wait_drained(pe, "low", "d", NB - 1)
            pe.wait_ge(pool_ready, 3)
            pe.wait_ge(pads_zero, 1)
            front(0)
            qkv(0)
            for g in range(G + 1):
                if g < G:
                    scores(g)
                if g > 0:
                    ln_turns(g - 1, 1)
                    mm1(g - 1)
                if g + 1 < G:
                    front(g + 1)
                if g > 0:
                    mm2(g - 1)
                if g + 1 < G:
                    qkv(g + 1)
                if g < G:
                    turn_weights(g, 0)
                    for q in range(QUADS):
                        if q + 1 < QUADS:
                            turn_weights(g, q + 1)
                        values(g, q)
                    out_proj(g)

        def drain_xT(eng, copy, g, wp, c):
            b = wait_filled(eng, "xT", g, wp, c)
            if g > 0:
                wait_filled(eng, "tok", g - 1, NT - 1)
            dst = patT[:, 3 * c:3 * c + 3, :].rearrange("p k (r w) -> p k r w", w=GRID)[:, :, :, wp]
            drain(copy(dst, b[:, 0:3 * BH].rearrange("p (k r) -> p k r", k=3)), "xT", g, wp, c)

        XT_ACT = [(wp, 0) for wp in range(GRID)]
        XT_DVE = [(wp, 1) for wp in range(GRID)]

        @block.scalar
        def _(act):
            def copy(dst, src):
                return act.activation(dst, src, ACT.Identity)

            for dst, src in small:
                act.dma_start(dst, src, allow_slow_non_contiguous=True).then_inc(small_loaded, 16)
            act.dma_start(nat_exp, t["L0_ffn_W_exp"].rearrange("(m p) d -> p m d", p=P)).then_inc(exp_loaded, 16)
            act.dma_start(expT[:, :, E:EB], t["L0_ffn_b_exp"].rearrange("(a p u) -> p a u", p=P, u=1),
                          allow_slow_non_contiguous=True).then_inc(exp_loaded, 16)
            act.wait_ge(small_loaded, 16 * len(small))
            for w in range(4):
                for k in range(2):
                    b = wait_filled(act, "attnT", w, k)
                    drain(copy(w_attn[:, w, k, :], b[:, 0:E]), "attnT", w, k)
            for a in range(NB):
                b = wait_filled(act, "expT", a)
                drain(copy(expT[:, a, 0:E], b[:, 0:E]), "expT", a)

            def mix(side, base):
                for step in range(3):
                    st = step if side == 0 else 2 - step
                    src, dst, width = mix_buffers(side, step)
                    if base + step > 0:
                        act.wait_ge(mix_done, base + step)
                    for pr in range(4):
                        lo = ((pr >> st) << (st + 1)) | (pr & (2 ** st - 1))
                        blk = [lo, lo + 2 ** st]
                        for o in range(2):
                            co = high[:, side, st, pr, 3 * o:3 * o + 1]
                            ins = act.activation(dst[:, blk[o], 0:width], src[:, blk[o], 0:width],
                                                 ACT.Copy, scale=co)
                    ins.then_inc(mix_first, 1)

            for a in range(NB):
                b = wait_filled(act, "low", "u", a)
                ins = copy(mixA[:, a, :], b[:, 0:EB])
                drain(ins, "low", "u", a)
            wait_drained(act, "low", "u", NB - 1)
            mix(0, 0)
            for k in range(2):
                for c in range(2):
                    b = wait_filled(act, "upT", k, c)
                    drain(copy(w_up[:, k, c * 512:(c + 1) * 512], b[:, :]), "upT", k, c)
            act.wait_ge(con_loaded, 16)
            act.wait_ge(hid_ready, 1)
            mix(1, 3)
            for a in range(NB):
                b = wait_filled(act, "low", "d", a)
                drain(copy(w_down[:, a, :], b[:, 0:E]), "low", "d", a)
            act.wait_ge(mix_done, 6)

            def drain_ln(g, which):
                dst = xnT
                for tt, (t0, tn) in enumerate(TILES):
                    b = wait_filled(act, "lnT", g, which, tt)
                    if which == 0 and g > 1:
                        wait_filled(act, "mm1", g - 2, NB - 1, 1)
                    if which == 1:
                        wait_filled(act, "v", min(g + 1, G - 1), NT - 1)
                    drain(copy(dst[:, :, t0:t0 + tn],
                               b[:, 0:2 * P].rearrange("p (k c) -> p k c", k=2)[:, :, 0:tn]), "lnT", g, which, tt)

            def drain_q(g, hg, hf):
                b = wait_filled(act, "q", g, hg, hf)
                if g > 0:
                    act.wait_ge(scores_filled, 2 * g)
                    act.wait_ge(q_rest_ready, 2 * g)
                for par in range(2):
                    ins = act.activation(qm[:, hg, par, hf * HALF:(hf + 1) * HALF], b[:, 0:HALF], ACT.Identity,
                                         bias=q_bias[:, hg, par:par + 1], scale=par_mask[:, par:par + 1])
                drain(ins, "q", g, hg, hf)

            def drain_scores(g, hg):
                act.wait_ge(scores_filled, 2 * g + hg + 1)
                if g > 0:
                    act.wait_ge(u_ready, 2 * NF * g)
                for r in range(4):
                    copy(s[:, hg, r * PAIRS * TOK:(r + 1) * PAIRS * TOK], att[r][:, 0:PAIRS * TOK])
                copy(s[:, hg, MAIN:COLS], att[4][:, 0:REST]).then_inc(scores_drained, 1)

            def arguments(g, hg, f):
                c = 2 * NF * g + NF * hg + f
                act.wait_ge(scores_drained, 2 * g + hg + 1)
                if c >= 1:
                    act.wait_ge(frac_ready, c)
                for k in range(5):
                    a0 = k * PAIRS * TOK
                    a1 = a0 + (PAIRS * TOK if k < 4 else REST)
                    ins = act.activation(u[:, a0:a1], s[:, hg, a0:a1], ACT.Identity,
                                         bias=turns_alpha[:, 5 * hg + k, f:f + 1], scale=inv_freq[:, f:f + 1])
                ins.then_inc(u_ready, 1)

            def sine(g, hg, f):
                c = 2 * NF * g + NF * hg + f
                act.wait_ge(frac_ready, c + 1)
                act.activation(n[:, c % 2, :], n[:, c % 2, :], ACT.Sin, scale=SIN_SCALE).then_inc(sin_ready, 1)

            def sigmoids(g):
                for hg in range(2):
                    act.wait_ge(acc_done, 2 * NF * g + NF * (hg + 1))
                    v = acc[:, hg, :, :, 0:TOK].rearrange("p r m j -> p (r m) j")
                    act.activation(v, v, ACT.Sigmoid)
                    v = acc_rest[:, hg, :, :]
                    act.activation(v, v, ACT.Sigmoid).then_inc(weights_ready, 1)

            def drain_weights(g, q):
                n_ = QUADS * g + q
                act.wait_ge(trans_filled, n_ + 1)
                if n_ >= 2:
                    act.wait_ge(pv_filled, n_ - 1)
                for i in range(2):
                    ins = copy(wT[:, n_ % 2, i, 0, :, 0:MAINQ].rearrange("p (r a) q -> p r a q", a=2),
                         att[0][:, :].rearrange("p (r i a q) -> p i r a q", r=4, i=2, a=2)[:, i])
                ins.then_inc(wT_act, 1)

            def even_heads(g, q):
                n_ = QUADS * g + q
                act.wait_ge(pv_filled, n_ + 1)
                if n_ >= 1:
                    act.wait_ge(oT_ready, 2 * n_)
                for sl in range(2):
                    src = att[2 + sl][:, 0:288].rearrange("p (x a i) -> p x a i", x=4, a=2)[:, :, 0, :]
                    act.activation(even[:, sl, :, :], src, ACT.Copy, scale=par_mask[:, 0:1])\
                       .then_inc(even_ready, 1)

            def gelus(g, lo, hi):
                for m in range(lo, hi):
                    for hf in range(2):
                        b = wait_filled(act, "mm1", g, m, hf)
                        if g > 0:
                            wait_filled(act, "mm2", g - 1, NT - 1)
                        drain(act.activation(gT[:, m, hf * HALF:(hf + 1) * HALF], b[:, 0:HALF], ACT.Gelu,
                                             bias=hid_bias[:, m:m + 1]), "mm1", g, m, hf)

            def front_step(g, i):
                if i == 3:
                    for wp, c in XT_ACT[0:3]:
                        drain_xT(act, copy, g, wp, c)
                if i == 4:
                    for wp, c in XT_ACT[3:6]:
                        drain_xT(act, copy, g, wp, c)

            def front_end(g):
                drain_ln(g, 0)
                for hg in range(2):
                    for hf in range(2):
                        drain_q(g, hg, hf)

            for wp, c in XT_ACT:
                drain_xT(act, copy, 0, wp, c)
            front_end(0)
            steps = [(hg, f) for hg in range(2) for f in range(NF)]
            for g in range(G + 1):
                if g < G:
                    drain_scores(g, 0)
                    drain_scores(g, 1)
                    arguments(g, *steps[0])
                if g > 0:
                    drain_ln(g - 1, 1)
                    gelus(g - 1, 0, NB)
                if g < G:
                    for i in range(len(steps)):
                        if i + 1 < len(steps):
                            arguments(g, *steps[i + 1])
                        sine(g, *steps[i])
                        if g + 1 < G:
                            front_step(g + 1, i)
                    sigmoids(g)
                    if g + 1 < G:
                        front_end(g + 1)
                    drain_weights(g, 0)
                    for q in range(QUADS):
                        if q + 1 < QUADS:
                            drain_weights(g, q + 1)
                        even_heads(g, q)

        @block.gpsimd
        def _(pool):
            pool.memset(half_pow[:, :], -0.5).then_inc(pool_ready, 1)
            pool.memset(mv[:, :, :, :], 1.0).then_inc(pool_ready, 1)
            pool.memset(w_rest[:, :, :, :, :], 0.0).then_inc(pool_ready, 1)
            wait_filled(pool, "bits", "u", LOW - 1, 1)
            pool.memset(acc_f, 0.0).then_inc(pads_zero, 1)

            def inv_std(g, which):
                k = ln_at[g, which]
                pool.wait_ge(mv_ready, k + 1)
                pool.tensor_scalar(var[:, which, :], mv[:, which, :, 1], 1e-5, 1.0, ALU.add, ALU.mult)\
                    .then_inc(var_ready, 1)
                pool.wait_ge(var_ready, k + 1)
                pool.tensor_tensor(rstd[:, which, :], var[:, which, :], half_pow[:, :], ALU.pow)\
                    .then_inc(rstd_ready, 1)

            def rest_queries(g):
                for hg in range(2):
                    wait_drained(pool, "q", g, hg, 0)
                    wait_drained(pool, "q", g, hg, 1)
                    for par in range(2):
                        src = qm[:, hg, par, :].rearrange("p (b i) -> p b i", i=TOK)[:, :, MAINQ:TOK]
                        dst = q_rest[:, hg, :, :].rearrange("p b (r a i) -> p b r a i", r=4, a=2)[:, :, :, par, :]
                        ins = pool.tensor_tensor(
                            dst, src.unsqueeze(2).to_broadcast([P, IPG, 4, RESTQ]),
                            pair_mask.unsqueeze(1).unsqueeze(3).to_broadcast([P, IPG, 4, RESTQ]), ALU.mult)
                    ins.then_inc(q_rest_ready, 1)

            def normalise(g):
                for hg in range(2):
                    pool.wait_ge(recip_ready, 2 * g + hg + 1)
                    v = acc[:, hg, :, :, 0:TOK].rearrange("p r m j -> p (r m) j")
                    rs = rsums[:, hg, 0:4 * PAIRS].unsqueeze(2).to_broadcast([P, 4 * PAIRS, TOK])
                    pool.tensor_tensor(v, v, rs, ALU.mult).then_inc(normed, 1)

            def with_beta(g):
                pool.wait_ge(mv_ready, ln_at[g, 0] + 1)
                if g > 0:
                    wait_drained(pool, "mm2", g - 1, NT - 1)
                row = row_beta.unsqueeze(1).to_broadcast([P, NT - 1, E])
                pool.tensor_tensor(hb[:, 0:NT - 1, :], h[:, g % 3, 0:NT - 1, :], row, ALU.add)
                pool.tensor_tensor(hb[0:64, NT - 1, :], h[0:64, g % 3, NT - 1, :], row_beta[0:64, :], ALU.add)\
                    .then_inc(hb_ready, 1)

            def with_con(g):
                pool.wait_ge(h1_ready, NT * (g + 1))
                row = row_con.unsqueeze(1).to_broadcast([P, NT - 1, E])
                pool.tensor_tensor(hb[:, 0:NT - 1, :], h[:, g % 3, 0:NT - 1, :], row, ALU.add)
                pool.tensor_tensor(hb[0:64, NT - 1, :], h[0:64, g % 3, NT - 1, :], row_con[0:64, :], ALU.add)\
                    .then_inc(hc_ready, 1)

            inv_std(0, 0)
            rest_queries(0)
            for g in range(G + 1):
                if g > 0:
                    inv_std(g - 1, 2)
                    with_con(g - 1)
                if g + 1 < G:
                    inv_std(g + 1, 0)
                if g < G:
                    normalise(g)
                    with_beta(g)
                if g + 1 < G:
                    rest_queries(g + 1)
                if g < G:
                    inv_std(g, 1)

        @block.vector
        def _(dve):
            def copy(dst, src):
                return dve.tensor_copy(dst, src)

            dve.wait_ge(small_loaded, 16 * len(small))
            k = 0

            def const(ins):
                nonlocal k
                k += 1
                ins.then_inc(consts_ready, 1)
                dve.wait_ge(consts_ready, k)

            const(dve.tensor_scalar(temp[:, 3:4], temp[:, 0:1], -1.0, None, ALU.mult))
            const(dve.tensor_tensor(temp[:, 3:4], temp[:, 0:1], temp[:, 3:4], ALU.max))
            const(dve.tensor_scalar(temp[:, 1:2], temp[:, 3:4], 0.1, None, ALU.add))
            const(dve.reciprocal(temp[:, 2:3], temp[:, 1:2]))
            for f, freq in enumerate(FREQS):
                const(dve.tensor_scalar(inv_freq[:, f:f + 1], temp[:, 2:3], 1.0 / freq, HD ** -0.5,
                                        ALU.mult, ALU.mult))
            for hg in range(2):
                for par in range(2):
                    const(dve.tensor_tensor(q_bias[:, hg, par:par + 1], qk_bias[:, 0, hg:hg + 1],
                                            par_mask[:, par:par + 1], ALU.mult))
            for kk in range(KC):
                b = wait_filled(dve, "wT", kk)
                drain(copy(w_tok[:, kk, :], b[:, 0:E]), "wT", kk)
            b = wait_filled(dve, "heads")
            tv = b[:, 0:20 * NF].rearrange("p (k f) -> p k f", k=10)
            dve.tensor_scalar(turns_alpha[:, :, 0:NF], tv[:, :, 0:NF], 1.0 / TWO_PI, None, ALU.mult)
            drain(copy(turns_alpha[:, :, NF:], tv[:, :, NF:]), "heads")
            for kk in range(2 * NT):
                b = wait_filled(dve, "rows", kk)
                drain(copy(rows[:, kk, :], b[:, 0:E]), "rows", kk)

            def multiply_stages(side):
                for st in range(LOW):
                    src, dst = chain[st % 2], chain[(st + 1) % 2]
                    parts = 2 if st == LOW - 1 else 1
                    blocks = NB // parts
                    w2 = 2 ** st
                    if st == 0 and side == "d":
                        wait_filled(dve, "low", "u", NB - 1)
                    if st > 0:
                        wait_drained(dve, "bits", side, st - 1, 0)
                    for c in range(parts):
                        b = wait_filled(dve, "bits", side, st, c)
                        wv = b[:, 0:blocks * 2 * w2].rearrange("p (a k o) -> p a o k", a=blocks, o=2)
                        dv = dst[:, c * blocks * 2 * w2:(c + 1) * blocks * 2 * w2].rearrange(
                            "p (a o k) -> p a o k", a=blocks, o=2)
                        if st == 0:
                            ins = copy(dv, wv)
                        else:
                            sv = src[:, c * blocks * w2:(c + 1) * blocks * w2].rearrange(
                                "p (a k) -> p a k", a=blocks)
                            ins = dve.tensor_tensor(dv, wv, sv.unsqueeze(2).to_broadcast([P, blocks, 2, w2]),
                                                    ALU.mult)
                        drain(ins, "bits", side, st, c)

            def mix(side, base):
                for step in range(3):
                    st = step if side == 0 else 2 - step
                    src, dst, width = mix_buffers(side, step)
                    dve.wait_ge(mix_first, base + step + 1)
                    for pr in range(4):
                        lo = ((pr >> st) << (st + 1)) | (pr & (2 ** st - 1))
                        blk = [lo, lo + 2 ** st]
                        for o in range(2):
                            j = 1 + o if side == 0 else 2 - o
                            co = high[:, side, st, pr, j:j + 1]
                            ins = dve.scalar_tensor_tensor(out=dst[:, blk[o], 0:width],
                                                           in0=src[:, blk[1 - o], 0:width],
                                                           scalar=co, in1=dst[:, blk[o], 0:width],
                                                           op0=ALU.mult, op1=ALU.add)
                    ins.then_inc(mix_done, 1)

            multiply_stages("u")
            mix(0, 0)
            dve.wait_ge(mix_done, 3)
            dve.tensor_tensor(hid_bias[:, :].unsqueeze(2), mixB[:, :, E:EB], up_bias[:, :].unsqueeze(2), ALU.add)\
                .then_inc(hid_ready, 1)
            multiply_stages("d")
            for c in range(2):
                b = wait_filled(dve, "lowT", c)
                drain(copy(lowT[:, 4 * c:4 * c + 4, :].rearrange("p a o -> p (a o)"), b[:, :]), "lowT", c)
            dve.wait_ge(con_loaded, 16)
            mix(1, 3)
            wait_filled(dve, "low", "d", NB - 1)
            dve.wait_ge(pads_zero, 1)
            dve.wait_ge(pool_ready, 3)

            def statistics(g, which, src):
                base = NT * ln_at[g, which]
                for tt, (t0, tn) in enumerate(TILES):
                    dve.wait_ge(stat_step, base + tt + 1)
                    ins = dve.bn_aggr(mv[0:tn, which, tt, :], stats[0:tn, tt, :])
                ins.then_inc(mv_ready, 1)

            def stat(g, which, tt, src):
                tn = TILES[tt][1]
                if ln_at[g, which] > 0:
                    dve.wait_ge(mv_ready, ln_at[g, which])
                dve.bn_stats(stats[0:tn, tt, :], src[0:tn, tt, :]).then_inc(stat_step, 1)

            def tok_tile(g, tt):
                tn = TILES[tt][1]
                b = wait_filled(dve, "tok", g, tt)
                if g >= 3:
                    dve.wait_ge(out_stored, 16 * NT * (g - 2))
                drain(dve.tensor_tensor(h[0:tn, g % 3, tt, :], b[0:tn, 0:E], pos[0:tn, tt, :], ALU.add), "tok", g, tt)

            def normed_tiles(g, which):
                w = 0 if which == 0 else 2
                dve.wait_ge(rstd_ready, ln_at[g, w] + 1)
                last_v = g + 1 if which == 1 else g - 1
                if 0 <= last_v < G:
                    dve.wait_ge(v_stored, 32 * (last_v + 1))
                if which == 0 and g >= 2:
                    wait_filled(dve, "lnT", g - 2, 1, NT - 1)
                if which == 1 and g > 0:
                    wait_filled(dve, "lnT", g, 0, NT - 1)
                for tt, (t0, tn) in enumerate(TILES):
                    dve.tensor_scalar(xn[0:tn, tt, :], h[0:tn, g % 3, tt, :], mv[0:tn, w, tt, 0:1],
                                      rstd[0:tn, w, tt:tt + 1], ALU.subtract, ALU.mult).then_inc(xn_ready, 1)

            def drain_k(g, hg, hf):
                b = wait_filled(dve, "k", g, hg, hf)
                if g > 0:
                    dve.wait_ge(scores_filled, 2 * g)
                drain(dve.tensor_scalar(kT[:, hg, hf * HALF:(hf + 1) * HALF], b[:, 0:HALF],
                                        qk_bias[:, 1, hg:hg + 1], None, ALU.add), "k", g, hg, hf)

            def drain_v(g, tt):
                tn = TILES[tt][1]
                b = wait_filled(dve, "v", g, tt)
                drain(dve.tensor_tensor(xn[0:tn, tt, :], b[0:tn, 0:E], row_bv[0:tn, :], ALU.add), "v", g, tt)

            def fractions(g, hg, f):
                c = 2 * NF * g + NF * hg + f
                dve.wait_ge(u_ready, c + 1)
                if c >= 2:
                    dve.wait_ge(acc_done, c - 1)
                dve.tensor_scalar(n[:, c % 2, :], u, ROUND, ROUND, ALU.add, ALU.subtract)\
                   .then_inc(rounded, 1)
                dve.wait_ge(rounded, c + 1)
                dve.tensor_tensor(n[:, c % 2, :], u, n[:, c % 2, :], ALU.subtract)\
                   .then_inc(frac_ready, 1)

            def accumulate(g, hg, f):
                c = 2 * NF * g + NF * hg + f
                dve.wait_ge(sin_ready, c + 1)
                if f > 0:
                    dve.wait_ge(acc_done, c)
                elif g > 0:
                    dve.wait_ge(trans_filled, QUADS * g)
                for k in range(5):
                    a0 = k * PAIRS * TOK
                    a1 = a0 + (PAIRS * TOK if k < 4 else REST)
                    dst = acc[:, hg, k, :, 0:TOK] if k < 4 else acc_rest[:, hg, :, :]
                    src = n[:, c % 2, a0:a1].rearrange("p (m j) -> p m j", j=TOK)
                    al = turns_alpha[:, 5 * hg + k, NF + f:NF + f + 1]
                    if f == 0:
                        ins = dve.tensor_scalar(dst, src, al, None, ALU.mult)
                    else:
                        ins = dve.scalar_tensor_tensor(out=dst, in0=src, scalar=al, in1=dst,
                                                       op0=ALU.mult, op1=ALU.add)
                ins.then_inc(acc_done, 1)

            def denominators(g):
                for hg in range(2):
                    k2 = 2 * g + hg
                    dve.wait_ge(weights_ready, k2 + 1)
                    if k2 > 1:
                        dve.wait_ge(normed, k2 - 1)
                    dve.tensor_reduce(sums[:, hg, 0:4 * PAIRS],
                                      acc[:, hg, :, :, 0:TOK].rearrange("p r m j -> p (r m) j"), AX.X, ALU.add)
                    dve.tensor_reduce(sums[:, hg, 4 * PAIRS:], acc_rest[:, hg, :, :], AX.X, ALU.add)\
                       .then_inc(sums_step, 1)
                    dve.wait_ge(sums_step, 2 * k2 + 1)
                    dve.tensor_scalar(sums[:, hg, :], sums[:, hg, :], 1e-10, None, ALU.add).then_inc(sums_step, 1)
                    dve.wait_ge(sums_step, 2 * k2 + 2)
                    dve.reciprocal(rsums[:, hg, :], sums[:, hg, :]).then_inc(recip_ready, 1)
                for hg in range(2):
                    dve.wait_ge(recip_ready, 2 * g + hg + 1)
                    for sl in range(2):
                        p0 = SLOT * sl
                        rs = rsums[p0:p0 + 64, hg, 4 * PAIRS:].unsqueeze(2).to_broadcast([64, QUADS, TOK])
                        ins = dve.tensor_tensor(w_rest[p0:p0 + 64, hg, :, sl, 0:TOK],
                                                acc_rest[p0:p0 + 64, hg, :, :], rs, ALU.mult)
                ins.then_inc(rest_normed, 1)

            def drain_weights(g, q):
                n_ = QUADS * g + q
                dve.wait_ge(trans_filled, n_ + 1)
                if n_ >= 2:
                    dve.wait_ge(pv_filled, n_ - 1)
                for i in range(2):
                    copy(wT[:, n_ % 2, i, 1, :, 0:MAINQ].rearrange("p (r a) q -> p r a q", a=2),
                         att[1][:, :].rearrange("p (r i a q) -> p i r a q", r=4, i=2, a=2)[:, i])
                for hg in range(2):
                    ins = copy(wT[:, n_ % 2, :, hg, :, MAINQ:TOK],
                               att[4][:, hg * 64:(hg + 1) * 64].rearrange("p (i h q) -> p i h q", i=2, h=8))
                ins.then_inc(wT_dve, 1)

            def odd_heads(g, q):
                n_ = QUADS * g + q
                if g > 0 and q == 0:
                    wait_filled(dve, "o", g - 1, NT - 1)
                for sl in range(2):
                    dve.wait_ge(even_ready, 2 * n_ + sl + 1)
                    src = att[2 + sl][:, 0:288].rearrange("p (x a i) -> p x a i", x=4, a=2)[:, :, 1, :]
                    im = 4 * q + 2 * sl
                    dve.scalar_tensor_tensor(
                        out=oT[:, :, im:im + 2, :], in0=src.rearrange("p (m b) i -> p m b i", m=2),
                        scalar=par_mask[:, 1:2], in1=even[:, sl, :, :].rearrange("p (m b) i -> p m b i", m=2),
                        op0=ALU.mult, op1=ALU.add).then_inc(oT_ready, 1)

            def attn_out(g):
                for tt, (t0, tn) in enumerate(TILES):
                    b = wait_filled(dve, "o", g, tt)
                    drain(dve.tensor_tensor(on[0:tn, tt, :], b[0:tn, 0:E], row_bo[0:tn, :], ALU.add), "o", g, tt)
                for tt in range(NT):
                    wait_drained(dve, "o", g, tt)
                    stat(g, 1, tt, on)
                statistics(g, 1, on)

            def attn_residual(g):
                dve.wait_ge(mv_ready, ln_at[g, 1] + 1)
                for tt, (t0, tn) in enumerate(TILES):
                    dve.scalar_tensor_tensor(out=on[0:tn, tt, :], in0=on[0:tn, tt, :],
                                             scalar=mv[0:tn, 1, tt, 0:1], in1=row_gamma[0:tn, :],
                                             op0=ALU.subtract, op1=ALU.mult).then_inc(on_step, 1)
                dve.wait_ge(rstd_ready, ln_at[g, 1] + 1)
                dve.wait_ge(hb_ready, g + 1)
                for tt, (t0, tn) in enumerate(TILES):
                    dve.wait_ge(on_step, NT * g + tt + 1)
                    dve.scalar_tensor_tensor(out=h[0:tn, g % 3, tt, :], in0=on[0:tn, tt, :],
                                             scalar=rstd[0:tn, 1, tt:tt + 1], in1=hb[0:tn, tt, :],
                                             op0=ALU.mult, op1=ALU.add).then_inc(h1_ready, 1)
                for tt in range(NT):
                    dve.wait_ge(h1_ready, NT * g + tt + 1)
                    stat(g, 2, tt, h[:, g % 3])
                statistics(g, 2, h)

            def last_sum(g, tt):
                tn = TILES[tt][1]
                b = wait_filled(dve, "mm2", g, tt)
                dve.wait_ge(hc_ready, g + 1)
                drain(dve.tensor_tensor(h[0:tn, g % 3, tt, :], b[0:tn, 0:E], hb[0:tn, tt, :], ALU.add), "mm2", g, tt)

            def tok_stats(g):
                for tt in range(NT):
                    wait_drained(dve, "tok", g, tt)
                    stat(g, 0, tt, h[:, g % 3])
                statistics(g, 0, h)

            for wp, c in XT_DVE:
                drain_xT(dve, copy, 0, wp, c)
            for tt in range(NT):
                tok_tile(0, tt)
            tok_stats(0)
            normed_tiles(0, 0)
            for hg in range(2):
                for hf in range(2):
                    drain_k(0, hg, hf)
            for tt in range(NT):
                drain_v(0, tt)

            steps = [(hg, f) for hg in range(2) for f in range(NF)]
            for g in range(G + 1):
                if g > 0:
                    normed_tiles(g - 1, 1)
                if g < G:
                    fractions(g, *steps[0])
                    for i in range(len(steps)):
                        if i + 1 < len(steps):
                            fractions(g, *steps[i + 1])
                        accumulate(g, *steps[i])
                        if g + 1 < G:
                            if i in (2, 3):
                                for wp, c in XT_DVE[3 * (i - 2):3 * (i - 1)]:
                                    drain_xT(dve, copy, g + 1, wp, c)
                            if i in (5, 6, 7):
                                for tt in ((0, 1), (2, 3), (4,))[i - 5]:
                                    tok_tile(g + 1, tt)
                            if i == 8:
                                tok_stats(g + 1)
                        if g > 0 and i >= 8:
                            for tt in ((0, 1), (2, 3, 4))[i - 8]:
                                last_sum(g - 1, tt)
                    denominators(g)
                else:
                    for tt in range(NT):
                        last_sum(g - 1, tt)
                if g + 1 < G:
                    normed_tiles(g + 1, 0)
                    for hg in range(2):
                        for hf in range(2):
                            drain_k(g + 1, hg, hf)
                    for tt in range(NT):
                        drain_v(g + 1, tt)
                if g < G:
                    drain_weights(g, 0)
                    for q in range(QUADS):
                        if q + 1 < QUADS:
                            drain_weights(g, q + 1)
                        odd_heads(g, q)
                    attn_out(g)
                    attn_residual(g)


_INS = ["x", "L0_tok_W_proj", "L0_tok_b_proj", "L0_tok_pos_emb", "L0_attn_Wq", "L0_attn_bq", "L0_attn_Wk",
        "L0_attn_bk", "L0_attn_Wv", "L0_attn_bv", "L0_attn_Wo", "L0_attn_bo", "L0_attn_alpha", "L0_attn_phi",
        "L0_attn_temperature", "L0_attn_gamma", "L0_attn_beta", "L0_ffn_W_exp", "L0_ffn_b_exp",
        "L0_ffn_up_weights", "L0_ffn_up_bias", "L0_ffn_down_weights", "L0_ffn_W_con", "L0_ffn_b_con",
        "L0_ffn_down_bias"]


def kernel(**inputs):
    import concourse.bacc as _bacc
    from concourse.bass_utils import run_bass_kernel_spmd as _run

    nc = _bacc.Bacc("TRN2", target_bir_lowering=False, num_devices=1)
    arrays, tensors = {}, {}

    def give(name, a):
        arrays[f"in_{name}"] = a
        tensors[name] = nc.dram_tensor(f"in_{name}", a.shape, mybir.dt.from_np(a.dtype), kind="ExternalInput").ap()

    for name in _INS:
        give(name, np.ascontiguousarray(inputs[name]))
    for name, a in zip(("misc", "heads", "bits", "rows"), shape_constants()):
        give(name, a)
    tensors["out"] = nc.dram_tensor("out", (IMAGES, TOK, E), F32, kind="ExternalOutput").ap()
    build(nc, tensors)
    r = _run(nc, [arrays], core_ids=[0])
    return r.results[0]["out"]
```

```python
from contextlib import ExitStack

import numpy as np

import concourse.bass as bass
from concourse import mybir

F32 = mybir.dt.float32
ALU = mybir.AluOpType
ACT = mybir.ActivationFunctionType
AX = mybir.AxisListType

P = 128
IMAGES, SIDE, CH, PATCH = 64, 96, 3, 16
GRID = SIDE // PATCH
TOK = GRID * GRID
PD = PATCH * PATCH * CH
ROW = PATCH * CH
E = 256
HEADS, HD = 16, 16
FREQS = [31.0, 37.0, 41.0, 43.0, 47.0]
NF = len(FREQS)
HID = 1024
NB = HID // P
LOW = 7
TWO_PI = 2.0 * float(np.pi)
SIN_SCALE = 6.283185
ROUND = 12582912.0

G = 4
IPG = IMAGES // G
TPG = IPG * TOK
TILES = [(t * P, min(P, TPG - t * P)) for t in range((TPG + P - 1) // P)]
NT = len(TILES)
HALF = TPG // 2
BH = IPG * GRID
KC = PD // P
MAINQ = 32
RESTQ = TOK - MAINQ
PAIRS = IPG // 2
QUADS = IPG // 4
MAIN = 4 * PAIRS * TOK
REST = QUADS * TOK
COLS = MAIN + REST
SLOT = 64
BANKS = 8
UNITS = 2 * G
UTILES = 3
CHAIN = UNITS * NF
N_CONSTS = 4 + NF + 4
ROWS_IN = TOK + 7


def turn_order():
    def patches(g):
        return [("xT", g, wp, c) for wp in range(GRID) for c in range(2)]

    def tokens(g):
        return [("tok", g, t) for t in range(NT)]

    def lnT(g, which):
        return [("lnT", g, which, t) for t in range(NT)]

    def qk(g, hg):
        return [(w, g, hg, hf) for w in "qk" for hf in range(2)]

    def scores(k):
        return [("s", k, r) for r in range(4)]

    def weights_turned(k):
        return [("T", k, q) for q in range(QUADS)] + [("rT", k)]

    def values(k):
        return [("V", k, qp, sl) for qp in range(QUADS // 2) for sl in range(2)]

    def bits(side):
        return [("bits", side, s, c) for s in range(LOW) for c in range(2 if s == LOW - 1 else 1)]

    def mm2(g, lo, hi):
        return [("mm2", g, t) for t in range(lo, hi)]

    names = [("wT", k) for k in range(KC)] + patches(0) + [("rows", k) for k in range(2 * NT)] + [("heads",)]
    names += tokens(0) + [("attnT", w, k) for w in range(4) for k in range(2)] + lnT(0, 0)
    names += qk(0, 0) + scores(0) + qk(0, 1) + [("v", 0, t) for t in range(NT)]
    for g in range(G + 2):
        if g < G:
            names += scores(2 * g + 1)
        if g + 1 < G:
            names += patches(g + 1)
        if g == 0:
            names += tokens(1) + [("expT", a) for a in range(NB)] + bits("u")
        if g >= 2:
            names += mm2(g - 2, 0, 2)
        if 1 <= g <= G:
            names += weights_turned(2 * g - 1)
        if g >= 2:
            names += mm2(g - 2, 2, NT)
        if g == 1:
            names += values(1) + [("low", "d", a) for a in range(NB)] + tokens(2)
        else:
            if 1 < g and g + 1 < G:
                names += tokens(g + 1)
            if 1 <= g <= G:
                names += values(2 * g - 1)
        if 1 <= g <= G:
            names += [("o", g - 1, t) for t in range(NT)]
        if g + 1 < G:
            names += lnT(g + 1, 0) + qk(g + 1, 0) + qk(g + 1, 1)
        if g == 0:
            names += [("low", "u", a) for a in range(NB)]
        if g < G:
            names += weights_turned(2 * g)
        if g + 1 < G:
            names += [("v", g + 1, t) for t in range(NT)]
        if g < G:
            names += values(2 * g)
        if g + 1 < G:
            names += scores(2 * g + 2)
        if g == 0:
            names += bits("d") + [("upT", k, c) for k in range(2) for c in range(2)]
            names += [("lowT", c) for c in range(2)]
        if 1 <= g <= G:
            names += lnT(g - 1, 1) + [("mm1", g - 1, m, hf) for m in range(NB) for hf in range(2)]
    return names


def shape_constants():
    ident = np.eye(P, dtype=np.float32)
    p = np.arange(P)
    i, hd8, q4 = (p % 64) // 32, (p % 32) // RESTQ, p % RESTQ
    fold = (((hd8 // 4) * 2 + i) * 16 + (hd8 % 4) * RESTQ + q4)[:, None] == np.arange(64)[None, :]
    par = np.stack([(p // HD) % 2 == 0, (p // HD) % 2 == 1], 1)
    pair = p[:, None] // 32 == np.arange(4)[None, :]
    misc = np.concatenate([ident, fold, par, pair], 1).astype(np.float32)
    heads = np.zeros((HEADS, 2 * UTILES, P), np.float32)
    for hg in range(2):
        for r in range(2):
            heads[8 * hg + 4 * r + p // 32, hg * UTILES + r, p] = 1
        heads[8 * hg + (p % 32) // RESTQ, hg * UTILES + 2, p] = 1
    bits = np.zeros((64, LOW, 2, P), np.float32)
    for s in range(LOW):
        bits[p >> (s + 1), s, (p >> s) & 1, p] = 1
    rows = np.zeros((ROWS_IN, 2 * NT, P), np.float32)
    for tt, (t0, tn) in enumerate(TILES):
        q = np.arange(tn)
        rows[(t0 + q) % TOK, tt, q] = 1
        rows[TOK, tt, :] = 1
    for k in range(5):
        rows[TOK + 1 + k, NT + k, :] = 1
    rows[TOK + 6, 2 * NT - 1, :] = 1
    return misc, heads.reshape(HEADS, 2 * UTILES * P), bits.reshape(64, LOW * 2 * P), rows.reshape(ROWS_IN, 2 * NT * P)


def build(nc, t):
    order = turn_order()
    turn = {name: i for i, name in enumerate(order)}
    with ExitStack() as ctx:
        def sb(name, *shape):
            return ctx.enter_context(nc.sbuf_tensor(name, list(shape), F32))

        def sem(name):
            return ctx.enter_context(nc.semaphore(name))

        banks = [ctx.enter_context(nc.psum_tensor(f"bank{k}", [P, 512], F32)) for k in range(BANKS)]

        misc = sb("misc", P, P + 64 + 2 + 4)
        ident, fold = misc[:, 0:P], misc[:, P:P + 64]
        par_mask, pair_mask = misc[:, P + 64:P + 66], misc[:, P + 66:P + 70]
        phi_alpha = sb("phi_alpha", HEADS, 2 * NF)
        turns_alpha = sb("turns_alpha", P, 2 * UTILES, 2 * NF)
        temp = sb("temp", P, 4)
        inv_freq = sb("inv_freq", P, NF)
        w_tok = sb("w_tok", P, KC, E)
        w_attn = sb("w_attn", P, 4, 2, E)
        w_up = sb("w_up", P, 2, HID)
        w_down = sb("w_down", P, NB, E)
        hid_bias = sb("hid_bias", P, NB)
        up_bias = sb("up_bias", P, NB)
        rows = sb("rows", P, 2 * NT, E)
        pos = rows[:, 0:NT, :]
        row_bv, row_bo, row_gamma, row_beta, row_con = (rows[:, NT + n, :] for n in range(5))
        qk_bias = sb("qk_bias", P, 2, 2)
        q_bias = sb("q_bias", P, 2, 2)
        half_pow = sb("half_pow", P, NT)
        high = sb("high", P, 2, 3, 4, 4)

        x_in = sb("x_in", BH, GRID, PD)
        patT = sb("patT", P, KC, TPG)
        patT_f = patT[:, :, :].rearrange("p k t -> p (k t)")
        xn0 = patT_f[:, 2 * TPG:2 * TPG + NT * E].rearrange("p (t e) -> p t e", e=E)
        on = sb("on", P, NT, E)
        xnT1 = sb("xnT1", P, 2, TPG)
        xn, xnT = (xn0, on), (patT[:, 0:2, :], xnT1[:, :, :])
        wT = sb("wT", P, QUADS, 2, 2, 4, TOK)
        oT = sb("oT", P, 2, IPG, TOK)
        h = sb("h", P, 3, NT, E)
        stats = sb("stats", P, NT, 6)
        mv = sb("mv", P, 3, NT, 2)
        var = sb("var", P, 3, NT)
        rstd = sb("rstd", P, 3, NT)
        qm = sb("qm", P, 2, 2, TPG)
        kT = sb("kT", P, 2, TPG)
        q_rest = sb("q_rest", P, 2, IPG, 32)
        v_sl = sb("v_sl", P, QUADS, 2, E)
        s = sb("s", P, 2, COLS)
        u = sb("u", P, 2, COLS)
        n = sb("n", P, 2, COLS)
        acc = sb("acc", P, 2, 4, PAIRS, SLOT)
        acc_rest = sb("acc_rest", P, 2, QUADS, TOK)
        w_rest = sb("w_rest", P, QUADS, 2, SLOT)
        sums = sb("sums", P, 2, 4 * PAIRS + QUADS)
        rsums = sb("rsums", P, 2, 4 * PAIRS + QUADS)
        even = sb("even", P, 2, 4, TOK)
        gT = sb("gT", P, NB, TPG)

        gT_f = gT[:, :, :].rearrange("p a b -> p (a b)")
        nat_tok = gT_f[:, 0:2 * PD].rearrange("p (m d) -> p m d", m=2)
        nat_attn = gT_f[:, 2 * PD:2 * PD + 8 * E].rearrange("p (w m e) -> p w m e", w=4, m=2)
        nat_exp = w_up
        EB = E + 1
        mixA, mixB = (gT_f[:, k * NB * EB:(k + 1) * NB * EB].rearrange("p (a e) -> p a e", a=NB) for k in range(2))
        expT = mixB
        h_f = h[:, 2, :, :].rearrange("p b c -> p (b c)")
        on_f = on[:, :, :].rearrange("p b c -> p (b c)")
        row_src = xnT1[0:ROWS_IN, 0, 0:E]
        row_sel = h_f[0:ROWS_IN, 0:2 * NT * P]
        head_sel = on_f[0:HEADS, 0:2 * UTILES * P]
        chain = [h_f[:, 0:HID], on_f[:, 0:HID]]
        lowT = chain[0].rearrange("p (a o) -> p a o", a=NB)
        x_f = x_in[:, :, :].rearrange("p a b -> p (a b)")
        stage_row = [0] * (LOW - 1) + [64]
        stage_at = [32 * (2 ** st - 1) for st in range(LOW - 1)] + [0]
        stage_w, bit_sel = [], []
        for st in range(LOW):
            rows_ = slice(stage_row[st], stage_row[st] + 2 ** (LOW - 1 - st))
            stage_w.append(x_f[rows_, stage_at[st]:stage_at[st] + 32 * 2 ** st].rearrange("p (a k) -> p a k", a=NB))
            at = 32 * 2 ** (LOW - 1) + 2 * P * st
            bit_sel.append(x_f[rows_, at:at + 2 * P].rearrange("p (i q) -> p i q", i=2))

        v_dram = nc.dram_tensor("v_scratch", (G, TPG, E), F32)

        filled = [sem(f"bank_filled{k}") for k in range(BANKS)]
        drained = [sem(f"bank_drained{k}") for k in range(BANKS)]
        misc_loaded = sem("misc_loaded")
        rows_loaded = sem("rows_loaded")
        small_loaded = sem("small_loaded")
        late_loaded = sem("late_loaded")
        tok_loaded = sem("tok_loaded")
        attn_loaded = sem("attn_loaded")
        exp_loaded = sem("exp_loaded")
        con_loaded = sem("con_loaded")
        bit_sel_loaded = sem("bit_sel_loaded")
        stages_loaded = sem("stages_loaded")
        x_loaded = [sem(f"x_loaded{wp}") for wp in range(GRID)]
        v_stored = sem("v_stored")
        v_loaded = sem("v_loaded")
        out_stored = sem("out_stored")
        consts_ready = sem("consts_ready")
        pool_ready = sem("pool_ready")
        mix_first = sem("mix_first")
        mix_done = sem("mix_done")
        hid_ready = sem("hid_ready")
        u_ready = sem("u_ready")
        rounded = sem("rounded")
        frac_ready = sem("frac_ready")
        sin_ready = sem("sin_ready")
        acc_done = sem("acc_done")
        weights_ready = sem("weights_ready")
        sums_step = sem("sums_step")
        recip_ready = sem("recip_ready")
        normed = sem("normed")
        rest_normed = sem("rest_normed")
        even_ready = sem("even_ready")
        stat_step = sem("stat_step")
        mv_ready = sem("mv_ready")
        var_ready = sem("var_ready")
        rstd_ready = sem("rstd_ready")
        xn_ready = [sem(f"xn{w}_ready") for w in range(2)]
        beta_added = sem("beta_added")
        on_step = sem("on_step")
        h1_ready = sem("h1_ready")
        con_added = sem("con_added")
        q_rest_ready = sem("q_rest_ready")
        gelu_done = sem("gelu_done")

        def open_turn(pe, *name):
            i = turn[name]
            if i >= BANKS:
                pe.wait_ge(drained[i % BANKS], i // BANKS)
            return banks[i % BANKS]

        def close_turn(ins, *name):
            ins.then_inc(filled[turn[name] % BANKS], 1)

        def wait_filled(eng, *name):
            i = turn[name]
            eng.wait_ge(filled[i % BANKS], i // BANKS + 1)
            return banks[i % BANKS]

        def drain(ins, *name):
            ins.then_inc(drained[turn[name] % BANKS], 1)

        def wait_drained(eng, *name):
            i = turn[name]
            eng.wait_ge(drained[i % BANKS], i // BANKS + 1)

        ln_order = [(0, 0)]
        for g in range(G + 1):
            ln_order += [(g + 1, 0)] * (g + 1 < G) + [(g - 1, 1), (g - 1, 2)] * (g > 0)
        ln_at = {name: k for k, name in enumerate(ln_order)}

        misc_in, head_in, bit_in = t["misc"], t["heads"], t["bits"]
        block = ctx.enter_context(nc.Block())

        row_loads = [(row_sel, t["rows"]), (row_src[0:TOK], t["L0_tok_pos_emb"])]
        for k, name in enumerate(("tok_b_proj", "attn_bv", "attn_bo", "attn_gamma", "attn_beta", "ffn_b_con",
                                  "ffn_down_bias")):
            row_loads.append((row_src[TOK + k:TOK + k + 1], t[f"L0_{name}"].unsqueeze(0)))
        small = [
            (head_sel, head_in),
            (phi_alpha[:, 0:NF], t["L0_attn_phi"]), (phi_alpha[:, NF:2 * NF], t["L0_attn_alpha"]),
            (temp[:, 0:1], t["L0_attn_temperature"].partition_broadcast(P)),
            (qk_bias[:, 0, :], t["L0_attn_bq"].rearrange("(m p) -> p m", p=P)),
            (qk_bias[:, 1, :], t["L0_attn_bk"].rearrange("(m p) -> p m", p=P)),
        ]
        late = [(up_bias[:, :], t["L0_ffn_up_bias"].rearrange("(a p) -> p a", p=P))]
        for side, name in ((0, "up"), (1, "down")):
            w = t[f"L0_ffn_{name}_weights"]
            for st in range(3):
                late.append((high[:, side, st, :, :],
                             w[LOW + st].rearrange("(g p) o i -> p g (o i)", p=P)))

        def mix_buffers(side, step):
            if side == 1 and step == 0:
                return w_down, mixB, E
            pair = (mixA, mixB) if step % 2 == 0 else (mixB, mixA)
            return *pair, EB if side == 0 else E

        def upper_stage(side, step):
            st = step if side == 0 else 2 - step
            los = [((pr >> st) << (st + 1)) | (pr & (2 ** st - 1)) for pr in range(4)]
            return st, [(pr, lo, lo + 2 ** st) for pr, lo in enumerate(los)]

        @block.sync
        def _(sp):
            def load_x(g):
                src = t["x"][g * IPG:(g + 1) * IPG].rearrange(
                    "b (hp i) (wp j) c -> (b hp) wp i (j c)", hp=GRID, wp=GRID)
                for wp in range(GRID):
                    if g == 2:
                        wait_filled(sp, "bits", "d", LOW - 1, 1)
                    elif g > 0:
                        wait_filled(sp, "xT", g - 1, wp, 1)
                    sp.dma_start(x_in[:, wp, :].rearrange("p (i k) -> p i k", i=PATCH),
                                 src[:, wp]).then_inc(x_loaded[wp], 16)

            def load_stages(name):
                w = t[f"L0_ffn_{name}_weights"]
                for st in range(LOW):
                    sp.dma_start(stage_w[st], w[st].rearrange("(a i k) o j -> i a (k o j)", a=NB, k=2 ** st))\
                      .then_inc(stages_loaded, 16)

            def store_v(g):
                wait_drained(sp, "v", g, NT - 1)
                full = TPG // P
                sp.dma_start(v_dram.ap()[g, 0:full * P, :].rearrange("(t p) e -> p t e", p=P),
                             xn0[:, 0:full, :]).then_inc(v_stored, 16)
                sp.dma_start(v_dram.ap()[g, full * P:TPG, :], xn0[0:TPG - full * P, full, :]).then_inc(v_stored, 16)

            def load_v(g):
                sp.wait_ge(v_stored, 32 * (g + 1))
                if g > 0:
                    for sl in range(2):
                        wait_filled(sp, "V", 2 * g - 1, QUADS // 2 - 1, sl)
                view = v_dram.ap()[g].rearrange("(q s i j) e -> s i j q e", q=QUADS, s=2, i=2)
                for sl in range(2):
                    for i in range(2):
                        sp.dma_start(v_sl[SLOT * sl:SLOT * sl + TOK, :, i, :], view[sl, i]).then_inc(v_loaded, 16)

            def store_out(g):
                for tt, (t0, tn) in enumerate(TILES):
                    wait_drained(sp, "mm2", g, tt)
                    sp.dma_start(t["out"].rearrange("b n e -> (b n) e")[g * TPG + t0:g * TPG + t0 + tn, :],
                                 h[0:tn, g % 3, tt, :]).then_inc(out_stored, 16)

            sp.dma_start(misc[:, :], misc_in).then_inc(misc_loaded, 16)
            sp.dma_start(nat_tok, t["L0_tok_W_proj"].rearrange("(m p) d -> p m d", p=P)).then_inc(tok_loaded, 16)
            load_x(0)
            for w, name in enumerate(("Wq", "Wk", "Wv", "Wo")):
                sp.dma_start(nat_attn[:, w], t[f"L0_attn_{name}"].rearrange("(m p) e -> p m e", p=P))\
                  .then_inc(attn_loaded, 16)
            load_x(1)
            sp.dma_start(nat_exp[:, :, :], t["L0_ffn_W_exp"].rearrange("(m p) d -> p m d", p=P))\
              .then_inc(exp_loaded, 16)
            sp.dma_start(w_down[:, :, :], t["L0_ffn_W_con"].rearrange("(a p) e -> p a e", p=P)).then_inc(con_loaded, 16)
            wait_filled(sp, "attnT", 3, 1)
            sp.dma_start(expT[:, :, E:EB], t["L0_ffn_b_exp"].rearrange("(a p u) -> p a u", p=P, u=1),
                         allow_slow_non_contiguous=True).then_inc(exp_loaded, 16)
            store_v(0)
            load_v(0)
            for wp in range(GRID):
                wait_filled(sp, "xT", 1, wp, 1)
            low_bits = 2 * P * (LOW - 1)
            sp.dma_start(x_f[0:64, 32 * 2 ** (LOW - 1):32 * 2 ** (LOW - 1) + low_bits], bit_in[:, 0:low_bits])\
              .then_inc(bit_sel_loaded, 16)
            sp.dma_start(bit_sel[LOW - 1].rearrange("p i q -> p (i q)"), bit_in[0:1, low_bits:])\
              .then_inc(bit_sel_loaded, 16)
            load_stages("up")
            for g in range(G + 2):
                if 3 <= g + 2 < G:
                    load_x(g + 2)
                if g >= 2:
                    store_out(g - 2)
                if 1 <= g < G:
                    load_v(g)
                if g + 1 < G:
                    store_v(g + 1)
                if g == 0:
                    wait_filled(sp, "bits", "u", LOW - 1, 1)
                    load_stages("down")
                    load_x(2)
            sp.wait_ge(out_stored, 16 * NT * G)

        @block.tensor
        def _(pe):
            def flip(out, in_, rows_):
                return pe.transpose(out, in_, ident[0:rows_, 0:rows_])

            def patches(g):
                for wp in range(GRID):
                    pe.wait_ge(x_loaded[wp], 16 * (g + 1))
                    for c in range(2):
                        b = open_turn(pe, "xT", g, wp, c)
                        for k in range(3):
                            d0 = (3 * c + k) * P
                            ins = flip(b[:, k * BH:(k + 1) * BH], x_in[:, wp, d0:d0 + P], BH)
                        close_turn(ins, "xT", g, wp, c)

            def tokens(g):
                for wp in range(GRID):
                    for c in range(2):
                        wait_drained(pe, "xT", g, wp, c)
                for tt, (t0, tn) in enumerate(TILES):
                    b = open_turn(pe, "tok", g, tt)
                    for k in range(KC):
                        ins = pe.matmul(b[0:tn, 0:E], patT[:, k, t0:t0 + tn], w_tok[:, k, :],
                                        start=(k == 0), stop=(k == KC - 1))
                    close_turn(ins, "tok", g, tt)

            def ln_turns(g, which):
                for tt, (t0, tn) in enumerate(TILES):
                    pe.wait_ge(xn_ready[which], NT * g + tt + 1)
                    b = open_turn(pe, "lnT", g, which, tt)
                    for k in range(2):
                        ins = flip(b[:, k * P:k * P + tn], xn[which][0:tn, tt, k * P:(k + 1) * P], tn)
                    close_turn(ins, "lnT", g, which, tt)
                for tt in range(NT):
                    wait_drained(pe, "lnT", g, which, tt)

            def qk(g, hg):
                for wi, w in enumerate("qk"):
                    for hf in range(2):
                        b = open_turn(pe, w, g, hg, hf)
                        for k in range(2):
                            ins = pe.matmul(b[:, 0:HALF], w_attn[:, wi, k, hg * P:(hg + 1) * P],
                                            xnT[0][:, k, hf * HALF:(hf + 1) * HALF],
                                            start=(k == 0), stop=(k == 1))
                        close_turn(ins, w, g, hg, hf)

            def v_tiles(g):
                for tt, (t0, tn) in enumerate(TILES):
                    b = open_turn(pe, "v", g, tt)
                    for k in range(2):
                        ins = pe.matmul(b[0:tn, 0:E], xnT[0][:, k, t0:t0 + tn], w_attn[:, 2, k, :],
                                        start=(k == 0), stop=(k == 1))
                    close_turn(ins, "v", g, tt)

            def scores(k):
                g, hg = divmod(k, 2)
                for hf in range(2):
                    wait_drained(pe, "q", g, hg, hf)
                    wait_drained(pe, "k", g, hg, hf)
                pe.wait_ge(q_rest_ready, k + 1)
                tiles = [open_turn(pe, "s", k, r) for r in range(4)]

                def main(swap):
                    last = {}
                    for m in range(PAIRS):
                        for r in range(2):
                            for a in range(2):
                                i = a ^ swap
                                t0 = (2 * m + i) * TOK
                                for par in range(2):
                                    c = 32 * (2 * a + par)
                                    rows_ = slice(32 * (2 * r + a), 32 * (2 * r + a) + 32)
                                    ins = pe.matmul(tiles[2 * r + i][c:c + 32, m * TOK:(m + 1) * TOK],
                                                    qm[rows_, hg, par, t0:t0 + MAINQ],
                                                    kT[rows_, hg, t0:t0 + TOK],
                                                    start=True, stop=True, skip_group_check=True)
                                    last[2 * r + i] = ins
                    return last

                main(0)
                for im in range(IPG):
                    c = 32 * (im % 4)
                    c0 = (PAIRS + im // 4) * TOK
                    pe.matmul(tiles[3][c:c + 32, c0:c0 + TOK],
                              q_rest[:, hg, im, :], kT[:, hg, im * TOK:(im + 1) * TOK],
                              start=True, stop=True, skip_group_check=True)
                for r, ins in main(1).items():
                    close_turn(ins, "s", k, r)

            def turn_weights(k):
                hg = k % 2
                pe.wait_ge(normed, k + 1)
                pe.wait_ge(rest_normed, k + 1)
                for q in range(QUADS):
                    b = open_turn(pe, "T", k, q)
                    for r in range(4):
                        ins = flip(b[:, r * P:(r + 1) * P],
                                   acc[:, hg, r, 2 * q:2 * q + 2, :].rearrange("p a b -> p (a b)"), P)
                    close_turn(ins, "T", k, q)
                b = open_turn(pe, "rT", k)
                for q in range(QUADS):
                    ins = pe.matmul(b[:, q * 64:(q + 1) * 64], w_rest[:, q, :, :].rearrange("p a b -> p (a b)"),
                                    fold, start=True, stop=True, skip_group_check=True)
                close_turn(ins, "rT", k)

            def values(k):
                g, hg = divmod(k, 2)
                pe.wait_ge(v_loaded, 64 * (g + 1))
                for q in range(QUADS):
                    wait_drained(pe, "T", k, q)
                wait_drained(pe, "rT", k)
                for qp in range(QUADS // 2):
                    b = [open_turn(pe, "V", k, qp, sl) for sl in range(2)]
                    last = [None, None]
                    for q2 in range(2):
                        q = 2 * qp + q2
                        for i in range(2):
                            for r in range(4):
                                for sl in range(2):
                                    p0 = SLOT * sl
                                    last[sl] = pe.matmul(
                                        b[sl][32 * r:32 * r + 32, (q2 * 2 + i) * 72:(q2 * 2 + i + 1) * 72],
                                        v_sl[p0:p0 + TOK, q, i, hg * P + 32 * r:hg * P + 32 * r + 32],
                                        wT[p0:p0 + TOK, q, r // 2, i, 2 * (r % 2):2 * (r % 2) + 2, :].rearrange(
                                            "p a b -> p (a b)"),
                                        start=True, stop=True, skip_group_check=True)
                    for sl in range(2):
                        close_turn(last[sl], "V", k, qp, sl)

            def out_proj(g):
                for k in (2 * g, 2 * g + 1):
                    for qp in range(2):
                        for sl in range(2):
                            wait_drained(pe, "V", k, qp, sl)
                flat = oT[:, :, :, :].rearrange("p m b i -> p m (b i)")
                for tt, (t0, tn) in enumerate(TILES):
                    b = open_turn(pe, "o", g, tt)
                    for k in range(2):
                        ins = pe.matmul(b[0:tn, 0:E], flat[:, k, t0:t0 + tn], w_attn[:, 3, k, :],
                                        start=(k == 0), stop=(k == 1))
                    close_turn(ins, "o", g, tt)

            def mm1(g):
                for m in range(NB):
                    for hf in range(2):
                        b = open_turn(pe, "mm1", g, m, hf)
                        for k in range(2):
                            ins = pe.matmul(b[:, 0:HALF], w_up[:, k, m * P:(m + 1) * P],
                                            xnT[1][:, k, hf * HALF:(hf + 1) * HALF],
                                            start=(k == 0), stop=(k == 1))
                        close_turn(ins, "mm1", g, m, hf)

            def mm2(g, lo, hi):
                pe.wait_ge(gelu_done, g + 1)
                for tt in range(lo, hi):
                    t0, tn = TILES[tt]
                    b = open_turn(pe, "mm2", g, tt)
                    for k in range(NB):
                        ins = pe.matmul(b[0:tn, 0:E], gT[:, k, t0:t0 + tn], w_down[:, k, :],
                                        start=(k == 0), stop=(k == NB - 1))
                    close_turn(ins, "mm2", g, tt)

            def stage_bits(side):
                for st in range(LOW):
                    parts = 2 if st == LOW - 1 else 1
                    for c in range(parts):
                        blocks = NB // parts
                        b = open_turn(pe, "bits", side, st, c)
                        width = blocks * 2 ** (st + 1)
                        for i in range(2):
                            src = stage_w[st][:, c * blocks:(c + 1) * blocks, :]
                            src = src.rearrange("p a (k i) -> p a k i", i=2)[:, :, :, i]
                            ins = pe.matmul(b[:, 0:width].rearrange("p (a k) -> p a k", a=blocks),
                                            bit_sel[st][:, i, :], src,
                                            start=(i == 0), stop=(i == 1))
                        close_turn(ins, "bits", side, st, c)

            def chain_out():
                return chain[LOW % 2].rearrange("p (a o) -> p a o", a=NB)

            pe.wait_ge(misc_loaded, 16)
            pe.wait_ge(tok_loaded, 16)
            for k in range(KC):
                b = open_turn(pe, "wT", k)
                for m in range(2):
                    ins = flip(b[:, m * P:(m + 1) * P], nat_tok[:, m, k * P:(k + 1) * P], P)
                close_turn(ins, "wT", k)
            patches(0)
            pe.wait_ge(rows_loaded, 16 * len(row_loads))
            for k in range(2 * NT):
                b = open_turn(pe, "rows", k)
                close_turn(pe.matmul(b[:, 0:E], row_sel[:, k * P:(k + 1) * P], row_src, start=True, stop=True),
                           "rows", k)
            pe.wait_ge(small_loaded, 16 * len(small))
            b = open_turn(pe, "heads")
            for k in range(2 * UTILES):
                ins = pe.matmul(b[:, k * 2 * NF:(k + 1) * 2 * NF], head_sel[:, k * P:(k + 1) * P],
                                phi_alpha[:, :], start=True, stop=True)
            close_turn(ins, "heads")
            for k in range(KC):
                wait_drained(pe, "wT", k)
            tokens(0)
            pe.wait_ge(attn_loaded, 16 * 4)
            for w in range(4):
                for k in range(2):
                    b = open_turn(pe, "attnT", w, k)
                    for m in range(2):
                        ins = flip(b[:, m * P:(m + 1) * P], nat_attn[:, w, m, k * P:(k + 1) * P], P)
                    close_turn(ins, "attnT", w, k)
            for w in range(4):
                for k in range(2):
                    wait_drained(pe, "attnT", w, k)
            ln_turns(0, 0)
            qk(0, 0)
            scores(0)
            qk(0, 1)
            v_tiles(0)
            for g in range(G + 2):
                if g < G:
                    scores(2 * g + 1)
                if g + 1 < G:
                    patches(g + 1)
                if g == 0:
                    tokens(1)
                    pe.wait_ge(exp_loaded, 32)
                    for a in range(NB):
                        b = open_turn(pe, "expT", a)
                        for m in range(2):
                            ins = flip(b[:, m * P:(m + 1) * P], nat_exp[:, m, a * P:(a + 1) * P], P)
                        close_turn(ins, "expT", a)
                    pe.wait_ge(bit_sel_loaded, 32)
                    pe.wait_ge(stages_loaded, 16 * LOW)
                    stage_bits("u")
                if g >= 2:
                    mm2(g - 2, 0, 2)
                if 1 <= g <= G:
                    turn_weights(2 * g - 1)
                if g >= 2:
                    mm2(g - 2, 2, NT)
                if g == 1:
                    values(1)
                    for c in range(2):
                        wait_drained(pe, "lowT", c)
                    pe.wait_ge(mix_done, 6)
                    for a in range(NB):
                        b = open_turn(pe, "low", "d", a)
                        ins = pe.matmul(b[:, 0:E], lowT[:, a, :], mixB[:, a, 0:E], start=True, stop=True)
                        close_turn(ins, "low", "d", a)
                    tokens(2)
                else:
                    if 1 < g and g + 1 < G:
                        tokens(g + 1)
                    if 1 <= g <= G:
                        values(2 * g - 1)
                if 1 <= g <= G:
                    out_proj(g - 1)
                if g + 1 < G:
                    ln_turns(g + 1, 0)
                    qk(g + 1, 0)
                    qk(g + 1, 1)
                if g == 0:
                    for c in range(2):
                        wait_drained(pe, "bits", "u", LOW - 1, c)
                    for a in range(NB):
                        wait_drained(pe, "expT", a)
                    for a in range(NB):
                        b = open_turn(pe, "low", "u", a)
                        ins = pe.matmul(b[:, 0:EB], chain_out()[:, a, :], expT[:, a, :], start=True, stop=True)
                        close_turn(ins, "low", "u", a)
                if g < G:
                    turn_weights(2 * g)
                if g + 1 < G:
                    v_tiles(g + 1)
                if g < G:
                    values(2 * g)
                if g + 1 < G:
                    scores(2 * g + 2)
                if g == 0:
                    pe.wait_ge(stages_loaded, 16 * 2 * LOW)
                    stage_bits("d")
                    pe.wait_ge(mix_done, 3)
                    for k in range(2):
                        for c in range(2):
                            b = open_turn(pe, "upT", k, c)
                            for a in range(4):
                                ins = flip(b[:, a * P:(a + 1) * P], mixB[:, 4 * c + a, k * P:(k + 1) * P], P)
                            close_turn(ins, "upT", k, c)
                    for c in range(2):
                        wait_drained(pe, "bits", "d", LOW - 1, c)
                    for c in range(2):
                        b = open_turn(pe, "lowT", c)
                        for a in range(4):
                            ins = flip(b[:, a * P:(a + 1) * P], chain_out()[:, 4 * c + a, :], P)
                        close_turn(ins, "lowT", c)
                if 1 <= g <= G:
                    if g == 1:
                        for k in range(2):
                            for c in range(2):
                                wait_drained(pe, "upT", k, c)
                        for a in range(NB):
                            wait_drained(pe, "low", "d", a)
                    ln_turns(g - 1, 1)
                    mm1(g - 1)

        def drain_xT(eng, copy, g, wp, c):
            b = wait_filled(eng, "xT", g, wp, c)
            if g > 0:
                wait_filled(eng, "v", g - 1, NT - 1)
                eng.wait_ge(v_stored, 32 * g)
            dst = patT[:, 3 * c:3 * c + 3, :].rearrange("p k (r w) -> p k r w", w=GRID)[:, :, :, wp]
            drain(copy(dst, b[:, 0:3 * BH].rearrange("p (k r) -> p k r", k=3)), "xT", g, wp, c)

        def drain_turned(eng, copy, k, q):
            b = wait_filled(eng, "T", k, q)
            if k > 0:
                for sl in range(2):
                    wait_filled(eng, "V", k - 1, q // 2, sl)
            drain(copy(wT[:, q, :, :, :, 0:MAINQ].rearrange("p r i h q -> p (r i h) q"),
                       b[:, :].rearrange("p (x q) -> p x q", q=MAINQ)), "T", k, q)

        def drain_mm1(eng, add_bias, g, m, hf):
            b = wait_filled(eng, "mm1", g, m, hf)
            if g > 0:
                wait_filled(eng, "mm2", g - 1, NT - 1)
            drain(add_bias(gT[:, m, hf * HALF:(hf + 1) * HALF], b[:, 0:HALF], hid_bias[:, m:m + 1]),
                  "mm1", g, m, hf)

        def parts(view):
            return [view[:, 0:MAIN // 2], view[:, MAIN // 2:MAIN], view[:, MAIN:COLS]]

        def acc_parts(hg):
            main = acc[:, hg].rearrange("p (r i) m j -> p r (i m) j", i=2)
            return [main[:, 0, :, 0:TOK], main[:, 1, :, 0:TOK], acc_rest[:, hg, :, :]]

        XT_ACT = [(wp, 0) for wp in range(GRID)]
        XT_DVE = [(wp, 1) for wp in range(GRID)]

        @block.scalar
        def _(act):
            def copy(dst, src):
                return act.activation(dst, src, ACT.Identity)

            def add_bias(dst, src, bias):
                return act.activation(dst, src, ACT.Identity, bias=bias)

            for dst, src in row_loads:
                act.dma_start(dst, src).then_inc(rows_loaded, 16)
            for dst, src in small:
                act.dma_start(dst, src, allow_slow_non_contiguous=True).then_inc(small_loaded, 16)
            for dst, src in late:
                act.dma_start(dst, src, allow_slow_non_contiguous=True).then_inc(late_loaded, 16)

            def mix(side, base, step):
                st, pairs = upper_stage(side, step)
                src, dst, width = mix_buffers(side, step)
                if base + step > 0:
                    act.wait_ge(mix_done, base + step)
                for pr, lo, hi in pairs:
                    for o, blk in enumerate((lo, hi)):
                        co = high[:, side, st, pr, 3 * o:3 * o + 1]
                        ins = act.activation(dst[:, blk, 0:width], src[:, blk, 0:width], ACT.Copy, scale=co)
                ins.then_inc(mix_first, 1)

            def drain_ln(g, which):
                for tt, (t0, tn) in enumerate(TILES):
                    b = wait_filled(act, "lnT", g, which, tt)
                    if which == 0:
                        wait_filled(act, "tok", g, NT - 1)
                    elif g > 0:
                        wait_filled(act, "mm1", g - 1, NB - 1, 1)
                    drain(copy(xnT[which][:, :, t0:t0 + tn],
                               b[:, 0:2 * P].rearrange("p (k c) -> p k c", k=2)[:, :, 0:tn]), "lnT", g, which, tt)

            def drain_q(g, hg):
                for hf in range(2):
                    b = wait_filled(act, "q", g, hg, hf)
                    if g > 0:
                        wait_filled(act, "s", 2 * g - 2 + hg, 3)
                        act.wait_ge(q_rest_ready, 2 * g - 1 + hg)
                    for par in range(2):
                        ins = act.activation(qm[:, hg, par, hf * HALF:(hf + 1) * HALF], b[:, 0:HALF], ACT.Identity,
                                             bias=q_bias[:, hg, par:par + 1], scale=par_mask[:, par:par + 1])
                    drain(ins, "q", g, hg, hf)

            def drain_scores(k):
                hg = k % 2
                for r in range(4):
                    b = wait_filled(act, "s", k, r)
                    w = PAIRS * TOK + (REST if r == 3 else 0)
                    drain(copy(s[:, hg, r * PAIRS * TOK:r * PAIRS * TOK + w], b[:, 0:w]), "s", k, r)

            def arguments(c):
                k, f = divmod(c, NF)
                hg = k % 2
                if f == 0:
                    for r in range(4):
                        wait_drained(act, "s", k, r)
                if c >= 2:
                    act.wait_ge(frac_ready, c - 1)
                for x, (dst, src) in enumerate(zip(parts(u[:, c % 2]), parts(s[:, hg]))):
                    ins = act.activation(dst, src, ACT.Identity, bias=turns_alpha[:, UTILES * hg + x, f:f + 1],
                                         scale=inv_freq[:, f:f + 1])
                ins.then_inc(u_ready, 1)

            def sine(c):
                act.wait_ge(frac_ready, c + 1)
                act.activation(n[:, c % 2, :], n[:, c % 2, :], ACT.Sin, scale=SIN_SCALE).then_inc(sin_ready, 1)

            def sigmoid(k):
                hg = k % 2
                act.wait_ge(acc_done, NF * (k + 1))
                v = acc[:, hg, :, :, 0:TOK].rearrange("p r m j -> p (r m) j")
                act.activation(v, v, ACT.Sigmoid)
                v = acc_rest[:, hg, :, :]
                act.activation(v, v, ACT.Sigmoid).then_inc(weights_ready, 1)

            def gelu(g):
                for m in range(NB):
                    for hf in range(2):
                        wait_drained(act, "mm1", g, m, hf)
                for m in range(0, NB, 2):
                    v = gT[:, m:m + 2, :].rearrange("p m x -> p (m x)")
                    ins = act.activation(v, v, ACT.Gelu)
                ins.then_inc(gelu_done, 1)

            def even_heads(k, qp):
                for sl in range(2):
                    b = wait_filled(act, "V", k, qp, sl)
                    if qp == 1:
                        wait_drained(act, "V", k, 0, sl)
                    elif k > 0:
                        wait_drained(act, "V", k - 1, 1, sl)
                    src = b[:, 0:288].rearrange("p (x a i) -> p x a i", x=4, a=2)[:, :, 0, :]
                    act.activation(even[:, sl, :, :], src, ACT.Copy, scale=par_mask[:, 0:1]).then_inc(even_ready, 1)

            def mm1_share(g, lo, hi):
                for m in range(lo, hi):
                    drain_mm1(act, add_bias, g, m, 0)

            act.wait_ge(misc_loaded, 16)
            act.wait_ge(pool_ready, 1)
            for wp, c in XT_ACT:
                drain_xT(act, copy, 0, wp, c)
            for k in range(NT, 2 * NT):
                b = wait_filled(act, "rows", k)
                drain(copy(rows[:, k, :], b[:, 0:E]), "rows", k)
            for w in range(4):
                for k in range(2):
                    b = wait_filled(act, "attnT", w, k)
                    drain(copy(w_attn[:, w, k, :], b[:, 0:E]), "attnT", w, k)
            drain_ln(0, 0)
            act.wait_ge(consts_ready, N_CONSTS)
            drain_q(0, 0)
            drain_scores(0)
            wait_drained(act, "heads")
            arguments(0)
            drain_q(0, 1)
            for step in range(2 * G + 3):
                g, odd = divmod(step, 2)
                for i in range(NF):
                    c = NF * step + i
                    if c + 1 < CHAIN:
                        arguments(c + 1)
                    if not odd:
                        if i == 1:
                            if g < G:
                                drain_scores(2 * g + 1)
                            if g + 1 < G:
                                for wp, cc in XT_ACT[0:3]:
                                    drain_xT(act, copy, g + 1, wp, cc)
                        if i == 0 and 0 <= g - 2 < G:
                            mm1_share(g - 2, 4, 6)
                        if g == 1:
                            if i == 0:
                                for k in range(2):
                                    for cc in range(2):
                                        b = wait_filled(act, "upT", k, cc)
                                        drain(copy(w_up[:, k, cc * 512:(cc + 1) * 512], b[:, :]), "upT", k, cc)
                            if i == 2:
                                act.wait_ge(con_loaded, 16)
                                act.wait_ge(hid_ready, 1)
                                mix(1, 3, 0)
                            if i == 4:
                                mix(1, 3, 2)
                    else:
                        if i == 1 and g + 1 < G:
                            drain_q(g + 1, 0)
                        if g == 0 and i == 2:
                            for a in range(NB):
                                b = wait_filled(act, "low", "u", a)
                                drain(copy(mixA[:, a, :], b[:, 0:EB]), "low", "u", a)
                        if g == 0 and i == 3:
                            for a in range(NB):
                                wait_drained(act, "low", "u", a)
                            act.wait_ge(late_loaded, 16 * len(late))
                            mix(0, 0, 0)
                        if g == 0 and i == 4:
                            mix(0, 0, 1)
                        if i == 4 and 1 <= g <= G:
                            drain_ln(g - 1, 1)
                            mm1_share(g - 1, 0, 2)
                    if c < CHAIN:
                        sine(c)
                    if not odd:
                        if i == 0:
                            if 0 <= g - 2 < G:
                                mm1_share(g - 2, 6, NB)
                            if 0 <= step - 1 < UNITS:
                                sigmoid(step - 1)
                            if 0 <= g - 2 < G:
                                gelu(g - 2)
                        if i == 1 and g + 1 < G:
                            for wp, cc in XT_ACT[3:6]:
                                drain_xT(act, copy, g + 1, wp, cc)
                        if i == 2 and 0 <= step - 1 < UNITS:
                            for q in range(2):
                                drain_turned(act, copy, step - 1, q)
                        if g == 1 and i == 3:
                            mix(1, 3, 1)
                        if g == 0 and i in (3, 4):
                            for a in range(4 * (i - 3), 4 * (i - 2)):
                                b = wait_filled(act, "expT", a)
                                drain(copy(expT[:, a, 0:E], b[:, 0:E]), "expT", a)
                        if i == 4:
                            if 0 <= step - 1 < UNITS:
                                for qp in range(2):
                                    even_heads(step - 1, qp)
                            if g == 1:
                                for a in range(NB):
                                    b = wait_filled(act, "low", "d", a)
                                    drain(copy(w_down[:, a, :], b[:, 0:E]), "low", "d", a)
                    else:
                        if i == 0:
                            if step - 1 < UNITS:
                                sigmoid(step - 1)
                            if g + 1 < G:
                                drain_ln(g + 1, 0)
                        if i == 1 and g + 1 < G:
                            drain_q(g + 1, 1)
                        if i == 2 and step - 1 < UNITS:
                            for q in range(2):
                                drain_turned(act, copy, step - 1, q)
                        if i == 3:
                            if step - 1 < UNITS:
                                for qp in range(2):
                                    even_heads(step - 1, qp)
                            if g + 1 < G:
                                drain_scores(2 * g + 2)
                        if i == 4:
                            if g == 0:
                                mix(0, 0, 2)
                            if 1 <= g <= G:
                                mm1_share(g - 1, 2, 4)

        @block.gpsimd
        def _(pool):
            pool.memset(half_pow[:, :], -0.5).then_inc(pool_ready, 1)
            pool.memset(mv[:, :, :, :], 1.0).then_inc(pool_ready, 1)
            pool.memset(w_rest[:, :, :, :], 0.0).then_inc(pool_ready, 1)
            pool.memset(acc[:, :, :, :, :].rearrange("p a b c d -> p (a b c d)"), 0.0).then_inc(pool_ready, 1)

            def inv_std(g, which):
                k = ln_at[g, which]
                pool.wait_ge(mv_ready, k + 1)
                pool.tensor_scalar(var[:, which, :], mv[:, which, :, 1], 1e-5, 1.0, ALU.add, ALU.mult)\
                    .then_inc(var_ready, 1)
                pool.wait_ge(var_ready, k + 1)
                pool.tensor_tensor(rstd[:, which, :], var[:, which, :], half_pow[:, :], ALU.pow)\
                    .then_inc(rstd_ready, 1)

            def rest_queries(g, hg):
                wait_drained(pool, "q", g, hg, 0)
                wait_drained(pool, "q", g, hg, 1)
                if g > 0:
                    wait_filled(pool, "s", 2 * g - 2 + hg, 3)
                for par in range(2):
                    src = qm[:, hg, par, :].rearrange("p (b i) -> p b i", i=TOK)[:, :, MAINQ:TOK]
                    dst = q_rest[:, hg, :, :].rearrange("p b (r a i) -> p b r a i", r=4, a=2)[:, :, :, par, :]
                    ins = pool.tensor_tensor(
                        dst, src.unsqueeze(2).to_broadcast([P, IPG, 4, RESTQ]),
                        pair_mask.unsqueeze(1).unsqueeze(3).to_broadcast([P, IPG, 4, RESTQ]), ALU.mult)
                ins.then_inc(q_rest_ready, 1)

            def normalise(k):
                hg = k % 2
                pool.wait_ge(recip_ready, k + 1)
                v = acc[:, hg, :, :, 0:TOK].rearrange("p r m j -> p (r m) j")
                rs = rsums[:, hg, 0:4 * PAIRS].unsqueeze(2).to_broadcast([P, 4 * PAIRS, TOK])
                pool.tensor_tensor(v, v, rs, ALU.mult).then_inc(normed, 1)

            def add_row(g, row, done):
                full = row.unsqueeze(1).to_broadcast([P, NT - 1, E])
                pool.tensor_tensor(h[:, g % 3, 0:NT - 1, :], h[:, g % 3, 0:NT - 1, :], full, ALU.add)
                pool.tensor_tensor(h[0:64, g % 3, NT - 1, :], h[0:64, g % 3, NT - 1, :], row[0:64, :], ALU.add)\
                    .then_inc(done, 1)

            def add_beta(g):
                pool.wait_ge(xn_ready[0], NT * (g + 1))
                add_row(g, row_beta, beta_added)

            def add_con(g):
                pool.wait_ge(xn_ready[1], NT * (g + 1))
                add_row(g, row_con, con_added)

            pool.wait_ge(misc_loaded, 16)
            inv_std(0, 0)
            rest_queries(0, 0)
            rest_queries(0, 1)
            for k in range(NT, 2 * NT):
                wait_drained(pool, "rows", k)
            add_beta(0)
            for g in range(G + 1):
                if g > 0:
                    normalise(2 * g - 1)
                if g + 1 < G:
                    inv_std(g + 1, 0)
                if g > 0:
                    inv_std(g - 1, 1)
                if g < G:
                    normalise(2 * g)
                if g + 1 < G:
                    rest_queries(g + 1, 0)
                    rest_queries(g + 1, 1)
                if g > 0:
                    inv_std(g - 1, 2)
                if g + 1 < G:
                    add_beta(g + 1)
                if g > 0:
                    add_con(g - 1)

        @block.vector
        def _(dve):
            def copy(dst, src):
                return dve.tensor_copy(dst, src)

            def add_bias(dst, src, bias):
                return dve.tensor_scalar(dst, src, bias, None, ALU.add)

            k = 0

            def const(ins):
                nonlocal k
                k += 1
                ins.then_inc(consts_ready, 1)
                dve.wait_ge(consts_ready, k)

            for kk in range(KC):
                b = wait_filled(dve, "wT", kk)
                drain(copy(w_tok[:, kk, :], b[:, 0:E]), "wT", kk)
            for wp, c in XT_DVE:
                drain_xT(dve, copy, 0, wp, c)
            for kk in range(NT):
                b = wait_filled(dve, "rows", kk)
                drain(copy(rows[:, kk, :], b[:, 0:E]), "rows", kk)
            dve.wait_ge(misc_loaded, 16)
            dve.wait_ge(small_loaded, 16 * len(small))
            const(dve.tensor_scalar(temp[:, 3:4], temp[:, 0:1], -1.0, None, ALU.mult))
            const(dve.tensor_tensor(temp[:, 3:4], temp[:, 0:1], temp[:, 3:4], ALU.max))
            const(dve.tensor_scalar(temp[:, 1:2], temp[:, 3:4], 0.1, None, ALU.add))
            const(dve.reciprocal(temp[:, 2:3], temp[:, 1:2]))
            for f, freq in enumerate(FREQS):
                const(dve.tensor_scalar(inv_freq[:, f:f + 1], temp[:, 2:3], 1.0 / freq, HD ** -0.5,
                                        ALU.mult, ALU.mult))
            for hg in range(2):
                for par in range(2):
                    const(dve.tensor_tensor(q_bias[:, hg, par:par + 1], qk_bias[:, 0, hg:hg + 1],
                                            par_mask[:, par:par + 1], ALU.mult))
            b = wait_filled(dve, "heads")
            tv = b[:, 0:2 * UTILES * 2 * NF].rearrange("p (k f) -> p k f", k=2 * UTILES)
            dve.tensor_scalar(turns_alpha[:, :, 0:NF], tv[:, :, 0:NF], 1.0 / TWO_PI, None, ALU.mult)
            drain(copy(turns_alpha[:, :, NF:], tv[:, :, NF:]), "heads")
            for kk in range(NT):
                wait_drained(dve, "rows", kk)

            def multiply_stage(side, st):
                src, dst = chain[st % 2], chain[(st + 1) % 2]
                parts_ = 2 if st == LOW - 1 else 1
                blocks = NB // parts_
                w2 = 2 ** st
                if st == 0 and side == "d":
                    wait_filled(dve, "low", "u", NB - 1)
                if st > 0:
                    wait_drained(dve, "bits", side, st - 1, 0)
                for c in range(parts_):
                    b = wait_filled(dve, "bits", side, st, c)
                    wv = b[:, 0:blocks * 2 * w2].rearrange("p (a k o) -> p a o k", a=blocks, o=2)
                    dv = dst[:, c * blocks * 2 * w2:(c + 1) * blocks * 2 * w2].rearrange(
                        "p (a o k) -> p a o k", a=blocks, o=2)
                    if st == 0:
                        ins = copy(dv, wv)
                    else:
                        sv = src[:, c * blocks * w2:(c + 1) * blocks * w2].rearrange(
                            "p (a k) -> p a k", a=blocks)
                        ins = dve.tensor_tensor(dv, wv, sv.unsqueeze(2).to_broadcast([P, blocks, 2, w2]),
                                                ALU.mult)
                    drain(ins, "bits", side, st, c)

            def mix(side, base, step):
                st, pairs = upper_stage(side, step)
                src, dst, width = mix_buffers(side, step)
                dve.wait_ge(mix_first, base + step + 1)
                for pr, lo, hi in pairs:
                    for o, (blk, other) in enumerate(((lo, hi), (hi, lo))):
                        j = 1 + o if side == 0 else 2 - o
                        ins = dve.scalar_tensor_tensor(out=dst[:, blk, 0:width], in0=src[:, other, 0:width],
                                                       scalar=high[:, side, st, pr, j:j + 1],
                                                       in1=dst[:, blk, 0:width], op0=ALU.mult, op1=ALU.add)
                ins.then_inc(mix_done, 1)

            def stats_of(g, which, src, waits):
                base = NT * ln_at[g, which]
                if ln_at[g, which] > 0:
                    dve.wait_ge(mv_ready, ln_at[g, which])
                for tt, (t0, tn) in enumerate(TILES):
                    waits(tt)
                    dve.bn_stats(stats[0:tn, tt, :], src[0:tn, tt, :]).then_inc(stat_step, 1)
                for tt, (t0, tn) in enumerate(TILES):
                    dve.wait_ge(stat_step, base + tt + 1)
                    ins = dve.bn_aggr(mv[0:tn, which, tt, :], stats[0:tn, tt, :])
                ins.then_inc(mv_ready, 1)

            def tok_tiles(g, lo, hi):
                for tt in range(lo, hi):
                    tn = TILES[tt][1]
                    b = wait_filled(dve, "tok", g, tt)
                    if g >= 3:
                        dve.wait_ge(out_stored, 16 * NT * (g - 2))
                    if g == 2:
                        wait_filled(dve, "low", "d", NB - 1)
                    drain(dve.tensor_tensor(h[0:tn, g % 3, tt, :], b[0:tn, 0:E], pos[0:tn, tt, :], ALU.add),
                          "tok", g, tt)

            def tok_stats(g):
                stats_of(g, 0, h[:, g % 3], lambda tt: wait_drained(dve, "tok", g, tt))

            def normed_tiles(g, which):
                w = 0 if which == 0 else 2
                dve.wait_ge(rstd_ready, ln_at[g, w] + 1)
                if which == 0:
                    wait_filled(dve, "tok", g, NT - 1)
                for tt, (t0, tn) in enumerate(TILES):
                    dve.tensor_scalar(xn[which][0:tn, tt, :], h[0:tn, g % 3, tt, :], mv[0:tn, w, tt, 0:1],
                                      rstd[0:tn, w, tt:tt + 1], ALU.subtract, ALU.mult).then_inc(xn_ready[which], 1)

            def drain_k(g, hg):
                for hf in range(2):
                    b = wait_filled(dve, "k", g, hg, hf)
                    if g > 0:
                        wait_filled(dve, "s", 2 * g - 2 + hg, 3)
                    drain(dve.tensor_scalar(kT[:, hg, hf * HALF:(hf + 1) * HALF], b[:, 0:HALF],
                                            qk_bias[:, 1, hg:hg + 1], None, ALU.add), "k", g, hg, hf)

            def drain_v(g):
                for tt, (t0, tn) in enumerate(TILES):
                    b = wait_filled(dve, "v", g, tt)
                    drain(dve.tensor_tensor(xn0[0:tn, tt, :], b[0:tn, 0:E], row_bv[0:tn, :], ALU.add), "v", g, tt)

            def fractions(c):
                dve.wait_ge(u_ready, c + 1)
                if c >= 2:
                    dve.wait_ge(acc_done, c - 1)
                dve.tensor_scalar(n[:, c % 2, :], u[:, c % 2, :], ROUND, ROUND, ALU.add, ALU.subtract)\
                   .then_inc(rounded, 1)
                dve.wait_ge(rounded, c + 1)
                dve.tensor_tensor(n[:, c % 2, :], u[:, c % 2, :], n[:, c % 2, :], ALU.subtract)\
                   .then_inc(frac_ready, 1)

            def accumulate(c):
                k, f = divmod(c, NF)
                hg = k % 2
                dve.wait_ge(sin_ready, c + 1)
                if f > 0:
                    dve.wait_ge(acc_done, c)
                elif k > 1:
                    for q in range(QUADS):
                        wait_filled(dve, "T", k - 2, q)
                srcs = [src.rearrange("p (m j) -> p m j", j=TOK) for src in parts(n[:, c % 2])]
                for x, (dst, src) in enumerate(zip(acc_parts(hg), srcs)):
                    al = turns_alpha[:, UTILES * hg + x, NF + f:NF + f + 1]
                    if f == 0:
                        ins = dve.tensor_scalar(dst, src, al, None, ALU.mult)
                    else:
                        ins = dve.scalar_tensor_tensor(out=dst, in0=src, scalar=al, in1=dst,
                                                       op0=ALU.mult, op1=ALU.add)
                ins.then_inc(acc_done, 1)

            def denominators(k):
                hg = k % 2
                dve.wait_ge(weights_ready, k + 1)
                dve.tensor_reduce(sums[:, hg, 0:4 * PAIRS],
                                  acc[:, hg, :, :, 0:TOK].rearrange("p r m j -> p (r m) j"), AX.X, ALU.add)
                dve.tensor_reduce(sums[:, hg, 4 * PAIRS:], acc_rest[:, hg, :, :], AX.X, ALU.add)\
                   .then_inc(sums_step, 1)
                dve.wait_ge(sums_step, 2 * k + 1)
                dve.tensor_scalar(sums[:, hg, :], sums[:, hg, :], 1e-10, None, ALU.add).then_inc(sums_step, 1)
                dve.wait_ge(sums_step, 2 * k + 2)
                if k > 1:
                    dve.wait_ge(normed, k - 1)
                dve.reciprocal(rsums[:, hg, :], sums[:, hg, :]).then_inc(recip_ready, 1)

            def normalise_rest(k):
                hg = k % 2
                dve.wait_ge(recip_ready, k + 1)
                if k > 0:
                    wait_filled(dve, "rT", k - 1)
                for sl in range(2):
                    p0 = SLOT * sl
                    rs = rsums[p0:p0 + 64, hg, 4 * PAIRS:].unsqueeze(2).to_broadcast([64, QUADS, TOK])
                    ins = dve.tensor_tensor(w_rest[p0:p0 + 64, :, sl, 0:TOK], acc_rest[p0:p0 + 64, hg, :, :], rs,
                                            ALU.mult)
                ins.then_inc(rest_normed, 1)

            def turned_share(k):
                for q in range(2, QUADS):
                    drain_turned(dve, copy, k, q)
                b = wait_filled(dve, "rT", k)
                drain(copy(wT[:, :, :, :, :, MAINQ:TOK].rearrange("p q r i h j -> p (q r i h) j"),
                           b[:, 0:QUADS * 64].rearrange("p (x j) -> p x j", j=RESTQ)), "rT", k)

            def odd_heads(k, qp):
                g, hg = divmod(k, 2)
                if g > 0 and hg == 0 and qp == 0:
                    wait_filled(dve, "o", g - 1, NT - 1)
                for sl in range(2):
                    dve.wait_ge(even_ready, 4 * k + 2 * qp + sl + 1)
                    b = banks[turn["V", k, qp, sl] % BANKS]
                    src = b[:, 0:288].rearrange("p (q i a j) -> p q i a j", q=2, i=2, a=2)[:, :, :, 1, :]
                    dst = oT[:, hg].rearrange("p (v q s i) j -> p v s q i j", v=2, q=2, s=2)[:, qp, sl]
                    ins = dve.scalar_tensor_tensor(
                        out=dst, in0=src, scalar=par_mask[:, 1:2],
                        in1=even[:, sl, :, :].rearrange("p (q i) j -> p q i j", q=2), op0=ALU.mult, op1=ALU.add)
                    drain(ins, "V", k, qp, sl)

            def attn_tiles(g):
                if g > 0:
                    wait_filled(dve, "lnT", g - 1, 1, NT - 1)
                for tt, (t0, tn) in enumerate(TILES):
                    b = wait_filled(dve, "o", g, tt)
                    drain(dve.tensor_tensor(on[0:tn, tt, :], b[0:tn, 0:E], row_bo[0:tn, :], ALU.add), "o", g, tt)

            def attn_stats(g):
                stats_of(g, 1, on, lambda tt: wait_drained(dve, "o", g, tt))

            def attn_residual(g):
                dve.wait_ge(mv_ready, ln_at[g, 1] + 1)
                for tt, (t0, tn) in enumerate(TILES):
                    dve.scalar_tensor_tensor(out=on[0:tn, tt, :], in0=on[0:tn, tt, :],
                                             scalar=mv[0:tn, 1, tt, 0:1], in1=row_gamma[0:tn, :],
                                             op0=ALU.subtract, op1=ALU.mult).then_inc(on_step, 1)
                dve.wait_ge(rstd_ready, ln_at[g, 1] + 1)
                dve.wait_ge(beta_added, g + 1)
                for tt, (t0, tn) in enumerate(TILES):
                    dve.wait_ge(on_step, NT * g + tt + 1)
                    dve.scalar_tensor_tensor(out=h[0:tn, g % 3, tt, :], in0=on[0:tn, tt, :],
                                             scalar=rstd[0:tn, 1, tt:tt + 1], in1=h[0:tn, g % 3, tt, :],
                                             op0=ALU.mult, op1=ALU.add).then_inc(h1_ready, 1)

            def residual_stats(g):
                stats_of(g, 2, h[:, g % 3], lambda tt: dve.wait_ge(h1_ready, NT * g + tt + 1))

            def last_sums(g, lo, hi):
                dve.wait_ge(con_added, g + 1)
                for tt in range(lo, hi):
                    tn = TILES[tt][1]
                    b = wait_filled(dve, "mm2", g, tt)
                    drain(dve.tensor_tensor(h[0:tn, g % 3, tt, :], b[0:tn, 0:E], h[0:tn, g % 3, tt, :], ALU.add),
                          "mm2", g, tt)

            def mm1_share(g, lo, hi):
                for m in range(lo, hi):
                    drain_mm1(dve, add_bias, g, m, 1)

            tok_tiles(0, 0, NT)
            dve.wait_ge(pool_ready, 4)
            tok_stats(0)
            normed_tiles(0, 0)
            for kk in range(NT, 2 * NT):
                wait_drained(dve, "rows", kk)
            drain_k(0, 0)
            fractions(0)
            drain_k(0, 1)
            drain_v(0)
            for step in range(2 * G + 3):
                g, odd = divmod(step, 2)
                has_unit = 0 <= step - 1 < UNITS
                for i in range(NF):
                    c = NF * step + i
                    if c + 1 < CHAIN:
                        fractions(c + 1)
                    if not odd:
                        if i == 0:
                            if 0 <= g - 2 < G:
                                mm1_share(g - 2, 4, 6)
                            if g == 1:
                                dve.wait_ge(mix_done, 3)
                                dve.tensor_tensor(hid_bias[:, :].unsqueeze(2), mixB[:, :, E:EB],
                                                  up_bias[:, :].unsqueeze(2), ALU.add).then_inc(hid_ready, 1)
                                for cc in range(2):
                                    b = wait_filled(dve, "lowT", cc)
                                    drain(copy(lowT[:, 4 * cc:4 * cc + 4, :].rearrange("p a o -> p (a o)"),
                                               b[:, :]), "lowT", cc)
                        if i == 1:
                            if has_unit:
                                denominators(step - 1)
                            if g + 1 < G:
                                for wp, cc in XT_DVE[0:3]:
                                    drain_xT(dve, copy, g + 1, wp, cc)
                        if i == 2 and 0 <= g - 2 < G:
                            last_sums(g - 2, 0, 2)
                        if i == 3 and 0 <= g - 2 < G:
                            last_sums(g - 2, 2, NT)
                        if i == (3 if g == 0 else 4) and g != 1 and g + 1 < G:
                            tok_tiles(g + 1, 3, NT)
                        if g == 1 and i == 4:
                            mix(1, 3, 1)
                    else:
                        if i == 0:
                            if g + 1 < G:
                                normed_tiles(g + 1, 0)
                            if 1 <= g <= G:
                                attn_tiles(g - 1)
                        if i == 1:
                            if has_unit:
                                denominators(step - 1)
                            if g + 1 < G:
                                drain_k(g + 1, 0)
                        if i == 2 and 1 <= g <= G:
                            attn_residual(g - 1)
                        if i == 3:
                            if 1 <= g <= G:
                                residual_stats(g - 1)
                            if g + 1 < G:
                                drain_v(g + 1)
                        if g == 0 and i == 4:
                            mix(0, 0, 0)
                    if c < CHAIN:
                        accumulate(c)
                    if not odd:
                        if i == 0 and 0 <= g - 2 < G:
                            mm1_share(g - 2, 6, NB)
                        if i == 1:
                            if has_unit:
                                normalise_rest(step - 1)
                            if g + 1 < G:
                                for wp, cc in XT_DVE[3:6]:
                                    drain_xT(dve, copy, g + 1, wp, cc)
                        if i == 2:
                            if has_unit:
                                turned_share(step - 1)
                            if g == 0:
                                tok_tiles(1, 0, 3)
                        if i == 3:
                            if 1 < g and g + 1 < G:
                                tok_tiles(g + 1, 0, 3)
                            if g == 1:
                                mix(1, 3, 0)
                        if i == 4:
                            if g == 1:
                                for qp in range(2):
                                    odd_heads(step - 1, qp)
                                mix(1, 3, 2)
                                tok_tiles(2, 0, NT)
                            if g + 1 < G:
                                tok_stats(g + 1)
                            if has_unit and g != 1:
                                for qp in range(2):
                                    odd_heads(step - 1, qp)
                            if g == 0:
                                for st in range(LOW):
                                    multiply_stage("u", st)
                    else:
                        if i == 0 and 1 <= g <= G:
                            attn_stats(g - 1)
                        if i == 1:
                            if has_unit:
                                normalise_rest(step - 1)
                            if g + 1 < G:
                                drain_k(g + 1, 1)
                        if i == 2 and has_unit:
                            turned_share(step - 1)
                        if i == 3:
                            if has_unit:
                                for qp in range(2):
                                    odd_heads(step - 1, qp)
                            if 1 <= g <= G:
                                normed_tiles(g - 1, 1)
                        if i == 4:
                            if g == 0:
                                mix(0, 0, 1)
                                mix(0, 0, 2)
                                for st in range(LOW):
                                    multiply_stage("d", st)
                            if 1 <= g <= G:
                                mm1_share(g - 1, 0, 4)


_INS = ["x", "L0_tok_W_proj", "L0_tok_b_proj", "L0_tok_pos_emb", "L0_attn_Wq", "L0_attn_bq", "L0_attn_Wk",
        "L0_attn_bk", "L0_attn_Wv", "L0_attn_bv", "L0_attn_Wo", "L0_attn_bo", "L0_attn_alpha", "L0_attn_phi",
        "L0_attn_temperature", "L0_attn_gamma", "L0_attn_beta", "L0_ffn_W_exp", "L0_ffn_b_exp",
        "L0_ffn_up_weights", "L0_ffn_up_bias", "L0_ffn_down_weights", "L0_ffn_W_con", "L0_ffn_b_con",
        "L0_ffn_down_bias"]


def kernel(**inputs):
    import concourse.bacc as _bacc
    from concourse.bass_utils import run_bass_kernel_spmd as _run

    nc = _bacc.Bacc("TRN2", target_bir_lowering=False, num_devices=1)
    arrays, tensors = {}, {}

    def give(name, a):
        arrays[f"in_{name}"] = a
        tensors[name] = nc.dram_tensor(f"in_{name}", a.shape, mybir.dt.from_np(a.dtype), kind="ExternalInput").ap()

    for name in _INS:
        give(name, np.ascontiguousarray(inputs[name]))
    for name, a in zip(("misc", "heads", "bits", "rows"), shape_constants()):
        give(name, a)
    tensors["out"] = nc.dram_tensor("out", (IMAGES, TOK, E), F32, kind="ExternalOutput").ap()
    build(nc, tensors)
    r = _run(nc, [arrays], core_ids=[0])
    return r.results[0]["out"]
```

```python
from contextlib import ExitStack

import numpy as np

import concourse.bass as bass
from concourse import mybir

F32 = mybir.dt.float32
ALU = mybir.AluOpType
ACT = mybir.ActivationFunctionType
AX = mybir.AxisListType

P = 128
IMAGES, SIDE, CH, PATCH = 64, 96, 3, 16
GRID = SIDE // PATCH
TOK = GRID * GRID
PD = PATCH * PATCH * CH
ROW = PATCH * CH
E = 256
HEADS, HD = 16, 16
FREQS = [31.0, 37.0, 41.0, 43.0, 47.0]
NF = len(FREQS)
HID = 1024
NB = HID // P
LOW = 7
TWO_PI = 2.0 * float(np.pi)
SIN_SCALE = 6.283185
ROUND = 12582912.0

G = 4
IPG = IMAGES // G
TPG = IPG * TOK
TILES = [(t * P, min(P, TPG - t * P)) for t in range((TPG + P - 1) // P)]
NT = len(TILES)
HALF = TPG // 2
BH = IPG * GRID
KC = PD // P
MAINQ = 32
RESTQ = TOK - MAINQ
PAIRS = IPG // 2
QUADS = IPG // 4
MAIN = 4 * PAIRS * TOK
REST = QUADS * TOK
COLS = MAIN + REST
SLOT = 64
BANKS = 8
UNITS = 2 * G
UTILES = 3
CHAIN = UNITS * NF
N_CONSTS = 4 + NF + 4


def turn_order():
    def patches(g):
        return [("xT", g, wp, c) for wp in range(GRID) for c in range(2)]

    def tokens(g):
        return [("tok", g, t) for t in range(NT)]

    def lnT(g, which):
        return [("lnT", g, which, t) for t in range(NT)]

    def qk(g, hg):
        return [(w, g, hg, hf) for w in "qk" for hf in range(2)]

    def scores(k):
        return [("s", k, r) for r in range(4)]

    def weights_turned(k):
        return [("T", k, q) for q in range(QUADS)] + [("rT", k)]

    def values(k):
        return [("V", k, qp, sl) for qp in range(QUADS // 2) for sl in range(2)]

    def bits(side):
        return [("bits", side, s, c) for s in range(LOW) for c in range(2 if s == LOW - 1 else 1)]

    def mm2(g, lo, hi):
        return [("mm2", g, t) for t in range(lo, hi)]

    names = [("wT", k) for k in range(KC)] + patches(0) + tokens(0)
    names += [("attnT", w, k) for w in range(4) for k in range(2)] + [("heads",)] + lnT(0, 0)
    names += qk(0, 0) + scores(0) + qk(0, 1) + [("v", 0, t) for t in range(NT)]
    for g in range(G + 2):
        if g + 1 < G and g != 1:
            names += patches(g + 1)
        if g < G:
            names += scores(2 * g + 1)
        if g == 1:
            names += patches(2)
        if g == 0:
            names += tokens(1) + [("expT", a) for a in range(NB)] + bits("u")
        if 2 <= g < G:
            names += mm2(g - 2, 0, 2)
        if 1 <= g <= G:
            names += weights_turned(2 * g - 1)
        if g == 1:
            names += [("upT", k, c) for k in range(2) for c in range(2)] + [("lowT", c) for c in range(2)]
        if 2 <= g < G - 1:
            names += mm2(g - 2, 2, NT)
        if 1 <= g < G - 1:
            names += tokens(g + 1)[0:3]
        if 1 <= g <= G:
            names += values(2 * g - 1)
        if 1 <= g < G - 1:
            names += tokens(g + 1)[3:]
        if 1 <= g <= G:
            if g == G - 1:
                names += mm2(g - 2, 2, 3)
            names += [("o", g - 1, t) for t in range(NT)]
        if g >= G:
            names += mm2(g - 2, 0, NT)
        if g + 1 < G:
            names += lnT(g + 1, 0) + qk(g + 1, 0) + qk(g + 1, 1)
        if g == 0:
            names += [("low", "u", a) for a in range(NB)]
        if g + 1 < G:
            names += scores(2 * g + 2)
        if g < G:
            names += weights_turned(2 * g)
        if g == G - 1:
            names += mm2(g - 2, 3, NT)
        if g + 1 < G:
            names += [("v", g + 1, t) for t in range(NT)]
        if g < G:
            names += values(2 * g)
        if g == 0:
            names += bits("d")
        if g == 1:
            names += [("low", "d", a) for a in range(NB)]
        if 1 <= g <= G:
            names += lnT(g - 1, 1) + [("mm1", g - 1, m, hf) for m in range(NB) for hf in range(2)]
    return names


def shape_constants():
    ident = np.eye(P, dtype=np.float32)
    p = np.arange(P)
    i, hd8, q4 = (p % 64) // 32, (p % 32) // RESTQ, p % RESTQ
    fold = (((hd8 // 4) * 2 + i) * 16 + (hd8 % 4) * RESTQ + q4)[:, None] == np.arange(64)[None, :]
    par = np.stack([(p // HD) % 2 == 0, (p // HD) % 2 == 1], 1)
    pair = p[:, None] // 32 == np.arange(4)[None, :]
    misc = np.concatenate([ident, fold, par, pair], 1).astype(np.float32)
    heads = np.zeros((HEADS, 2 * UTILES, P), np.float32)
    for hg in range(2):
        for r in range(2):
            heads[8 * hg + 4 * r + p // 32, hg * UTILES + r, p] = 1
        heads[8 * hg + (p % 32) // RESTQ, hg * UTILES + 2, p] = 1
    bits = np.zeros((64, LOW, 2, P), np.float32)
    for s in range(LOW):
        bits[p >> (s + 1), s, (p >> s) & 1, p] = 1
    return misc, heads.reshape(HEADS, 2 * UTILES * P), bits.reshape(64, LOW * 2 * P)


def build(nc, t):
    order = turn_order()
    turn = {name: i for i, name in enumerate(order)}
    with ExitStack() as ctx:
        def sb(name, *shape):
            return ctx.enter_context(nc.sbuf_tensor(name, list(shape), F32))

        def sem(name):
            return ctx.enter_context(nc.semaphore(name))

        banks = [ctx.enter_context(nc.psum_tensor(f"bank{k}", [P, 512], F32)) for k in range(BANKS)]

        misc = sb("misc", P, P + 64 + 2 + 4)
        ident, fold = misc[:, 0:P], misc[:, P:P + 64]
        par_mask, pair_mask = misc[:, P + 64:P + 66], misc[:, P + 66:P + 70]
        phi_alpha = sb("phi_alpha", HEADS, 2 * NF)
        turns_alpha = sb("turns_alpha", P, 2 * UTILES, 2 * NF)
        temp = sb("temp", P, 4)
        inv_freq = sb("inv_freq", P, NF)
        w_tok = sb("w_tok", P, KC, E)
        w_attn = sb("w_attn", P, 4, 2, E)
        w_up = sb("w_up", P, 2, HID)
        w_down = sb("w_down", P, NB, E)
        hid_bias = sb("hid_bias", P, NB)
        up_bias = sb("up_bias", P, NB)
        rows = sb("rows", P, 2 * NT, E)
        pos = rows[:, 0:NT, :]
        row_bv, row_bo, row_gamma, row_beta, row_con = (rows[:, NT + n, :] for n in range(5))
        qk_bias = sb("qk_bias", P, 2, 2)
        q_bias = sb("q_bias", P, 2, 2)
        half_pow = sb("half_pow", P, NT)
        high = sb("high", P, 2, 3, 4, 4)

        x_in = sb("x_in", BH, GRID, PD)
        patT = sb("patT", P, KC, TPG)
        patT_f = patT[:, :, :].rearrange("p k t -> p (k t)")
        xn0 = patT_f[:, 2 * TPG:2 * TPG + NT * E].rearrange("p (t e) -> p t e", e=E)
        on = sb("on", P, NT, E)
        xnT1 = sb("xnT1", P, 2, TPG)
        xn, xnT = (xn0, on), (patT[:, 0:2, :], xnT1[:, :, :])
        wT = sb("wT", P, QUADS, 2, 2, 4, TOK)
        oT = sb("oT", P, 2, IPG, TOK)
        h = sb("h", P, 3, NT, E)
        stats = sb("stats", P, NT, 6)
        mv = sb("mv", P, 3, NT, 2)
        var = sb("var", P, 3, NT)
        rstd = sb("rstd", P, 3, NT)
        qm = sb("qm", P, 2, 2, TPG)
        kT = sb("kT", P, 2, TPG)
        q_rest = sb("q_rest", P, 2, IPG, 32)
        v_sl = sb("v_sl", P, QUADS, 2, E)
        s = sb("s", P, 2, COLS)
        u = sb("u", P, 2, COLS)
        n = sb("n", P, 2, COLS)
        acc = sb("acc", P, 2, 4, PAIRS, SLOT)
        acc_rest = sb("acc_rest", P, 2, QUADS, TOK)
        w_rest = sb("w_rest", P, QUADS, 2, SLOT)
        sums = sb("sums", P, 2, 4 * PAIRS + QUADS)
        rsums = sb("rsums", P, 2, 4 * PAIRS + QUADS)
        even = sb("even", P, 2, 4, TOK)
        gT = sb("gT", P, NB, TPG)

        gT_f = gT[:, :, :].rearrange("p a b -> p (a b)")
        nat_tok = gT_f[:, 0:2 * PD].rearrange("p (m d) -> p m d", m=2)
        nat_attn = gT_f[:, 2 * PD:2 * PD + 8 * E].rearrange("p (w m e) -> p w m e", w=4, m=2)
        nat_exp = w_up
        EB = E + 1
        mixA, mixB = (gT_f[:, k * NB * EB:(k + 1) * NB * EB].rearrange("p (a e) -> p a e", a=NB) for k in range(2))
        expT = mixB
        h_f = h[:, 2, :, :].rearrange("p b c -> p (b c)")
        on_f = on[:, :, :].rearrange("p b c -> p (b c)")
        row_proj, row_down = xnT1[:, 0, 0:E], xnT1[:, 1, 0:E]
        head_sel = on_f[0:HEADS, 0:2 * UTILES * P]
        chain = [h_f[:, 0:HID], on_f[:, 0:HID]]
        lowT = xnT1[:, :, :].rearrange("p a b -> p (a b)")[:, 0:HID].rearrange("p (a o) -> p a o", a=NB)
        x_f = x_in[:, :, :].rearrange("p a b -> p (a b)")
        stage_row = [0] * (LOW - 1) + [64]
        stage_at = [32 * (2 ** st - 1) for st in range(LOW - 1)] + [0]
        stage_w, bit_sel = [], []
        for st in range(LOW):
            rows_ = slice(stage_row[st], stage_row[st] + 2 ** (LOW - 1 - st))
            stage_w.append(x_f[rows_, stage_at[st]:stage_at[st] + 32 * 2 ** st].rearrange("p (a k) -> p a k", a=NB))
            at = 32 * 2 ** (LOW - 1) + 2 * P * st
            bit_sel.append(x_f[rows_, at:at + 2 * P].rearrange("p (i q) -> p i q", i=2))

        v_dram = nc.dram_tensor("v_scratch", (G, TPG, E), F32)
        pos_dram = nc.dram_tensor("pos_scratch", (TPG, E), F32)

        filled = [sem(f"bank_filled{k}") for k in range(BANKS)]
        drained = [sem(f"bank_drained{k}") for k in range(BANKS)]
        misc_loaded = sem("misc_loaded")
        rows_loaded = sem("rows_loaded")
        pos_stored = sem("pos_stored")
        pos_loaded = sem("pos_loaded")
        rows_ready = sem("rows_ready")
        small_loaded = sem("small_loaded")
        late_loaded = sem("late_loaded")
        tok_loaded = sem("tok_loaded")
        attn_loaded = sem("attn_loaded")
        exp_loaded = sem("exp_loaded")
        con_loaded = sem("con_loaded")
        bit_sel_loaded = sem("bit_sel_loaded")
        stages_loaded = sem("stages_loaded")
        x_loaded = [sem(f"x_loaded{wp}") for wp in range(GRID)]
        v_stored = sem("v_stored")
        v_loaded = sem("v_loaded")
        out_stored = sem("out_stored")
        consts_ready = sem("consts_ready")
        pool_ready = sem("pool_ready")
        mix_first = sem("mix_first")
        mix_done = sem("mix_done")
        hid_ready = sem("hid_ready")
        u_ready = sem("u_ready")
        rounded = sem("rounded")
        frac_ready = sem("frac_ready")
        sin_ready = sem("sin_ready")
        acc_done = sem("acc_done")
        weights_ready = sem("weights_ready")
        sums_step = sem("sums_step")
        recip_ready = sem("recip_ready")
        normed = sem("normed")
        rest_normed = sem("rest_normed")
        even_ready = sem("even_ready")
        stat_step = sem("stat_step")
        mv_ready = sem("mv_ready")
        var_ready = sem("var_ready")
        rstd_ready = sem("rstd_ready")
        xn_ready = [sem(f"xn{w}_ready") for w in range(2)]
        beta_added = sem("beta_added")
        on_step = sem("on_step")
        h1_ready = sem("h1_ready")
        con_added = sem("con_added")
        q_rest_ready = sem("q_rest_ready")
        gelu_done = sem("gelu_done")

        def open_turn(pe, *name):
            i = turn[name]
            if i >= BANKS:
                pe.wait_ge(drained[i % BANKS], i // BANKS)
            return banks[i % BANKS]

        def close_turn(ins, *name):
            ins.then_inc(filled[turn[name] % BANKS], 1)

        def wait_filled(eng, *name):
            i = turn[name]
            eng.wait_ge(filled[i % BANKS], i // BANKS + 1)
            return banks[i % BANKS]

        def drain(ins, *name):
            ins.then_inc(drained[turn[name] % BANKS], 1)

        def wait_drained(eng, *name):
            i = turn[name]
            eng.wait_ge(drained[i % BANKS], i // BANKS + 1)

        ln_order = [(0, 0)]
        for g in range(G + 1):
            ln_order += [(g + 1, 0)] * (g + 1 < G) + [(g - 1, 1), (g - 1, 2)] * (g > 0)
        ln_at = {name: k for k, name in enumerate(ln_order)}

        misc_in, head_in, bit_in = t["misc"], t["heads"], t["bits"]
        block = ctx.enter_context(nc.Block())

        row_loads = [(dst, t[f"L0_{name}"].partition_broadcast(P)) for dst, name in (
            (row_proj, "tok_b_proj"), (row_bv, "attn_bv"), (row_bo, "attn_bo"), (row_gamma, "attn_gamma"),
            (row_beta, "attn_beta"), (row_con, "ffn_b_con"), (row_down, "ffn_down_bias"))]
        small = [
            (head_sel, head_in),
            (phi_alpha[:, 0:NF], t["L0_attn_phi"]), (phi_alpha[:, NF:2 * NF], t["L0_attn_alpha"]),
            (temp[:, 0:1], t["L0_attn_temperature"].partition_broadcast(P)),
            (qk_bias[:, 0, :], t["L0_attn_bq"].rearrange("(m p) -> p m", p=P)),
            (qk_bias[:, 1, :], t["L0_attn_bk"].rearrange("(m p) -> p m", p=P)),
        ]
        late = [(up_bias[:, :], t["L0_ffn_up_bias"].rearrange("(a p) -> p a", p=P))]
        for side, name in ((0, "up"), (1, "down")):
            w = t[f"L0_ffn_{name}_weights"]
            for st in range(3):
                late.append((high[:, side, st, :, :],
                             w[LOW + st].rearrange("(g p) o i -> p g (o i)", p=P)))

        def mix_buffers(side, step):
            if side == 1 and step == 0:
                return w_down, mixB, E
            pair = (mixA, mixB) if step % 2 == 0 else (mixB, mixA)
            return *pair, EB if side == 0 else E

        def upper_stage(side, step):
            st = step if side == 0 else 2 - step
            los = [((pr >> st) << (st + 1)) | (pr & (2 ** st - 1)) for pr in range(4)]
            return st, [(pr, lo, lo + 2 ** st) for pr, lo in enumerate(los)]

        @block.sync
        def _(sp):
            def load_x(g):
                src = t["x"][g * IPG:(g + 1) * IPG].rearrange(
                    "b (hp i) (wp j) c -> (b hp) wp i (j c)", hp=GRID, wp=GRID)
                for wp in range(GRID):
                    if g == 2:
                        wait_filled(sp, "bits", "d", LOW - 1, 1)
                    elif g > 0:
                        wait_filled(sp, "xT", g - 1, wp, 1)
                    sp.dma_start(x_in[:, wp, :].rearrange("p (i k) -> p i k", i=PATCH),
                                 src[:, wp]).then_inc(x_loaded[wp], 16)

            def load_stages(name):
                w = t[f"L0_ffn_{name}_weights"]
                for st in range(LOW):
                    sp.dma_start(stage_w[st], w[st].rearrange("(a i k) o j -> i a (k o j)", a=NB, k=2 ** st))\
                      .then_inc(stages_loaded, 16)

            def store_v(g):
                wait_drained(sp, "v", g, NT - 1)
                full = TPG // P
                sp.dma_start(v_dram.ap()[g, 0:full * P, :].rearrange("(t p) e -> p t e", p=P),
                             xn0[:, 0:full, :]).then_inc(v_stored, 16)
                sp.dma_start(v_dram.ap()[g, full * P:TPG, :], xn0[0:TPG - full * P, full, :]).then_inc(v_stored, 16)

            def load_v(g):
                sp.wait_ge(v_stored, 32 * (g + 1))
                if g > 0:
                    for sl in range(2):
                        wait_filled(sp, "V", 2 * g - 1, QUADS // 2 - 1, sl)
                view = v_dram.ap()[g].rearrange("(q s i j) e -> s i j q e", q=QUADS, s=2, i=2)
                for sl in range(2):
                    for i in range(2):
                        sp.dma_start(v_sl[SLOT * sl:SLOT * sl + TOK, :, i, :], view[sl, i]).then_inc(v_loaded, 16)

            def store_out(g):
                for tt, (t0, tn) in enumerate(TILES):
                    wait_drained(sp, "mm2", g, tt)
                    sp.dma_start(t["out"].rearrange("b n e -> (b n) e")[g * TPG + t0:g * TPG + t0 + tn, :],
                                 h[0:tn, g % 3, tt, :]).then_inc(out_stored, 16)

            sp.dma_start(misc[:, :], misc_in).then_inc(misc_loaded, 16)
            load_x(0)
            for w, name in enumerate(("Wq", "Wk", "Wv", "Wo")):
                sp.dma_start(nat_attn[:, w], t[f"L0_attn_{name}"].rearrange("(m p) e -> p m e", p=P))\
                  .then_inc(attn_loaded, 16)
            load_x(1)
            sp.dma_start(nat_exp[:, :, :], t["L0_ffn_W_exp"].rearrange("(m p) d -> p m d", p=P))\
              .then_inc(exp_loaded, 16)
            sp.dma_start(w_down[:, :, :], t["L0_ffn_W_con"].rearrange("(a p) e -> p a e", p=P)).then_inc(con_loaded, 16)
            wait_filled(sp, "attnT", 3, 1)
            sp.dma_start(expT[:, :, E:EB], t["L0_ffn_b_exp"].rearrange("(a p u) -> p a u", p=P, u=1),
                         allow_slow_non_contiguous=True).then_inc(exp_loaded, 16)
            store_v(0)
            load_v(0)
            for wp in range(GRID):
                wait_filled(sp, "xT", 1, wp, 1)
            low_bits = 2 * P * (LOW - 1)
            sp.dma_start(x_f[0:64, 32 * 2 ** (LOW - 1):32 * 2 ** (LOW - 1) + low_bits], bit_in[:, 0:low_bits])\
              .then_inc(bit_sel_loaded, 16)
            sp.dma_start(bit_sel[LOW - 1].rearrange("p i q -> p (i q)"), bit_in[0:1, low_bits:])\
              .then_inc(bit_sel_loaded, 16)
            load_stages("up")
            for g in range(G + 2):
                if 3 <= g + 2 < G:
                    load_x(g + 2)
                if g == G - 1:
                    load_v(g)
                if g >= 2:
                    store_out(g - 2)
                if 1 <= g < G - 1:
                    load_v(g)
                if g == 0:
                    wait_filled(sp, "bits", "u", LOW - 1, 1)
                    load_stages("down")
                if g + 1 < G:
                    store_v(g + 1)
                if g == 0:
                    load_x(2)
            sp.wait_ge(out_stored, 16 * NT * G)

        @block.tensor
        def _(pe):
            def flip(out, in_, rows_):
                return pe.transpose(out, in_, ident[0:rows_, 0:rows_])

            def patches(g):
                for wp in range(GRID):
                    pe.wait_ge(x_loaded[wp], 16 * (g + 1))
                    for c in range(2):
                        b = open_turn(pe, "xT", g, wp, c)
                        for k in range(3):
                            d0 = (3 * c + k) * P
                            ins = flip(b[:, k * BH:(k + 1) * BH], x_in[:, wp, d0:d0 + P], BH)
                        close_turn(ins, "xT", g, wp, c)

            def tokens(g, lo=0, hi=NT):
                for wp in range(GRID):
                    for c in range(2):
                        wait_drained(pe, "xT", g, wp, c)
                for tt in range(lo, hi):
                    t0, tn = TILES[tt]
                    b = open_turn(pe, "tok", g, tt)
                    for k in range(KC):
                        ins = pe.matmul(b[0:tn, 0:E], patT[:, k, t0:t0 + tn], w_tok[:, k, :],
                                        start=(k == 0), stop=(k == KC - 1))
                    close_turn(ins, "tok", g, tt)

            def ln_turns(g, which):
                for tt, (t0, tn) in enumerate(TILES):
                    pe.wait_ge(xn_ready[which], NT * g + tt + 1)
                    b = open_turn(pe, "lnT", g, which, tt)
                    for k in range(2):
                        ins = flip(b[:, k * P:k * P + tn], xn[which][0:tn, tt, k * P:(k + 1) * P], tn)
                    close_turn(ins, "lnT", g, which, tt)
                for tt in range(NT):
                    wait_drained(pe, "lnT", g, which, tt)

            def qk(g, hg):
                for wi, w in enumerate("qk"):
                    for hf in range(2):
                        b = open_turn(pe, w, g, hg, hf)
                        for k in range(2):
                            ins = pe.matmul(b[:, 0:HALF], w_attn[:, wi, k, hg * P:(hg + 1) * P],
                                            xnT[0][:, k, hf * HALF:(hf + 1) * HALF],
                                            start=(k == 0), stop=(k == 1))
                        close_turn(ins, w, g, hg, hf)

            def v_tiles(g):
                for tt, (t0, tn) in enumerate(TILES):
                    b = open_turn(pe, "v", g, tt)
                    for k in range(2):
                        ins = pe.matmul(b[0:tn, 0:E], xnT[0][:, k, t0:t0 + tn], w_attn[:, 2, k, :],
                                        start=(k == 0), stop=(k == 1))
                    close_turn(ins, "v", g, tt)

            def scores(k):
                g, hg = divmod(k, 2)
                for hf in range(2):
                    wait_drained(pe, "q", g, hg, hf)
                    wait_drained(pe, "k", g, hg, hf)
                pe.wait_ge(q_rest_ready, k + 1)
                tiles = [open_turn(pe, "s", k, r) for r in range(4)]

                def main(swap):
                    last = {}
                    for m in range(PAIRS):
                        for r in range(2):
                            for a in range(2):
                                i = a ^ swap
                                t0 = (2 * m + i) * TOK
                                for par in range(2):
                                    c = 32 * (2 * a + par)
                                    rows_ = slice(32 * (2 * r + a), 32 * (2 * r + a) + 32)
                                    ins = pe.matmul(tiles[2 * r + i][c:c + 32, m * TOK:(m + 1) * TOK],
                                                    qm[rows_, hg, par, t0:t0 + MAINQ],
                                                    kT[rows_, hg, t0:t0 + TOK],
                                                    start=True, stop=True, skip_group_check=True)
                                    last[2 * r + i] = ins
                    return last

                main(0)
                for im in range(IPG):
                    c = 32 * (im % 4)
                    c0 = (PAIRS + im // 4) * TOK
                    pe.matmul(tiles[3][c:c + 32, c0:c0 + TOK],
                              q_rest[:, hg, im, :], kT[:, hg, im * TOK:(im + 1) * TOK],
                              start=True, stop=True, skip_group_check=True)
                for r, ins in main(1).items():
                    close_turn(ins, "s", k, r)

            def turn_weights(k):
                hg = k % 2
                pe.wait_ge(normed, k + 1)
                pe.wait_ge(rest_normed, k + 1)
                for q in range(QUADS):
                    b = open_turn(pe, "T", k, q)
                    for r in range(4):
                        ins = flip(b[:, r * P:(r + 1) * P],
                                   acc[:, hg, r, 2 * q:2 * q + 2, :].rearrange("p a b -> p (a b)"), P)
                    close_turn(ins, "T", k, q)
                b = open_turn(pe, "rT", k)
                for q in range(QUADS):
                    ins = pe.matmul(b[:, q * 64:(q + 1) * 64], w_rest[:, q, :, :].rearrange("p a b -> p (a b)"),
                                    fold, start=True, stop=True, skip_group_check=True)
                close_turn(ins, "rT", k)

            def values(k):
                g, hg = divmod(k, 2)
                pe.wait_ge(v_loaded, 64 * (g + 1))
                for q in range(QUADS):
                    wait_drained(pe, "T", k, q)
                wait_drained(pe, "rT", k)
                for qp in range(QUADS // 2):
                    b = [open_turn(pe, "V", k, qp, sl) for sl in range(2)]
                    last = [None, None]
                    for q2 in range(2):
                        q = 2 * qp + q2
                        for i in range(2):
                            for r in range(4):
                                for sl in range(2):
                                    p0 = SLOT * sl
                                    last[sl] = pe.matmul(
                                        b[sl][32 * r:32 * r + 32, (q2 * 2 + i) * 72:(q2 * 2 + i + 1) * 72],
                                        v_sl[p0:p0 + TOK, q, i, hg * P + 32 * r:hg * P + 32 * r + 32],
                                        wT[p0:p0 + TOK, q, r // 2, i, 2 * (r % 2):2 * (r % 2) + 2, :].rearrange(
                                            "p a b -> p (a b)"),
                                        start=True, stop=True, skip_group_check=True)
                    for sl in range(2):
                        close_turn(last[sl], "V", k, qp, sl)

            def out_proj(g):
                for k in (2 * g, 2 * g + 1):
                    for qp in range(2):
                        for sl in range(2):
                            wait_drained(pe, "V", k, qp, sl)
                flat = oT[:, :, :, :].rearrange("p m b i -> p m (b i)")
                for tt, (t0, tn) in enumerate(TILES):
                    b = open_turn(pe, "o", g, tt)
                    for k in range(2):
                        ins = pe.matmul(b[0:tn, 0:E], flat[:, k, t0:t0 + tn], w_attn[:, 3, k, :],
                                        start=(k == 0), stop=(k == 1))
                    close_turn(ins, "o", g, tt)

            def mm1(g):
                for m in range(NB):
                    for hf in range(2):
                        b = open_turn(pe, "mm1", g, m, hf)
                        for k in range(2):
                            ins = pe.matmul(b[:, 0:HALF], w_up[:, k, m * P:(m + 1) * P],
                                            xnT[1][:, k, hf * HALF:(hf + 1) * HALF],
                                            start=(k == 0), stop=(k == 1))
                        close_turn(ins, "mm1", g, m, hf)

            def mm2(g, lo, hi):
                if g < G - 1:
                    pe.wait_ge(gelu_done, g + 1)
                else:
                    for m in range(NB):
                        for hf in range(2):
                            wait_drained(pe, "mm1", g, m, hf)
                for tt in range(lo, hi):
                    t0, tn = TILES[tt]
                    b = open_turn(pe, "mm2", g, tt)
                    for k in range(NB):
                        ins = pe.matmul(b[0:tn, 0:E], gT[:, k, t0:t0 + tn], w_down[:, k, :],
                                        start=(k == 0), stop=(k == NB - 1))
                    close_turn(ins, "mm2", g, tt)

            def stage_bits(side):
                for st in range(LOW):
                    parts = 2 if st == LOW - 1 else 1
                    for c in range(parts):
                        blocks = NB // parts
                        b = open_turn(pe, "bits", side, st, c)
                        width = blocks * 2 ** (st + 1)
                        for i in range(2):
                            src = stage_w[st][:, c * blocks:(c + 1) * blocks, :]
                            src = src.rearrange("p a (k i) -> p a k i", i=2)[:, :, :, i]
                            ins = pe.matmul(b[:, 0:width].rearrange("p (a k) -> p a k", a=blocks),
                                            bit_sel[st][:, i, :], src,
                                            start=(i == 0), stop=(i == 1))
                        close_turn(ins, "bits", side, st, c)

            def chain_out():
                return chain[LOW % 2].rearrange("p (a o) -> p a o", a=NB)

            pe.wait_ge(misc_loaded, 16)
            pe.wait_ge(tok_loaded, 16)
            for k in range(KC):
                b = open_turn(pe, "wT", k)
                for m in range(2):
                    ins = flip(b[:, m * P:(m + 1) * P], nat_tok[:, m, k * P:(k + 1) * P], P)
                close_turn(ins, "wT", k)
            patches(0)
            for k in range(KC):
                wait_drained(pe, "wT", k)
            tokens(0)
            pe.wait_ge(attn_loaded, 16 * 4)
            for w in range(4):
                for k in range(2):
                    b = open_turn(pe, "attnT", w, k)
                    for m in range(2):
                        ins = flip(b[:, m * P:(m + 1) * P], nat_attn[:, w, m, k * P:(k + 1) * P], P)
                    close_turn(ins, "attnT", w, k)
            pe.wait_ge(small_loaded, 16 * len(small))
            b = open_turn(pe, "heads")
            for k in range(2 * UTILES):
                ins = pe.matmul(b[:, k * 2 * NF:(k + 1) * 2 * NF], head_sel[:, k * P:(k + 1) * P],
                                phi_alpha[:, :], start=True, stop=True)
            close_turn(ins, "heads")
            for w in range(4):
                for k in range(2):
                    wait_drained(pe, "attnT", w, k)
            ln_turns(0, 0)
            qk(0, 0)
            scores(0)
            qk(0, 1)
            v_tiles(0)
            for g in range(G + 2):
                if g + 1 < G and g != 1:
                    patches(g + 1)
                if g < G:
                    scores(2 * g + 1)
                if g == 1:
                    patches(2)
                if g == 0:
                    tokens(1)
                    pe.wait_ge(exp_loaded, 32)
                    for a in range(NB):
                        b = open_turn(pe, "expT", a)
                        for m in range(2):
                            ins = flip(b[:, m * P:(m + 1) * P], nat_exp[:, m, a * P:(a + 1) * P], P)
                        close_turn(ins, "expT", a)
                    pe.wait_ge(bit_sel_loaded, 32)
                    pe.wait_ge(stages_loaded, 16 * LOW)
                    stage_bits("u")
                if 2 <= g < G:
                    mm2(g - 2, 0, 2)
                if 1 <= g <= G:
                    turn_weights(2 * g - 1)
                if g == 1:
                    pe.wait_ge(mix_done, 3)
                    for k in range(2):
                        for c in range(2):
                            b = open_turn(pe, "upT", k, c)
                            for a in range(4):
                                ins = flip(b[:, a * P:(a + 1) * P], mixB[:, 4 * c + a, k * P:(k + 1) * P], P)
                            close_turn(ins, "upT", k, c)
                    for c in range(2):
                        wait_drained(pe, "bits", "d", LOW - 1, c)
                    for c in range(2):
                        b = open_turn(pe, "lowT", c)
                        for a in range(4):
                            ins = flip(b[:, a * P:(a + 1) * P], chain_out()[:, 4 * c + a, :], P)
                        close_turn(ins, "lowT", c)
                if 2 <= g < G - 1:
                    mm2(g - 2, 2, NT)
                if 1 <= g < G - 1:
                    tokens(g + 1, 0, 3)
                if 1 <= g <= G:
                    values(2 * g - 1)
                if 1 <= g < G - 1:
                    tokens(g + 1, 3)
                if 1 <= g <= G:
                    if g == G - 1:
                        mm2(g - 2, 2, 3)
                    out_proj(g - 1)
                if g >= G:
                    mm2(g - 2, 0, NT)
                if g + 1 < G:
                    ln_turns(g + 1, 0)
                    qk(g + 1, 0)
                    qk(g + 1, 1)
                if g == 0:
                    for c in range(2):
                        wait_drained(pe, "bits", "u", LOW - 1, c)
                    for a in range(NB):
                        wait_drained(pe, "expT", a)
                    for a in range(NB):
                        b = open_turn(pe, "low", "u", a)
                        ins = pe.matmul(b[:, 0:EB], chain_out()[:, a, :], expT[:, a, :], start=True, stop=True)
                        close_turn(ins, "low", "u", a)
                if g + 1 < G:
                    scores(2 * g + 2)
                if g < G:
                    turn_weights(2 * g)
                if g == G - 1:
                    mm2(g - 2, 3, NT)
                if g + 1 < G:
                    v_tiles(g + 1)
                if g < G:
                    values(2 * g)
                if g == 0:
                    pe.wait_ge(stages_loaded, 16 * 2 * LOW)
                    stage_bits("d")
                if g == 1:
                    for c in range(2):
                        wait_drained(pe, "lowT", c)
                    pe.wait_ge(mix_done, 6)
                    for a in range(NB):
                        b = open_turn(pe, "low", "d", a)
                        ins = pe.matmul(b[:, 0:E], lowT[:, a, :], mixB[:, a, 0:E], start=True, stop=True)
                        close_turn(ins, "low", "d", a)
                if 1 <= g <= G:
                    if g == 1:
                        for k in range(2):
                            for c in range(2):
                                wait_drained(pe, "upT", k, c)
                        for a in range(NB):
                            wait_drained(pe, "low", "d", a)
                    ln_turns(g - 1, 1)
                    mm1(g - 1)

        def drain_xT(eng, copy, g, wp, c):
            b = wait_filled(eng, "xT", g, wp, c)
            if g > 0:
                wait_filled(eng, "v", g - 1, NT - 1)
                eng.wait_ge(v_stored, 32 * g)
            dst = patT[:, 3 * c:3 * c + 3, :].rearrange("p k (r w) -> p k r w", w=GRID)[:, :, :, wp]
            drain(copy(dst, b[:, 0:3 * BH].rearrange("p (k r) -> p k r", k=3)), "xT", g, wp, c)

        def drain_turned(eng, copy, k, q):
            b = wait_filled(eng, "T", k, q)
            if k > 0:
                for sl in range(2):
                    wait_filled(eng, "V", k - 1, q // 2, sl)
            drain(copy(wT[:, q, :, :, :, 0:MAINQ].rearrange("p r i h q -> p (r i h) q"),
                       b[:, :].rearrange("p (x q) -> p x q", q=MAINQ)), "T", k, q)

        def drain_mm1(eng, add_bias, g, m, hf):
            b = wait_filled(eng, "mm1", g, m, hf)
            if g > 0:
                wait_filled(eng, "mm2", g - 1, NT - 1)
            drain(add_bias(gT[:, m, hf * HALF:(hf + 1) * HALF], b[:, 0:HALF], hid_bias[:, m:m + 1]),
                  "mm1", g, m, hf)

        def parts(view):
            return [view[:, 0:MAIN // 2], view[:, MAIN // 2:MAIN], view[:, MAIN:COLS]]

        def acc_parts(hg):
            main = acc[:, hg].rearrange("p (r i) m j -> p r (i m) j", i=2)
            return [main[:, 0, :, 0:TOK], main[:, 1, :, 0:TOK], acc_rest[:, hg, :, :]]

        XT_ACT = [(wp, 0) for wp in range(GRID)]
        XT_DVE = [(wp, 1) for wp in range(GRID)]

        @block.scalar
        def _(act):
            def copy(dst, src):
                return act.activation(dst, src, ACT.Identity)

            def add_bias(dst, src, bias):
                return act.activation(dst, src, ACT.Identity, bias=bias)

            act.dma_start(nat_tok, t["L0_tok_W_proj"].rearrange("(m p) d -> p m d", p=P)).then_inc(tok_loaded, 16)
            for dst, src in small:
                act.dma_start(dst, src, allow_slow_non_contiguous=True).then_inc(small_loaded, 16)

            def mix(side, base, step):
                st, pairs = upper_stage(side, step)
                src, dst, width = mix_buffers(side, step)
                if base + step > 0:
                    act.wait_ge(mix_done, base + step)
                for pr, lo, hi in pairs:
                    for o, blk in enumerate((lo, hi)):
                        co = high[:, side, st, pr, 3 * o:3 * o + 1]
                        ins = act.activation(dst[:, blk, 0:width], src[:, blk, 0:width], ACT.Copy, scale=co)
                ins.then_inc(mix_first, 1)

            def drain_ln(g, which):
                for tt, (t0, tn) in enumerate(TILES):
                    b = wait_filled(act, "lnT", g, which, tt)
                    if which == 0:
                        wait_filled(act, "tok", g, NT - 1)
                    elif g > 0:
                        wait_filled(act, "mm1", g - 1, NB - 1, 1)
                    else:
                        wait_filled(act, "low", "d", NB - 1)
                    drain(copy(xnT[which][:, :, t0:t0 + tn],
                               b[:, 0:2 * P].rearrange("p (k c) -> p k c", k=2)[:, :, 0:tn]), "lnT", g, which, tt)

            def drain_q(g, hg):
                for hf in range(2):
                    b = wait_filled(act, "q", g, hg, hf)
                    if g > 0:
                        wait_filled(act, "s", 2 * g - 2 + hg, 3)
                        act.wait_ge(q_rest_ready, 2 * g - 1 + hg)
                    for par in range(2):
                        ins = act.activation(qm[:, hg, par, hf * HALF:(hf + 1) * HALF], b[:, 0:HALF], ACT.Identity,
                                             bias=q_bias[:, hg, par:par + 1], scale=par_mask[:, par:par + 1])
                    drain(ins, "q", g, hg, hf)

            def drain_k(g, hg):
                for hf in range(2):
                    b = wait_filled(act, "k", g, hg, hf)
                    if g > 0:
                        wait_filled(act, "s", 2 * g - 2 + hg, 3)
                    drain(add_bias(kT[:, hg, hf * HALF:(hf + 1) * HALF], b[:, 0:HALF], qk_bias[:, 1, hg:hg + 1]),
                          "k", g, hg, hf)

            def drain_scores(k):
                hg = k % 2
                for r in range(4):
                    b = wait_filled(act, "s", k, r)
                    w = PAIRS * TOK + (REST if r == 3 else 0)
                    drain(copy(s[:, hg, r * PAIRS * TOK:r * PAIRS * TOK + w], b[:, 0:w]), "s", k, r)

            def arguments(c):
                k, f = divmod(c, NF)
                hg = k % 2
                if f == 0:
                    for r in range(4):
                        wait_drained(act, "s", k, r)
                if c >= 2:
                    act.wait_ge(frac_ready, c - 1)
                for x, (dst, src) in enumerate(zip(parts(u[:, c % 2]), parts(s[:, hg]))):
                    ins = act.activation(dst, src, ACT.Identity, bias=turns_alpha[:, UTILES * hg + x, f:f + 1],
                                         scale=inv_freq[:, f:f + 1])
                ins.then_inc(u_ready, 1)

            def sine(c):
                act.wait_ge(frac_ready, c + 1)
                act.activation(n[:, c % 2, :], n[:, c % 2, :], ACT.Sin, scale=-SIN_SCALE).then_inc(sin_ready, 1)

            def sigmoid(k):
                hg = k % 2
                act.wait_ge(acc_done, NF * (k + 1))
                v = acc[:, hg, :, :, 0:TOK].rearrange("p r m j -> p (r m) j")
                act.activation(v, v, ACT.Sigmoid)
                v = acc_rest[:, hg, :, :]
                act.activation(v, v, ACT.Sigmoid).then_inc(weights_ready, 1)

            def gelu(g):
                for m in range(NB):
                    for hf in range(2):
                        wait_drained(act, "mm1", g, m, hf)
                for m in range(0, NB, 2):
                    v = gT[:, m:m + 2, :].rearrange("p m x -> p (m x)")
                    ins = act.activation(v, v, ACT.Gelu)
                ins.then_inc(gelu_done, 1)

            def direct_gelu(g):
                for m in range(NB):
                    for hf in range(2):
                        b = wait_filled(act, "mm1", g, m, hf)
                        wait_filled(act, "mm2", g - 1, NT - 1)
                        ins = act.activation(gT[:, m, hf * HALF:(hf + 1) * HALF], b[:, 0:HALF], ACT.Gelu,
                                             bias=hid_bias[:, m:m + 1])
                        drain(ins, "mm1", g, m, hf)

            def even_heads(k, qp):
                for sl in range(2):
                    b = wait_filled(act, "V", k, qp, sl)
                    if qp == 1:
                        wait_drained(act, "V", k, 0, sl)
                    elif k > 0:
                        wait_drained(act, "V", k - 1, 1, sl)
                    src = b[:, 0:288].rearrange("p (x a i) -> p x a i", x=4, a=2)[:, :, 0, :]
                    act.activation(even[:, sl, :, :], src, ACT.Copy, scale=par_mask[:, 0:1]).then_inc(even_ready, 1)

            def mm1_share(g, lo, hi):
                for m in range(lo, hi):
                    drain_mm1(act, add_bias, g, m, 0)

            for wp, c in XT_ACT:
                drain_xT(act, copy, 0, wp, c)
            for w in range(4):
                for k in range(2):
                    b = wait_filled(act, "attnT", w, k)
                    drain(copy(w_attn[:, w, k, :], b[:, 0:E]), "attnT", w, k)
            drain_ln(0, 0)
            act.wait_ge(misc_loaded, 16)
            act.wait_ge(consts_ready, N_CONSTS)
            drain_q(0, 0)
            drain_k(0, 0)
            drain_scores(0)
            wait_drained(act, "heads")
            arguments(0)
            arguments(1)
            drain_q(0, 1)
            drain_k(0, 1)
            for step in range(2 * G + 3):
                g, odd = divmod(step, 2)
                has_unit = 0 <= step - 1 < UNITS
                for i in range(NF):
                    c = NF * step + i
                    if c < CHAIN:
                        sine(c)
                    if c + 2 < CHAIN:
                        arguments(c + 2)
                    if not odd:
                        if i == 0:
                            if 0 <= g - 2 < G - 1:
                                mm1_share(g - 2, 4, NB)
                            if g == 0:
                                for wp, cc in XT_ACT:
                                    drain_xT(act, copy, 1, wp, cc)
                            if has_unit and g < G:
                                sigmoid(step - 1)
                            if 0 <= g - 2 < G - 2:
                                gelu(g - 2)
                        if g == 1 and i in (0, 1):
                            mix(0, 0, 1 + i)
                        if i == 1:
                            if g < G:
                                drain_scores(2 * g + 1)
                        if i == 2:
                            if has_unit:
                                for q in range(2):
                                    drain_turned(act, copy, step - 1, q)
                            if g == 1:
                                for k in range(2):
                                    for cc in range(2):
                                        b = wait_filled(act, "upT", k, cc)
                                        drain(copy(w_up[:, k, cc * 512:(cc + 1) * 512], b[:, :]), "upT", k, cc)
                            if g == G:
                                gelu(g - 2)
                        if i == 3 and g == 1:
                            act.wait_ge(con_loaded, 16)
                            act.wait_ge(hid_ready, 1)
                            mix(1, 3, 0)
                        if g == 0 and i in (3, 4):
                            for a in range(4 * (i - 3), 4 * (i - 2)):
                                b = wait_filled(act, "expT", a)
                                drain(copy(expT[:, a, 0:E], b[:, 0:E]), "expT", a)
                        if i == 4:
                            if has_unit:
                                for qp in range(2):
                                    even_heads(step - 1, qp)
                        if i == 4:
                            if g == 1:
                                mix(1, 3, 1)
                    else:
                        if i == 0:
                            if has_unit:
                                sigmoid(step - 1)
                            if g + 1 < G:
                                drain_ln(g + 1, 0)
                        if i == 1 and g == G - 1:
                            for q in range(2):
                                drain_turned(act, copy, step - 1, q)
                        if i == 1 and g + 1 < G:
                            drain_q(g + 1, 0)
                            drain_k(g + 1, 0)
                        if i == 2:
                            if g + 1 < G:
                                drain_q(g + 1, 1)
                                drain_k(g + 1, 1)
                            if g == 0:
                                for a in range(NB):
                                    b = wait_filled(act, "low", "u", a)
                                    drain(copy(mixA[:, a, :], b[:, 0:EB]), "low", "u", a)
                            if g + 1 < G:
                                drain_scores(2 * g + 2)
                            if has_unit and g != G - 1:
                                for q in range(2):
                                    drain_turned(act, copy, step - 1, q)
                            if g == 1:
                                mix(1, 3, 2)
                        if i == 3:
                            if g == 0:
                                for a in range(NB):
                                    wait_drained(act, "low", "u", a)
                                act.wait_ge(late_loaded, 16 * len(late))
                                mix(0, 0, 0)
                            if has_unit:
                                for qp in range(2):
                                    even_heads(step - 1, qp)
                            if g == 1:
                                for a in range(NB):
                                    b = wait_filled(act, "low", "d", a)
                                    drain(copy(w_down[:, a, :], b[:, 0:E]), "low", "d", a)
                            if 1 <= g <= G:
                                drain_ln(g - 1, 1)
                        if i == 4:
                            if g == G - 1:
                                sigmoid(step)
                            if 1 <= g < G:
                                mm1_share(g - 1, 0, 4)
                            if g == G:
                                direct_gelu(g - 1)

        @block.gpsimd
        def _(pool):
            pool.dma_start(pos_dram.ap().rearrange("(b t) e -> b t e", t=TOK),
                           t["L0_tok_pos_emb"].unsqueeze(0).to_broadcast([IPG, TOK, E])).then_inc(pos_stored, 16)
            for dst, src in row_loads:
                pool.dma_start(dst, src).then_inc(rows_loaded, 16)
            full = TPG // P
            pool.wait_ge(pos_stored, 16)
            pool.dma_start(pos[:, 0:full, :], pos_dram.ap()[0:full * P, :].rearrange("(t p) e -> p t e", p=P))\
                .then_inc(pos_loaded, 16)
            pool.dma_start(pos[0:TPG - full * P, full, :], pos_dram.ap()[full * P:TPG, :]).then_inc(pos_loaded, 16)
            pool.memset(half_pow[:, :], -0.5).then_inc(pool_ready, 1)
            pool.memset(mv[:, :, :, :], 1.0).then_inc(pool_ready, 1)
            pool.memset(w_rest[:, :, :, :], 0.0).then_inc(pool_ready, 1)
            pool.memset(acc[:, :, :, :, :].rearrange("p a b c d -> p (a b c d)"), 0.0).then_inc(pool_ready, 1)

            def inv_std(g, which):
                k = ln_at[g, which]
                pool.wait_ge(mv_ready, k + 1)
                pool.tensor_scalar(var[:, which, :], mv[:, which, :, 1], 1e-5, 1.0, ALU.add, ALU.mult)\
                    .then_inc(var_ready, 1)
                pool.wait_ge(var_ready, k + 1)
                pool.tensor_tensor(rstd[:, which, :], var[:, which, :], half_pow[:, :], ALU.pow)\
                    .then_inc(rstd_ready, 1)

            def rest_queries(g, hg):
                wait_drained(pool, "q", g, hg, 0)
                wait_drained(pool, "q", g, hg, 1)
                if g > 0:
                    wait_filled(pool, "s", 2 * g - 2 + hg, 3)
                for par in range(2):
                    src = qm[:, hg, par, :].rearrange("p (b i) -> p b i", i=TOK)[:, :, MAINQ:TOK]
                    dst = q_rest[:, hg, :, :].rearrange("p b (r a i) -> p b r a i", r=4, a=2)[:, :, :, par, :]
                    ins = pool.tensor_tensor(
                        dst, src.unsqueeze(2).to_broadcast([P, IPG, 4, RESTQ]),
                        pair_mask.unsqueeze(1).unsqueeze(3).to_broadcast([P, IPG, 4, RESTQ]), ALU.mult)
                ins.then_inc(q_rest_ready, 1)

            def normalise(k):
                hg = k % 2
                pool.wait_ge(recip_ready, k + 1)
                v = acc[:, hg, :, :, 0:TOK].rearrange("p r m j -> p (r m) j")
                rs = rsums[:, hg, 0:4 * PAIRS].unsqueeze(2).to_broadcast([P, 4 * PAIRS, TOK])
                pool.tensor_tensor(v, v, rs, ALU.mult).then_inc(normed, 1)

            def round_argument(c):
                pool.wait_ge(u_ready, c + 1)
                if c >= 2:
                    pool.wait_ge(acc_done, c - 1)
                pool.tensor_scalar(n[:, c % 2, :], u[:, c % 2, :], 1.0, ROUND, ALU.mult, ALU.add)\
                    .then_inc(rounded, 1)

            def add_row(g, row, done):
                full = row.unsqueeze(1).to_broadcast([P, NT - 1, E])
                pool.tensor_tensor(h[:, g % 3, 0:NT - 1, :], h[:, g % 3, 0:NT - 1, :], full, ALU.add)
                pool.tensor_tensor(h[0:64, g % 3, NT - 1, :], h[0:64, g % 3, NT - 1, :], row[0:64, :], ALU.add)\
                    .then_inc(done, 1)

            def add_beta(g):
                pool.wait_ge(xn_ready[0], NT * (g + 1))
                add_row(g, row_beta, beta_added)

            def add_con(g):
                pool.wait_ge(xn_ready[1], NT * (g + 1))
                add_row(g, row_con, con_added)

            for dst, src in late:
                pool.dma_start(dst, src, allow_slow_non_contiguous=True).then_inc(late_loaded, 16)
            pool.wait_ge(misc_loaded, 16)
            inv_std(0, 0)
            rest_queries(0, 0)
            round_argument(0)
            rest_queries(0, 1)
            pool.wait_ge(rows_ready, 3)
            for step in range(2 * G + 2):
                g, odd = divmod(step, 2)
                has_unit = 0 <= step - 1 < UNITS
                for i in range(NF):
                    c = NF * step + i
                    if c + 1 < CHAIN:
                        round_argument(c + 1)
                    if not odd:
                        if i == 0 and g == 0:
                            add_beta(0)
                        if i == 1 and has_unit:
                            normalise(step - 1)
                        if i == 4 and g + 1 < G:
                            inv_std(g + 1, 0)
                    else:
                        if i == 0 and g == G - 1:
                            normalise(step - 1)
                        if i == 1:
                            if 1 <= g <= G:
                                inv_std(g - 1, 1)
                            if g + 1 < G:
                                rest_queries(g + 1, 0)
                            if has_unit and g != G - 1:
                                normalise(step - 1)
                            if g + 1 < G:
                                rest_queries(g + 1, 1)
                        if i == 2 and g + 1 < G:
                            add_beta(g + 1)
                        if i == 3 and 1 <= g <= G:
                            inv_std(g - 1, 2)
                        if i == 4 and 1 <= g <= G:
                            add_con(g - 1)

        @block.vector
        def _(dve):
            def copy(dst, src):
                return dve.tensor_copy(dst, src)

            def add_bias(dst, src, bias):
                return dve.tensor_scalar(dst, src, bias, None, ALU.add)

            k = 0

            def const(ins):
                nonlocal k
                k += 1
                ins.then_inc(consts_ready, 1)
                dve.wait_ge(consts_ready, k)

            def multiply_stage(side, st):
                src, dst = chain[st % 2], chain[(st + 1) % 2]
                parts_ = 2 if st == LOW - 1 else 1
                blocks = NB // parts_
                w2 = 2 ** st
                if st == 0 and side == "d":
                    wait_filled(dve, "low", "u", NB - 1)
                if st > 0:
                    wait_drained(dve, "bits", side, st - 1, 0)
                for c in range(parts_):
                    b = wait_filled(dve, "bits", side, st, c)
                    wv = b[:, 0:blocks * 2 * w2].rearrange("p (a k o) -> p a o k", a=blocks, o=2)
                    dv = dst[:, c * blocks * 2 * w2:(c + 1) * blocks * 2 * w2].rearrange(
                        "p (a o k) -> p a o k", a=blocks, o=2)
                    if st == 0:
                        ins = copy(dv, wv)
                    else:
                        sv = src[:, c * blocks * w2:(c + 1) * blocks * w2].rearrange(
                            "p (a k) -> p a k", a=blocks)
                        ins = dve.tensor_tensor(dv, wv, sv.unsqueeze(2).to_broadcast([P, blocks, 2, w2]),
                                                ALU.mult)
                    drain(ins, "bits", side, st, c)

            def mix(side, base, step):
                st, pairs = upper_stage(side, step)
                src, dst, width = mix_buffers(side, step)
                dve.wait_ge(mix_first, base + step + 1)
                for pr, lo, hi in pairs:
                    for o, (blk, other) in enumerate(((lo, hi), (hi, lo))):
                        j = 1 + o if side == 0 else 2 - o
                        ins = dve.scalar_tensor_tensor(out=dst[:, blk, 0:width], in0=src[:, other, 0:width],
                                                       scalar=high[:, side, st, pr, j:j + 1],
                                                       in1=dst[:, blk, 0:width], op0=ALU.mult, op1=ALU.add)
                ins.then_inc(mix_done, 1)

            def tile_stats(g, which, tt, src):
                tn = TILES[tt][1]
                if tt == 0 and ln_at[g, which] > 0:
                    dve.wait_ge(mv_ready, ln_at[g, which])
                dve.bn_stats(stats[0:tn, tt, :], src[0:tn, tt, :]).then_inc(stat_step, 1)

            def mean_and_variance(g, which):
                for tt, (t0, tn) in enumerate(TILES):
                    dve.wait_ge(stat_step, NT * ln_at[g, which] + tt + 1)
                    ins = dve.bn_aggr(mv[0:tn, which, tt, :], stats[0:tn, tt, :])
                ins.then_inc(mv_ready, 1)

            def tok_tiles(g, lo, hi):
                for tt in range(lo, hi):
                    tn = TILES[tt][1]
                    b = wait_filled(dve, "tok", g, tt)
                    if g >= 3:
                        dve.wait_ge(out_stored, 16 * NT * (g - 2))
                    if g == 2:
                        wait_filled(dve, "lowT", 1)
                    drain(dve.tensor_tensor(h[0:tn, g % 3, tt, :], b[0:tn, 0:E], pos[0:tn, tt, :], ALU.add),
                          "tok", g, tt)

            def tok_stats(g, lo, hi):
                for tt in range(lo, hi):
                    wait_drained(dve, "tok", g, tt)
                    tile_stats(g, 0, tt, h[:, g % 3])
                if hi == NT:
                    mean_and_variance(g, 0)

            def normed_tiles(g, which):
                w = 0 if which == 0 else 2
                dve.wait_ge(rstd_ready, ln_at[g, w] + 1)
                if which == 0:
                    wait_filled(dve, "tok", g, NT - 1)
                for tt, (t0, tn) in enumerate(TILES):
                    dve.tensor_scalar(xn[which][0:tn, tt, :], h[0:tn, g % 3, tt, :], mv[0:tn, w, tt, 0:1],
                                      rstd[0:tn, w, tt:tt + 1], ALU.subtract, ALU.mult).then_inc(xn_ready[which], 1)

            def drain_v(g):
                for tt, (t0, tn) in enumerate(TILES):
                    b = wait_filled(dve, "v", g, tt)
                    drain(dve.tensor_tensor(xn0[0:tn, tt, :], b[0:tn, 0:E], row_bv[0:tn, :], ALU.add), "v", g, tt)

            def fractions(c):
                dve.wait_ge(u_ready, c + 1)
                dve.wait_ge(rounded, c + 1)
                dve.scalar_tensor_tensor(out=n[:, c % 2, :], in0=n[:, c % 2, :], scalar=ROUND, in1=u[:, c % 2, :],
                                         op0=ALU.subtract, op1=ALU.subtract).then_inc(frac_ready, 1)

            def accumulate(c):
                k, f = divmod(c, NF)
                hg = k % 2
                dve.wait_ge(sin_ready, c + 1)
                if f > 0:
                    dve.wait_ge(acc_done, c)
                elif k > 1:
                    for q in range(QUADS):
                        wait_filled(dve, "T", k - 2, q)
                srcs = [src.rearrange("p (m j) -> p m j", j=TOK) for src in parts(n[:, c % 2])]
                for x, (dst, src) in enumerate(zip(acc_parts(hg), srcs)):
                    al = turns_alpha[:, UTILES * hg + x, NF + f:NF + f + 1]
                    if f == 0:
                        ins = dve.tensor_scalar(dst, src, al, None, ALU.mult)
                    else:
                        ins = dve.scalar_tensor_tensor(out=dst, in0=src, scalar=al, in1=dst,
                                                       op0=ALU.mult, op1=ALU.add)
                ins.then_inc(acc_done, 1)

            def denominators(k):
                hg = k % 2
                dve.wait_ge(weights_ready, k + 1)
                dve.tensor_reduce(sums[:, hg, 0:4 * PAIRS],
                                  acc[:, hg, :, :, 0:TOK].rearrange("p r m j -> p (r m) j"), AX.X, ALU.add)
                dve.tensor_reduce(sums[:, hg, 4 * PAIRS:], acc_rest[:, hg, :, :], AX.X, ALU.add)\
                   .then_inc(sums_step, 1)
                dve.wait_ge(sums_step, 2 * k + 1)
                dve.tensor_scalar(sums[:, hg, :], sums[:, hg, :], 1e-10, None, ALU.add).then_inc(sums_step, 1)
                dve.wait_ge(sums_step, 2 * k + 2)
                if k > 1:
                    dve.wait_ge(normed, k - 1)
                dve.reciprocal(rsums[:, hg, :], sums[:, hg, :]).then_inc(recip_ready, 1)

            def normalise_rest(k):
                hg = k % 2
                dve.wait_ge(recip_ready, k + 1)
                if k > 0:
                    wait_filled(dve, "rT", k - 1)
                for sl in range(2):
                    p0 = SLOT * sl
                    rs = rsums[p0:p0 + 64, hg, 4 * PAIRS:].unsqueeze(2).to_broadcast([64, QUADS, TOK])
                    ins = dve.tensor_tensor(w_rest[p0:p0 + 64, :, sl, 0:TOK], acc_rest[p0:p0 + 64, hg, :, :], rs,
                                            ALU.mult)
                ins.then_inc(rest_normed, 1)

            def turned_share(k):
                for q in range(2, QUADS):
                    drain_turned(dve, copy, k, q)
                b = wait_filled(dve, "rT", k)
                drain(copy(wT[:, :, :, :, :, MAINQ:TOK].rearrange("p q r i h j -> p (q r i h) j"),
                           b[:, 0:QUADS * 64].rearrange("p (x j) -> p x j", j=RESTQ)), "rT", k)

            def odd_heads(k, qp):
                g, hg = divmod(k, 2)
                if g > 0 and hg == 0 and qp == 0:
                    wait_filled(dve, "o", g - 1, NT - 1)
                for sl in range(2):
                    dve.wait_ge(even_ready, 4 * k + 2 * qp + sl + 1)
                    b = banks[turn["V", k, qp, sl] % BANKS]
                    src = b[:, 0:288].rearrange("p (q i a j) -> p q i a j", q=2, i=2, a=2)[:, :, :, 1, :]
                    dst = oT[:, hg].rearrange("p (v q s i) j -> p v s q i j", v=2, q=2, s=2)[:, qp, sl]
                    ins = dve.scalar_tensor_tensor(
                        out=dst, in0=src, scalar=par_mask[:, 1:2],
                        in1=even[:, sl, :, :].rearrange("p (q i) j -> p q i j", q=2), op0=ALU.mult, op1=ALU.add)
                    drain(ins, "V", k, qp, sl)

            def attn_tiles(g):
                if g > 0:
                    wait_filled(dve, "lnT", g - 1, 1, NT - 1)
                for tt, (t0, tn) in enumerate(TILES):
                    b = wait_filled(dve, "o", g, tt)
                    drain(dve.tensor_tensor(on[0:tn, tt, :], b[0:tn, 0:E], row_bo[0:tn, :], ALU.add), "o", g, tt)

            def attn_stats(g):
                for tt in range(NT):
                    wait_drained(dve, "o", g, tt)
                    tile_stats(g, 1, tt, on)
                mean_and_variance(g, 1)

            def attn_residual(g):
                dve.wait_ge(mv_ready, ln_at[g, 1] + 1)
                for tt, (t0, tn) in enumerate(TILES):
                    dve.scalar_tensor_tensor(out=on[0:tn, tt, :], in0=on[0:tn, tt, :],
                                             scalar=mv[0:tn, 1, tt, 0:1], in1=row_gamma[0:tn, :],
                                             op0=ALU.subtract, op1=ALU.mult).then_inc(on_step, 1)
                dve.wait_ge(rstd_ready, ln_at[g, 1] + 1)
                dve.wait_ge(beta_added, g + 1)
                for tt, (t0, tn) in enumerate(TILES):
                    dve.wait_ge(on_step, NT * g + tt + 1)
                    dve.scalar_tensor_tensor(out=h[0:tn, g % 3, tt, :], in0=on[0:tn, tt, :],
                                             scalar=rstd[0:tn, 1, tt:tt + 1], in1=h[0:tn, g % 3, tt, :],
                                             op0=ALU.mult, op1=ALU.add).then_inc(h1_ready, 1)

            def residual_stats(g):
                for tt in range(NT):
                    dve.wait_ge(h1_ready, NT * g + tt + 1)
                    tile_stats(g, 2, tt, h[:, g % 3])
                mean_and_variance(g, 2)

            def last_sums(g, lo, hi):
                dve.wait_ge(con_added, g + 1)
                for tt in range(lo, hi):
                    tn = TILES[tt][1]
                    b = wait_filled(dve, "mm2", g, tt)
                    drain(dve.tensor_tensor(h[0:tn, g % 3, tt, :], b[0:tn, 0:E], h[0:tn, g % 3, tt, :], ALU.add),
                          "mm2", g, tt)

            def mm1_share(g, lo, hi):
                for m in range(lo, hi):
                    drain_mm1(dve, add_bias, g, m, 1)

            for kk in range(KC):
                b = wait_filled(dve, "wT", kk)
                drain(copy(w_tok[:, kk, :], b[:, 0:E]), "wT", kk)
            for wp, c in XT_DVE:
                drain_xT(dve, copy, 0, wp, c)
            dve.wait_ge(pos_loaded, 32)
            dve.wait_ge(rows_loaded, 16 * len(row_loads))
            full = TPG // P
            dve.tensor_tensor(pos[:, 0:full, :], pos[:, 0:full, :],
                              row_proj.unsqueeze(1).to_broadcast([P, full, E]), ALU.add).then_inc(rows_ready, 1)
            dve.tensor_tensor(pos[0:TPG - full * P, full, :], pos[0:TPG - full * P, full, :],
                              row_proj[0:TPG - full * P, :], ALU.add).then_inc(rows_ready, 1)
            dve.tensor_tensor(row_con, row_con, row_down, ALU.add).then_inc(rows_ready, 1)
            dve.wait_ge(rows_ready, 3)
            dve.wait_ge(misc_loaded, 16)
            dve.wait_ge(small_loaded, 16 * len(small))
            const(dve.tensor_scalar(temp[:, 3:4], temp[:, 0:1], -1.0, None, ALU.mult))
            const(dve.tensor_tensor(temp[:, 3:4], temp[:, 0:1], temp[:, 3:4], ALU.max))
            const(dve.tensor_scalar(temp[:, 1:2], temp[:, 3:4], 0.1, None, ALU.add))
            const(dve.reciprocal(temp[:, 2:3], temp[:, 1:2]))
            for f, freq in enumerate(FREQS):
                const(dve.tensor_scalar(inv_freq[:, f:f + 1], temp[:, 2:3], 1.0 / freq, HD ** -0.5,
                                        ALU.mult, ALU.mult))
            for hg in range(2):
                for par in range(2):
                    const(dve.tensor_tensor(q_bias[:, hg, par:par + 1], qk_bias[:, 0, hg:hg + 1],
                                            par_mask[:, par:par + 1], ALU.mult))
            dve.wait_ge(pool_ready, 4)
            for tt in range(NT):
                tok_tiles(0, tt, tt + 1)
                tok_stats(0, tt, tt + 1)

            normed_tiles(0, 0)
            b = wait_filled(dve, "heads")
            tv = b[:, 0:2 * UTILES * 2 * NF].rearrange("p (k f) -> p k f", k=2 * UTILES)
            dve.tensor_scalar(turns_alpha[:, :, 0:NF], tv[:, :, 0:NF], 1.0 / TWO_PI, None, ALU.mult)
            drain(copy(turns_alpha[:, :, NF:], tv[:, :, NF:]), "heads")
            fractions(0)
            drain_v(0)
            for step in range(2 * G + 3):
                g, odd = divmod(step, 2)
                has_unit = 0 <= step - 1 < UNITS
                for i in range(NF):
                    c = NF * step + i
                    if odd and i == 0:
                        if g + 1 < G:
                            normed_tiles(g + 1, 0)
                        if g == G - 1:
                            denominators(step - 1)
                            normalise_rest(step - 1)
                            last_sums(g - 2, 2, 3)
                        if 1 <= g <= G:
                            attn_tiles(g - 1)
                    if c + 1 < CHAIN:
                        fractions(c + 1)
                    if not odd:
                        if i == 0:
                            if g == G:
                                denominators(step - 1)
                                normalise_rest(step - 1)
                            if 0 <= g - 2 < G - 1:
                                mm1_share(g - 2, 4, NB)
                        if i == 1:
                            if has_unit and g != G:
                                denominators(step - 1)
                        if i == 2 and 0 <= g - 2 < G and g != G:
                            last_sums(g - 2, 0, 2)
                        if i == 2 and g == 1:
                            dve.wait_ge(mix_done, 3)
                            dve.tensor_tensor(hid_bias[:, :].unsqueeze(2), mixB[:, :, E:EB],
                                              up_bias[:, :].unsqueeze(2), ALU.add).then_inc(hid_ready, 1)
                        if i == 3:
                            if 0 <= g - 2 < G and g not in (G - 1, G):
                                last_sums(g - 2, 2, NT)
                            if g == 0:
                                tok_tiles(1, 3, NT)
                                tok_stats(1, 0, NT)
                        if i == 4:
                            if has_unit:
                                for qp in range(2):
                                    odd_heads(step - 1, qp)
                        if i == 4:
                            if 1 <= g < G - 1:
                                tok_tiles(g + 1, 3, NT)
                                tok_stats(g + 1, 3, NT)
                    else:
                        if i == 1:
                            if has_unit and g != G - 1:
                                denominators(step - 1)
                        if i == 2 and has_unit and g != G - 1:
                            turned_share(step - 1)
                        if i == 3 and 1 <= g <= G:
                            normed_tiles(g - 1, 1)
                            if g == G:
                                last_sums(g - 2, 0, NT)
                        if i == 3:
                            if g == G - 1:
                                last_sums(g - 2, 3, NT)
                            if has_unit:
                                for qp in range(2):
                                    odd_heads(step - 1, qp)
                        if g == 0 and i == 4:
                            mix(0, 0, 0)
                    if c < CHAIN:
                        accumulate(c)
                    if not odd:
                        if i == (1 if g == 1 else 0) and g + 1 < G:
                            for wp in range(GRID):
                                if g > 0:
                                    drain_xT(dve, copy, g + 1, wp, 0)
                                drain_xT(dve, copy, g + 1, wp, 1)
                        if i == 1 and has_unit and g != G:
                            normalise_rest(step - 1)
                        if g == 1 and i in (0, 1):
                            mix(0, 0, 1 + i)
                        if i == 2:
                            if has_unit:
                                turned_share(step - 1)
                            if g == 1:
                                for cc in range(2):
                                    b = wait_filled(dve, "lowT", cc)
                                    drain(copy(lowT[:, 4 * cc:4 * cc + 4, :].rearrange("p a o -> p (a o)"),
                                               b[:, :]), "lowT", cc)
                            if g == 0:
                                tok_tiles(1, 0, 3)
                        if i == 3:
                            if 1 <= g < G - 1:
                                tok_tiles(g + 1, 0, 3)
                                tok_stats(g + 1, 0, 3)
                            if g == 1:
                                mix(1, 3, 0)
                        if i == 4:
                            if g == 1:
                                mix(1, 3, 1)
                            if g == 0:
                                for st in range(LOW):
                                    multiply_stage("u", st)
                    else:
                        if i == 0 and 1 <= g <= G:
                            attn_stats(g - 1)
                        if i == 1:
                            if has_unit and g != G - 1:
                                normalise_rest(step - 1)
                            if g == G - 1:
                                turned_share(step - 1)
                            if 1 <= g <= G:
                                attn_residual(g - 1)
                        if i == 2 and 1 <= g <= G:
                            residual_stats(g - 1)
                            if g == 1:
                                mix(1, 3, 2)
                        if i == 2 and g + 1 < G:
                            drain_v(g + 1)
                        if i == 4:
                            if g == 0:
                                for st in range(LOW):
                                    multiply_stage("d", st)
                            if 1 <= g < G:
                                mm1_share(g - 1, 0, 4)


_INS = ["x", "L0_tok_W_proj", "L0_tok_b_proj", "L0_tok_pos_emb", "L0_attn_Wq", "L0_attn_bq", "L0_attn_Wk",
        "L0_attn_bk", "L0_attn_Wv", "L0_attn_bv", "L0_attn_Wo", "L0_attn_bo", "L0_attn_alpha", "L0_attn_phi",
        "L0_attn_temperature", "L0_attn_gamma", "L0_attn_beta", "L0_ffn_W_exp", "L0_ffn_b_exp",
        "L0_ffn_up_weights", "L0_ffn_up_bias", "L0_ffn_down_weights", "L0_ffn_W_con", "L0_ffn_b_con",
        "L0_ffn_down_bias"]


def kernel(**inputs):
    import concourse.bacc as _bacc
    from concourse.bass_utils import run_bass_kernel_spmd as _run

    nc = _bacc.Bacc("TRN2", target_bir_lowering=False, num_devices=1)
    arrays, tensors = {}, {}

    def give(name, a):
        arrays[f"in_{name}"] = a
        tensors[name] = nc.dram_tensor(f"in_{name}", a.shape, mybir.dt.from_np(a.dtype), kind="ExternalInput").ap()

    for name in _INS:
        give(name, np.ascontiguousarray(inputs[name]))
    for name, a in zip(("misc", "heads", "bits"), shape_constants()):
        give(name, a)
    tensors["out"] = nc.dram_tensor("out", (IMAGES, TOK, E), F32, kind="ExternalOutput").ap()
    build(nc, tensors)
    r = _run(nc, [arrays], core_ids=[0])
    return r.results[0]["out"]
```
